# Optimizing a Trainium2 kernel written in Bass

```python
import numpy as np
import jax
import jax.numpy as jnp

def _softmax(x, axis=-1):
    return jax.nn.softmax(x, axis=axis)

def _gelu(x):
    return jax.nn.gelu(x, approximate=True)

def _silu(x):
    return jax.nn.silu(x)

def _sigmoid(x):
    return jax.nn.sigmoid(x)

def _layernorm(x, axis=-1, eps=1e-05):
    m = jnp.mean(x, axis=axis, keepdims=True)
    v = jnp.var(x, axis=axis, keepdims=True)
    return (x - m) / jnp.sqrt(v + eps)

def _scatter_add(tgt, idx, src, axis=0):
    return tgt.at[idx].add(src)

def _segment_sum(src, seg, n):
    return jax.ops.segment_sum(src, seg, n)
kernel_name = 'mk_gps_d1_gnn_r8_efc33c'

def setup_inputs(seed: int=0):
    np.random.seed(seed)
    _w = jnp.asarray

    def _rec_inputs():
        import jax
        import jax.numpy as jnp
        _gk = jax.random.key(seed)
        x = -0.0003713 + 1 * jax.random.normal(jax.random.fold_in(_gk, 1), (6250, 256), jnp.float32)
        src = jax.random.randint(jax.random.fold_in(_gk, 2), (100000,), 0, 6250, jnp.int32)
        dst = jnp.minimum((6250 * jax.random.uniform(jax.random.fold_in(_gk, 3), (100000,)) ** 2.0).astype(jnp.int32), 49999)
        _o = jnp.argsort(dst, stable=True)
        src = src[_o]
        dst = dst[_o]
        return (x, src, dst)
    x, src, dst = _rec_inputs()

    def _L0_gnn_setup():
        import jax, jax.numpy as jnp
        import numpy as np
        N_NODES = 6250
        N_EDGES = 125000
        F_IN = 256
        HEADS = 8
        F_HEAD = 32
        NEG_SLOPE = 0.2
        key = jax.random.key(seed)
        ks = jax.random.split(key, 6)
        x = jax.random.normal(ks[0], (N_NODES, F_IN), dtype=jnp.float32)
        W = jax.random.normal(ks[1], (F_IN, HEADS * F_HEAD), dtype=jnp.float32) / np.sqrt(F_IN)
        att_src = jax.random.normal(ks[2], (HEADS, F_HEAD), dtype=jnp.float32) / np.sqrt(F_HEAD)
        att_dst = jax.random.normal(ks[3], (HEADS, F_HEAD), dtype=jnp.float32) / np.sqrt(F_HEAD)
        bias = jnp.zeros((HEADS * F_HEAD,), dtype=jnp.float32)
        edge_index = jax.random.randint(ks[4], (2, N_EDGES), 0, N_NODES, dtype=jnp.int64)
        return {'x': x, 'W': W, 'att_src': att_src, 'att_dst': att_dst, 'bias': bias, 'edge_index': edge_index}
    _L0_gnn_all = _L0_gnn_setup()
    _L0_gnn_in = {k: v for k, v in _L0_gnn_all.items() if k in ('W', 'att_src', 'att_dst', 'bias')}
    del _L0_gnn_all

    def _L0_mix_setup():
        import jax, jax.numpy as jnp
        import numpy as np
        D_MODEL = 256
        NUM_HEADS = 8
        DEPTH = D_MODEL // NUM_HEADS
        B, L = (32, 512)

        def _feature_map(x):
            return jax.nn.elu(x) + 1.0
        key = jax.random.key(seed)
        ks = jax.random.split(key, 9)
        sc = 1.0 / np.sqrt(D_MODEL)
        return {'x': jax.random.normal(ks[0], (B, L, D_MODEL), dtype=jnp.float32), 'wq': jax.random.normal(ks[1], (D_MODEL, D_MODEL), dtype=jnp.float32) * sc, 'bq': jnp.zeros((D_MODEL,), dtype=jnp.float32), 'wk': jax.random.normal(ks[2], (D_MODEL, D_MODEL), dtype=jnp.float32) * sc, 'bk': jnp.zeros((D_MODEL,), dtype=jnp.float32), 'wv': jax.random.normal(ks[3], (D_MODEL, D_MODEL), dtype=jnp.float32) * sc, 'bv': jnp.zeros((D_MODEL,), dtype=jnp.float32), 'wo': jax.random.normal(ks[4], (D_MODEL, D_MODEL), dtype=jnp.float32) * sc, 'bo': jnp.zeros((D_MODEL,), dtype=jnp.float32)}
    _L0_mix_all = _L0_mix_setup()
    _L0_mix_in = {k: v for k, v in _L0_mix_all.items() if k in ('wq', 'bq', 'wk', 'bk', 'wv', 'bv', 'wo', 'bo')}
    del _L0_mix_all

    def _L0_ffn_setup():
        import math
        import jax, jax.numpy as jnp
        import numpy as np
        CAPACITY_FACTOR = 1.25
        TOP_K = 2
        LN_EPS = 1e-05

        def _layer_norm(x, gamma, beta):
            mu = jnp.mean(x, axis=-1, keepdims=True)
            var = jnp.var(x, axis=-1, keepdims=True)
            return (x - mu) * jax.lax.rsqrt(var + LN_EPS) * gamma + beta
        key = jax.random.key(seed)
        ks = jax.random.split(key, 4)
        B, S, D, F, E = (8, 512, 256, 512, 8)
        x = jax.random.normal(ks[0], (B, S, D), dtype=jnp.float32)
        Wr = jax.random.normal(ks[1], (D, E), dtype=jnp.float32) / np.sqrt(D)
        br = jnp.zeros((E,), jnp.float32)
        W1 = jax.random.normal(ks[2], (E, D, F), dtype=jnp.float32) / np.sqrt(D)
        b1 = jnp.zeros((E, F), jnp.float32)
        W2 = jax.random.normal(ks[3], (E, F, D), dtype=jnp.float32) / np.sqrt(F)
        b2 = jnp.zeros((E, D), jnp.float32)
        gamma = jnp.ones((D,), jnp.float32)
        beta = jnp.zeros((D,), jnp.float32)
        return {'x': x, 'Wr': Wr, 'br': br, 'W1': W1, 'b1': b1, 'W2': W2, 'b2': b2, 'gamma': gamma, 'beta': beta}
    _L0_ffn_all = _L0_ffn_setup()
    _L0_ffn_in = {k: v for k, v in _L0_ffn_all.items() if k in ('Wr', 'br', 'W1', 'b1', 'W2', 'b2', 'gamma', 'beta')}
    del _L0_ffn_all
    return {'x': x, 'src': src, 'dst': dst, 'L0_gnn_W': _L0_gnn_in['W'], 'L0_gnn_att_src': _L0_gnn_in['att_src'], 'L0_gnn_att_dst': _L0_gnn_in['att_dst'], 'L0_gnn_bias': _L0_gnn_in['bias'], 'L0_mix_wq': _L0_mix_in['wq'], 'L0_mix_bq': _L0_mix_in['bq'], 'L0_mix_wk': _L0_mix_in['wk'], 'L0_mix_bk': _L0_mix_in['bk'], 'L0_mix_wv': _L0_mix_in['wv'], 'L0_mix_bv': _L0_mix_in['bv'], 'L0_mix_wo': _L0_mix_in['wo'], 'L0_mix_bo': _L0_mix_in['bo'], 'L0_ffn_Wr': _L0_ffn_in['Wr'], 'L0_ffn_br': _L0_ffn_in['br'], 'L0_ffn_W1': _L0_ffn_in['W1'], 'L0_ffn_b1': _L0_ffn_in['b1'], 'L0_ffn_W2': _L0_ffn_in['W2'], 'L0_ffn_b2': _L0_ffn_in['b2'], 'L0_ffn_gamma': _L0_ffn_in['gamma'], 'L0_ffn_beta': _L0_ffn_in['beta']}

def reference(x, src, dst, L0_gnn_W, L0_gnn_att_src, L0_gnn_att_dst, L0_gnn_bias, L0_mix_wq, L0_mix_bq, L0_mix_wk, L0_mix_bk, L0_mix_wv, L0_mix_bv, L0_mix_wo, L0_mix_bo, L0_ffn_Wr, L0_ffn_br, L0_ffn_W1, L0_ffn_b1, L0_ffn_W2, L0_ffn_b2, L0_ffn_gamma, L0_ffn_beta):
    import jax
    import jax.numpy as jnp

    def _L0_gnn_ref(x, W, att_src, att_dst, bias, edge_index):
        import jax, jax.numpy as jnp
        import numpy as np
        N_NODES = 6250
        N_EDGES = 125000
        F_IN = 256
        HEADS = 8
        F_HEAD = 32
        NEG_SLOPE = 0.2
        N = x.shape[0]
        src, dst = (edge_index[0], edge_index[1])
        h = (x @ W).reshape(N, HEADS, F_HEAD)
        a_src = jnp.einsum('nhf,hf->nh', h, att_src)
        a_dst = jnp.einsum('nhf,hf->nh', h, att_dst)
        e = jax.nn.leaky_relu(a_src[src] + a_dst[dst], NEG_SLOPE)
        e_max = jax.ops.segment_max(e, dst, num_segments=N)
        e_exp = jnp.exp(e - e_max[dst])
        denom = jax.ops.segment_sum(e_exp, dst, num_segments=N)
        alpha = e_exp / denom[dst]
        msgs = alpha[:, :, None] * h[src]
        out = jax.ops.segment_sum(msgs, dst, num_segments=N)
        return out.reshape(N, HEADS * F_HEAD) + bias

    def _L0_mix_ref(x, wq, bq, wk, bk, wv, bv, wo, bo):
        import jax, jax.numpy as jnp
        import numpy as np
        D_MODEL = 256
        NUM_HEADS = 8
        DEPTH = D_MODEL // NUM_HEADS
        B, L = (32, 512)

        def _feature_map(x):
            return jax.nn.elu(x) + 1.0
        b, l, _ = x.shape
        q = (x @ wq + bq).reshape(b, l, NUM_HEADS, DEPTH)
        k = (x @ wk + bk).reshape(b, l, NUM_HEADS, DEPTH)
        v = (x @ wv + bv).reshape(b, l, NUM_HEADS, DEPTH)
        q = _feature_map(q)
        k = _feature_map(k)
        kv = jnp.einsum('blhd,blhe->bhde', k, v)
        k_sum = jnp.sum(k, axis=1)
        qkv = jnp.einsum('blhd,bhde->blhe', q, kv)
        normalizer = jnp.einsum('blhd,bhd->blh', q, k_sum) + 1e-06
        out = qkv / normalizer[..., None]
        out = out.reshape(b, l, D_MODEL)
        return out @ wo + bo

    def _L0_ffn_ref(x, Wr, br, W1, b1, W2, b2, gamma, beta):
        import math
        import jax, jax.numpy as jnp
        import numpy as np
        CAPACITY_FACTOR = 1.25
        TOP_K = 2
        LN_EPS = 1e-05

        def _layer_norm(x, gamma, beta):
            mu = jnp.mean(x, axis=-1, keepdims=True)
            var = jnp.var(x, axis=-1, keepdims=True)
            return (x - mu) * jax.lax.rsqrt(var + LN_EPS) * gamma + beta
        B, S, D = x.shape
        E = Wr.shape[1]
        N = B * S
        K = TOP_K
        logits = jnp.mean(x, axis=1) @ Wr + br
        routing_weights = jax.nn.softmax(logits, axis=-1)
        capacity = float(math.ceil(N * CAPACITY_FACTOR / E))
        expected_loads = routing_weights.sum(axis=0) * (N / B)
        scale = jnp.where(expected_loads > capacity, capacity / expected_loads, 1.0)
        routing_weights = jax.nn.softmax(routing_weights * scale, axis=-1)
        rw_tok = jnp.broadcast_to(routing_weights[:, None, :], (B, S, E)).reshape(N, E)
        top_w, top_i = jax.lax.top_k(rw_tok, K)
        top_w = jax.nn.softmax(top_w, axis=-1)
        xf = x.reshape(N, D)
        h = jax.nn.gelu(jnp.einsum('nd,edf->enf', xf, W1) + b1[:, None, :], approximate=False)
        y = jnp.einsum('enf,efd->end', h, W2) + b2[:, None, :]
        w_dense = jnp.zeros((N, E), x.dtype).at[jnp.arange(N)[:, None], top_i].add(top_w)
        out = jnp.einsum('ne,end->nd', w_dense, y).reshape(B, S, D)
        out = _layer_norm(out + x, gamma, beta)
        return out
    edge_index = jnp.stack([src, dst])
    xn = _layernorm(x, axis=-1)
    x = x + _L0_gnn_ref(xn, L0_gnn_W, L0_gnn_att_src, L0_gnn_att_dst, L0_gnn_bias, edge_index) + _L0_mix_ref(xn[None], L0_mix_wq, L0_mix_bq, L0_mix_wk, L0_mix_bk, L0_mix_wv, L0_mix_bv, L0_mix_wo, L0_mix_bo)[0]
    x = x + _L0_ffn_ref(_layernorm(x, axis=-1)[None], L0_ffn_Wr, L0_ffn_br, L0_ffn_W1, L0_ffn_b1, L0_ffn_W2, L0_ffn_b2, L0_ffn_gamma, L0_ffn_beta)[0]
    return x

_drawn_inputs = setup_inputs


def setup_inputs(seed=0):
    import zlib

    import numpy as np

    out = dict(_drawn_inputs(seed))
    spreads = {'L0_gnn_bias': (0.0, 0.1),
     'L0_mix_bq': (0.0, 2.0),
     'L0_mix_bk': (0.0, 2.0),
     'L0_mix_bv': (0.0, 0.1),
     'L0_mix_bo': (0.0, 0.1),
     'L0_ffn_br': (0.0, 0.8),
     'L0_ffn_b1': (0.0, 0.391),
     'L0_ffn_b2': (0.0, 0.267),
     'L0_ffn_gamma': (1.0, 0.2),
     'L0_ffn_beta': (0.0, 0.1)}
    factors = {'L0_mix_wq': 8.0, 'L0_mix_wk': 6.93, 'L0_mix_wv': 4.331, 'L0_ffn_Wr': 64.0}
    for name, (base, spread) in spreads.items():
        noise = np.random.default_rng([zlib.crc32(name.encode()), seed]).standard_normal(out[name].shape)
        drawn = base * np.exp(spread * noise) if base else spread * noise
        out[name] = jnp.asarray(drawn.astype(out[name].dtype))
    for name, factor in factors.items():
        out[name] = (out[name] * factor).astype(out[name].dtype)
    return out
```

```python
from contextlib import ExitStack

import concourse.bass as bass
from concourse import mybir

F32 = mybir.dt.float32
I32 = mybir.dt.int32
ALU = mybir.AluOpType
ACT = mybir.ActivationFunctionType
AX_X = mybir.AxisListType.X

P = 128
N, D = 6250, 256
HEADS, FH = 8, 32
EDGES = 100000
EXPERTS, HIDDEN, TOPK = 8, 512, 2
LN_EPS = 1e-5
NORM_EPS = 1e-6
SLOPE = 0.2
CAPACITY = float(-(-N * 5 // (4 * EXPERTS)))
SPREAD = 60.0
LOW = -1.0e38
CONSTS, WEIGHTS, ROUTE = 15, 12, 33
EXPS = (5, 14, 28)

NT = -(-N // P)
NP = NT * P
LAST = N - (NT - 1) * P
ROW = D + HEADS
XW = D + 1
C = D // P
HW = D + 2 * HEADS
QUAD = 4
BODY = 4 * QUAD
ET = 784
EP = ET * P
STEPS = ET + NT - 1
BODIES = STEPS // BODY
SC = -(-STEPS // P)
SW = SC * P
WHOLE = EDGES // P
NB = NT - 1
CH = 112
CL = EP // CH
SUMS = (0, 1, 3, 4)
PAIRS = NT // 2
FJ = HIDDEN // P
EJ = TOPK * FJ
PAD_DST = NP - 1
assert STEPS == BODIES * BODY and NT % 16 == 1 and BODIES >= 2 * PAIRS + 4 and CL % 16 == 0


def gps_layer(nc, x, src, dst, gW, g_as, g_ad, g_bias, wq, bq, wk, bk, wv, bv, wo, bo, Wr, br, W1, b1, W2, b2,
              gamma, beta, out, table, src_pad, dst_pad, asrc_tab, smax_tab, xn_d, xa_d, spread):
    with ExitStack() as ctx:
        def sb(name, shape, dt=F32):
            return ctx.enter_context(nc.sbuf_tensor(name, shape, dt))

        def sem(name):
            return ctx.enter_context(nc.semaphore(name))

        bank = [ctx.enter_context(nc.psum_tensor(f"bank{i}", [P, 512], F32)) for i in range(8)]

        xT = sb("xT", [P, C * NP])
        xTv = xT[:].rearrange("p (c n) -> p c n", c=C)
        acc = sb("acc", [P, NT * ROW])
        accx = acc[:, 0:NT * D].rearrange("p (n f) -> p n f", f=D)
        accv = acc[:].rearrange("p (n f) -> p n f", f=ROW)
        aa = sb("aa", [P, NT * 24])
        aav = aa[:].rearrange("p (n k) -> p n k", k=24)
        mr = sb("mr", [P, NT * 2])
        mrv = mr[:].rearrange("p (n k) -> p n k", k=2)
        ident = sb("ident", [P, P])
        iota_f = sb("iota_f", [P, P])
        ones = sb("ones", [P, P])
        zeros = sb("zeros", [P, XW])
        headmask = sb("headmask", [P, P])
        kbmask = sb("kbmask", [P, C, HEADS])
        wg = sb("wg", [P, C, HW])
        wqs, wks, wvs, wos = (sb(n, [P, C, D]) for n in ("wqs", "wks", "wvs", "wos"))
        bks, bvs, bos, gbs, bsum = (sb(n, [1, D]) for n in ("bks", "bvs", "bos", "gbs", "bsum"))
        brs = sb("brs", [1, EXPERTS])
        bqs = sb("bqs", [P, C])
        gam = sb("gam", [P, D])
        bet = sb("bet", [P, D])
        wrs = sb("wrs", [P, C, EXPERTS])
        brow_aa = sb("brow_aa", [1, SW], I32)
        brow_acc = sb("brow_acc", [1, SW], I32)
        dl = sb("dl", [P, SW])
        srci = sb("srci", [P, SW], I32)
        idx = sb("idx", [P, BODY], I32)
        kb = sb("kb", [P, C, HEADS])
        m_sb = sb("m_sb", [P, C, D])
        half = sb("half", [P, 8])
        flag = sb("flag", [1, 1], I32)
        mult7 = sb("mult7", [P, 7])
        pidx7 = sb("pidx7", [P, 7])

        WORK = 17080
        work = sb("work", [P, WORK])
        worki = work[:].bitcast(I32)
        at = [0]

        def area(size, parts=P, ints=False):
            a = at[0]
            at[0] += size
            assert at[0] <= WORK, at[0]
            return (worki if ints else work)[0:parts, a:a + size]

        ld_i, ld_f = area(WHOLE, 1, True), area(WHOLE, 1)
        before, stepk, moved = area(WHOLE, NB), area(SW, NB), area(SW, NB)
        kcol, bcol, tcol, tcol_i = area(SC), area(SC), area(SC), area(SC, ints=True)
        b128 = area(SC)
        bthr, bnum, cnt, key = area(1, NB), area(1, NB), area(1, NB), area(1, NB)
        pad_i = area(2 * (EP - EDGES), 1, True).rearrange("p (k e) -> p k e", k=2)
        rows_i = area(2 * SW, ints=True).rearrange("p (k c e) -> p k c e", k=2, c=SC)
        rows_f = area(2 * SW).rearrange("p (k c e) -> p k c e", k=2, c=SC)
        stats = area(48).rearrange("p (t k) -> p t k", k=6)
        mv = [area(16).rearrange("p (t k) -> p t k", k=2) for _ in range(2)]
        rstd = [area(8) for _ in range(2)]
        attb = area(2 * D).rearrange("p (k f) -> p k f", k=2)
        xs = [area(D) for _ in range(2)]
        xts = [area(D).rearrange("p (c n) -> p c n", c=C) for _ in range(2)]
        prod = area(2 * C * D).rearrange("p (k c f) -> p k c f", k=2, c=C)
        ext, exb, exm, exr, exd = area(16), area(16), area(8), area(1, 16), area(16, 16)
        ht = area(16 * HW).rearrange("p (t f) -> p t f", f=HW)
        sm = area(NT * HEADS).rearrange("p (n k) -> p n k", k=HEADS)

        at[0] = 0
        gath = area(BODY * ROW).rearrange("p (t f) -> p t f", f=ROW)
        oh = [area(QUAD * P).rearrange("p (t d) -> p t d", t=QUAD) for _ in range(4)]
        oht = area(QUAD * P).rearrange("p (t d) -> p t d", t=QUAD)
        et, el = area(QUAD * HEADS).rearrange("p (t k) -> p t k", t=QUAD), area(QUAD * HEADS).rearrange("p (t k) -> p t k", t=QUAD)
        eu = [area(QUAD * HEADS).rearrange("p (t k) -> p t k", t=QUAD) for _ in range(2)]
        ev = area(QUAD * HEADS).rearrange("p (t k) -> p t k", t=QUAD)
        kxs = area(2 * D).rearrange("p (c n) -> p c n", c=C)
        ea, eb, ph, qn = area(2 * D), area(2 * D), area(2 * D), area(2 * D)
        xg = area(2 * XW).rearrange("p (t f) -> p t f", f=XW)
        xr, xo = area(2 * D).rearrange("p (t f) -> p t f", f=D), area(2 * D).rearrange("p (t f) -> p t f", f=D)
        rq, rq2, rqx = area(16), area(16), area(2 * D)
        kvg = area(C * XW).rearrange("p (m f) -> p m f", m=C)
        gT, kvm, ksr = area(C * D), area(C * P).rearrange("p (m f) -> p m f", m=C), area(D, 1)

        at[0] = 0
        ys = [area(2 * D).rearrange("p (t f) -> p t f", f=D) for _ in range(2)]
        xa = [area(2 * D).rearrange("p (t f) -> p t f", f=D) for _ in range(2)]
        st2 = area(12).rearrange("p (t k) -> p t k", k=6)
        mv2 = [area(4).rearrange("p (t k) -> p t k", k=2) for _ in range(2)]
        mrow, mcol, rt, sel, selb = area(D, 1), area(C), area(128, 1), area(4, 1), area(4)
        eidx = area(7 * TOPK, ints=True).rearrange("p (e k) -> p e k", k=7)
        w1s = area(TOPK * C * HIDDEN).rearrange("p (e c f) -> p e c f", e=TOPK, c=C)
        w2s = area(EJ * D).rearrange("p (k f) -> p k f", f=D)
        b1s = area(EJ)
        b2s = area(TOPK * D).rearrange("p (e f) -> p e f", e=TOPK)
        b2w = dl[:, 2 * D:3 * D]
        hT = area(EJ * 4 * P).rearrange("p (k n) -> p k n", k=EJ)
        zt, ot = ([area(D) for _ in range(2)] for _ in range(2))
        yb = [dl[:, D * k:D * k + D] for k in range(2)]
        st3, mv3 = area(6), area(2)

        const, ld, pads, padded, wts, w_att = (sem(n) for n in ("const", "ld", "pads", "padded", "weights", "w_att"))
        setup_dve, setup_pe, rows_got, watt = (sem(n) for n in ("setup_dve", "setup_pe", "rows_got", "watt"))
        x_in = [sem(f"x_in{i}") for i in range(2)]
        rstd_made, rstd2_made, rstd3_made = (sem(n) for n in ("rstd_made", "rstd2_made", "rstd3_made"))
        stat, xs_made, xn_made, xs_turned, xts_out, xts_kept = (sem(n) for n in ("stat", "xs_made", "xn_made", "xs_turned", "xts_out", "xts_kept"))
        h_made, ht_out, aa_kept, xn_stored = (sem(n) for n in ("h_made", "ht_out", "aa_kept", "xn_stored"))
        stored = [sem(f"table_stored{i}") for i in range(2)]
        rows_turned, srci_made, shift_dve, shift_pe, sm_ready, shift_ready = (sem(n) for n in ("rows_turned", "srci_made", "shift_dve", "shift_pe", "sm_ready", "shift_ready"))
        gen_dve, gen_pe, gen_pool, gen_dma, gen_copy, gen_copy2, gen_got, gen_put, gen_scan, gen_done = (
            sem(n) for n in ("gen_dve", "gen_pe", "gen_pool", "gen_dma", "gen_copy", "gen_copy2", "gen_got", "gen_put",
                             "gen_scan", "gen_done"))
        acc_zero, seeded = sem("acc_zero"), sem("seeded")
        idx_staged, oh_made, oh_turned, oht_out, ad_made, eu_made, eu_pos, p_made, weighed, summed, added = (
            sem(n) for n in ("idx_staged", "oh_made", "oh_turned", "oht_out", "ad_made", "eu_made", "eu_pos", "p_made",
                             "weighed", "summed", "added"))
        e_dve = sem("e_dve")
        got = [sem(f"gathered{i}") for i in range(BODY)]
        xg_in, kx_out, k_made, k_out, phi_made, g_made = (sem(n) for n in ("xg_in", "kx_out", "k_made", "k_out", "phi_made", "g_made"))
        m_dve, m_pe = sem("m_dve"), sem("m_pe")
        xr_in, q_made, q_out, phiq_made, norm_made, norm_dve, rq_made, rqx_made, rq_spread, qn_made, att_made, xo_made, xo_stored, xo_free = (
            sem(n) for n in ("xr_in", "q_made", "q_out", "phiq_made", "norm_made", "norm_dve", "rq_made", "rqx_made",
                             "rq_spread", "qn_made", "att_made", "xo_made", "xo_stored", "xo_free"))
        den_done, x1_dve, x1_made, y_made, y_turned, y_out, y_used = (sem(n) for n in ("den_done", "x1_dve", "x1_made", "y_made", "y_turned", "y_out", "y_used"))
        xa_in = [sem(f"xa_in{i}") for i in range(2)]
        route_dve, route_pe, route_act, w_picked, w2_scaled = (sem(n) for n in ("route_dve", "route_pe", "route_act", "w_picked", "w2_scaled"))
        hid_made, hid_out, moe_made, yb_made, yb_full, z_made, z_dve, zn_made, zg_made, out_made = (
            sem(n) for n in ("hid_made", "hid_out", "moe_made", "yb_made", "yb_full", "z_made", "z_dve", "zn_made", "zg_made", "out_made"))
        out_stored = [sem(f"out_stored{i}") for i in range(2)]

        def field(a, ints=False):
            return (acc[:].bitcast(I32) if ints else acc[:])[0:CH, CL * a:CL * a + CL]

        score = acc[0:CH, 0:CL * HEADS].rearrange("p (j k) -> p j k", k=HEADS)
        f_step, f_dst, i_src, i_dst, i_to = field(8), field(9), field(10, True), field(11, True), field(12, True)
        gx = acc[0:CH, CL * 13:CL * 13 + 16 * HEADS].rearrange("p (j k) -> p j k", k=HEADS)
        gi = acc[:].bitcast(I32)[0:CH, CL * 13 + 128:CL * 13 + 144]
        ends = acc[0:CH, CL * 13 + 144:CL * 13 + 168].rearrange("p (a k) -> p a k", k=HEADS)
        f_next = acc[0:CH, CL * 13 + 168:CL * 13 + 169]
        i_next = acc[:].bitcast(I32)[0:CH, CL * 13 + 169:CL * 13 + 170]
        carry = acc[0:CH, CL * 13 + 176:CL * 13 + 184]
        erow = acc[0:HEADS, CL * 13 + 184:CL * 13 + 184 + 3 * CH].rearrange("p (a c) -> p a c", a=3)
        crow = acc[0:HEADS, CL * 13 + 520:CL * 13 + 520 + 3 * CH].rearrange("p (a c) -> p a c", a=3)
        FAR = 65536.0

        def exact_maxima_pool(pool):
            dst_flat, src_flat = dst_pad.rearrange("t e -> (t e)"), src_pad.rearrange("t e -> (t e)")
            pool.wait_ge(xn_stored, 16 * 7)
            pool.memset(i_next, PAD_DST + 1).then_inc(gen_pool, 1)
            pool.wait_ge(gen_pool, 1)
            pool.dma_start(i_src, src_flat.rearrange("(p j) -> p j", j=CL)).then_inc(gen_dma, 16)
            pool.dma_start(i_dst, dst_flat.rearrange("(p j) -> p j", j=CL)).then_inc(gen_dma, 16)
            with nc.allow_non_contiguous_dma(reason="one number for each chunk"):
                pool.dma_start(i_next[0:CH - 1, :], dst_flat.rearrange("(p j) -> p j", j=CL)[1:CH, 0:1]).then_inc(gen_dma, 16)
            for t in (asrc_tab, smax_tab):
                pool.dma_start(t.rearrange("(n p) f -> p n f", p=P), aav[:, :, 0:HEADS]).then_inc(gen_dma, 16)
            pool.wait_ge(gen_dma, 80)
            pool.sem_inc(gen_pool, 1)
            with pool.Fori(0, CL // 16) as i:
                pool.tensor_copy(gi, i_src[:, bass.ds(16 * i, 16)]).then_inc(gen_copy, 1)
                pool.wait_ge(gen_copy, 2 * i + 1)
                settle(pool)                   
                for j in range(16):
                    pool.indirect_dma_start(out=gx[:, j, :], out_offset=None, in_=asrc_tab[:, :],
                                            in_offset=bass.IndirectOffsetOnAxis(ap=gi[:, j:j + 1], axis=0)).then_inc(gen_got, 16)
                pool.wait_ge(gen_got, 256 * i + 256)
                pool.tensor_copy(score[:, bass.ds(16 * i, 16), :], gx).then_inc(gen_copy, 1)
                pool.wait_ge(gen_copy, 2 * i + 2)
                settle(pool)
            pool.sem_inc(gen_pool, 1)
            pool.wait_ge(gen_done, 1)
            with pool.Fori(0, CL // 16) as i:
                pool.tensor_copy(gi, i_to[:, bass.ds(16 * i, 16)]).then_inc(gen_copy2, 1)
                pool.tensor_copy(gx, score[:, bass.ds(16 * i, 16), :]).then_inc(gen_copy2, 1)
                pool.wait_ge(gen_copy2, 2 * i + 2)
                settle(pool)
                for j in range(16):
                    pool.indirect_dma_start(out=smax_tab[:, :], out_offset=bass.IndirectOffsetOnAxis(ap=gi[:, j:j + 1], axis=0),
                                            in_=gx[:, j, :], in_offset=None, bounds_check=NP - 1, oob_is_err=False).then_inc(gen_put, 16)
                pool.wait_ge(gen_put, 256 * i + 256)
                settle(pool)
            pool.dma_start(sm, smax_tab.rearrange("(n p) f -> p n f", p=P)).then_inc(gen_dma, 16)
            pool.wait_ge(gen_dma, 96)

        def exact_maxima_pe(pe):
            pe.wait_ge(gen_dve, 6)
            for a in range(3):
                last = pe.matmul(bank[0][0:HEADS, a * CH:a * CH + CH], ends[:, a, :], ident[0:CH, 0:CH], start=True, stop=True)
            last.then_inc(gen_pe, 1)
            pe.wait_ge(gen_dve, 12)
            pe.matmul(bank[1][0:CH, 0:HEADS], crow[:, 2, :], ident[0:HEADS, 0:HEADS], start=True, stop=True).then_inc(gen_pe, 1)

        def exact_maxima_dve(dve, linker):
            then = linker(gen_dve)
            dve.wait_ge(gen_pool, 2)
            dve.tensor_copy(f_next, i_next)
            then(dve.tensor_copy(f_dst, i_dst))
            dve.tensor_tensor(f_step[:, 0:CL - 1], f_dst[:, 0:CL - 1], f_dst[:, 1:CL], ALU.is_equal)
            then(dve.tensor_tensor(f_step[:, CL - 1:CL], f_dst[:, CL - 1:CL], f_next, ALU.is_equal))
            then(dve.scalar_tensor_tensor(out=i_to, in0=f_step, scalar=FAR, in1=f_dst, op0=ALU.mult, op1=ALU.add))
            dve.tensor_tensor(f_step[:, 1:CL], f_dst[:, 1:CL], f_dst[:, 0:CL - 1], ALU.not_equal)
            dve.memset(f_step[:, 0:1], 1.0)
            dve.wait_ge(gen_pool, 3)
            then(dve.tensor_copy(ends[:, 1, :], f_dst[:, CL - 1:CL].broadcast_to([CH, HEADS])))
            dve.tensor_copy(ends[:, 2, :], f_dst[:, 0:1].broadcast_to([CH, HEADS]))
            then(dve.tensor_scalar(f_step, f_step, LOW, None, ALU.mult))
            for k in range(HEADS):
                last = dve.tensor_tensor_scan(score[:, :, k], f_step, score[:, :, k], LOW, ALU.add, ALU.max)
            last.then_inc(gen_scan, 1)
            dve.wait_ge(gen_scan, 1)
            then(dve.tensor_copy(ends[:, 0, :], score[:, CL - 1, :]))
            dve.wait_ge(gen_pe, 1)
            then(dve.tensor_copy(erow, bank[0][0:HEADS, 0:3 * CH].rearrange("p (a c) -> p a c", a=3)))
            dve.memset(crow[:, 0, 0:1], LOW)
            dve.memset(crow[:, 2, 0:1], LOW)
            then(dve.tensor_tensor(crow[:, 0, 1:CH], erow[:, 1, 1:CH], erow[:, 1, 0:CH - 1], ALU.not_equal))
            then(dve.tensor_scalar(crow[:, 0, 1:CH], crow[:, 0, 1:CH], LOW, None, ALU.mult))
            dve.tensor_tensor(crow[:, 2, 1:CH], erow[:, 2, 1:CH], erow[:, 1, 0:CH - 1], ALU.not_equal)
            then(dve.tensor_tensor_scan(crow[:, 1, :], crow[:, 0, :], erow[:, 0, :], LOW, ALU.add, ALU.max))
            then(dve.tensor_scalar(crow[:, 2, 1:CH], crow[:, 2, 1:CH], LOW, None, ALU.mult))
            then(dve.tensor_add(crow[:, 2, 1:CH], crow[:, 2, 1:CH], crow[:, 1, 0:CH - 1]))
            dve.wait_ge(gen_pe, 2)
            dve.tensor_copy(carry, bank[1][0:CH, 0:HEADS])
            then(dve.tensor_scalar(f_step, f_dst, f_dst[:, 0:1], None, ALU.not_equal))
            then(dve.tensor_scalar(f_step, f_step, LOW, None, ALU.mult))
            for k in range(HEADS):
                last = dve.scalar_tensor_tensor(out=score[:, :, k], in0=f_step, scalar=carry[:, k:k + 1], in1=score[:, :, k], op0=ALU.add, op1=ALU.max)
            last.then_inc(gen_done, 1)

        block = ctx.enter_context(nc.Block())
        settled = sem("settled")

        def settle(eng):
            eng.sem_inc(settled, 1)

        def blocks_of(engine, starts, width, k, n):
            return nc.values_load_multi_w_load_instructions(
                starts[0:1, bass.ds(k, n)], engines=[engine], min_val=0, max_val=NB * width,
                skip_runtime_bounds_check_because="a block is the sum of NB comparisons, times width")[1]

        def rows_of(t, i, n=1):
            return t[bass.ds(i * P, n * P), :].rearrange("(n p) f -> p n f", p=P)

        @block.sync
        def _(sp):
            with nc.allow_non_contiguous_dma(reason="the last destination of each edge tile"):
                sp.dma_start(ld_i, dst[0:WHOLE * P].rearrange("(t e) -> e t", e=P)[P - 1:P, :]).then_inc(ld, 16)
            for h in range(2):
                sp.dma_start(accx[:, 8 * h:8 * h + 8, :], rows_of(x, 8 * h, 8)).then_inc(x_in[h], 16)
            for k, (a, b) in enumerate(((src, src_pad), (dst, dst_pad))):
                flat = b.rearrange("t e -> (t e)")
                sp.dma_start(flat[0:EDGES].rearrange("(a b) -> a b", a=32), a.rearrange("(a b) -> a b", a=32)).then_inc(padded, 16)
                if k == 0:
                    sp.wait_ge(pads, 2)
                sp.dma_start(flat[EDGES:EP].rearrange("(a b) -> a b", a=1), pad_i[:, k, :]).then_inc(padded, 16)
            for t, w in ((wg[:, :, 0:D], gW), (wks[:], wk), (wqs[:], wq), (wvs[:], wv), (wos[:], wo), (wrs[:], Wr)):
                sp.dma_start(t, w.rearrange("(c p) f -> p c f", p=P)).then_inc(wts, 16)
            for t, w in ((bks, bk), (bvs, bv), (bos, bo), (gbs, g_bias), (brs, br)):
                sp.dma_start(t[:], w.rearrange("(a f) -> a f", a=1)).then_inc(wts, 16)
            with nc.allow_non_contiguous_dma(reason="256 numbers"):
                sp.dma_start(bqs[:], bq.rearrange("(c p) -> p c", p=P)).then_inc(wts, 16)
            for k, (t, w) in enumerate(((gam, gamma), (bet, beta))):
                sp.dma_start(t[:], w.rearrange("(a f) -> a f", a=1).broadcast_to([P, D])).then_inc(out_stored[k], 16)
            for k, w in enumerate((g_as, g_ad)):
                sp.dma_start(attb[:, k, :], w.rearrange("(a h) f -> a (h f)", a=1).broadcast_to([P, D])).then_inc(stored[k], 16)

            def store(u, h):
                g = 2 * u + h
                sp.wait_ge(ht_out, 8 * (g + 1) + 2)
                sp.dma_start(rows_of(table, 8 * g, 8), ht[:, 8 * h:8 * h + 8, 0:ROW]).then_inc(stored[h], 16)
                sp.wait_ge(xn_made, 8 * (g + 1))
                sp.dma_start(rows_of(xn_d, 8 * g, 8), accx[:, bass.ds(8 * g, 8), :]).then_inc(xn_stored, 16)

            with sp.Fori(0, 2) as u:
                for h in range(2):
                    store(u, h)
                    sp.dma_start(accx[:, bass.ds(16 * u + 16 + 8 * h, 8), :], rows_of(x, 16 * u + 16 + 8 * h, 8)).then_inc(x_in[h], 16)
            store(2, 0)
            sp.wait_ge(const, CONSTS)
            sp.dma_start(accx[0:LAST, NT - 1, :], x[(NT - 1) * P:N, :]).then_inc(x_in[0], 16)
            store(2, 1)
            sp.wait_ge(ht_out, NT + 2)
            sp.dma_start(table[(NT - 1) * P:NP, :], ht[:, 0, 0:ROW]).then_inc(stored[0], 16)
            sp.wait_ge(xn_made, NT)
            sp.dma_start(xn_d[(NT - 1) * P:NP, :], accx[:, NT - 1, :]).then_inc(xn_stored, 16)
            sp.wait_ge(xn_stored, 16 * 7)

            def kv(r, w=2):
                sp.wait_ge(g_made, r + 1)
                if w == 2:
                    sp.dma_start(xg[:, :, 0:D], rows_of(xn_d, 2 * r, 2)).then_inc(xg_in, 16)
                else:
                    sp.dma_start(xg[:, 0, 0:D], xn_d[(NT - 1) * P:NP, :]).then_inc(xg_in, 16)

            def att(r, w=2):
                sp.wait_ge(xo_made, r + 1)
                if w == 2:
                    sp.dma_start(xr, rows_of(x, 2 * r, 2)).then_inc(xr_in, 16)
                else:
                    sp.dma_start(xr[0:LAST, 0, :], x[(NT - 1) * P:N, :]).then_inc(xr_in, 16)
                sp.wait_ge(xo_made, r + 2)
                if w == 2:
                    sp.dma_start(rows_of(xa_d, 2 * r, 2), xo).then_inc(xo_stored, 16)
                else:
                    sp.dma_start(xa_d[(NT - 1) * P:NP, :], xo[:, 0, :]).then_inc(xo_stored, 16)
                sp.wait_ge(xo_stored, 16 * (r + 1))
                sp.sem_inc(xo_free, 1)

            with sp.Fori(0, PAIRS) as r:
                kv(r)
            kv(PAIRS, 1)
            with sp.Fori(0, PAIRS) as r:
                att(r)
            att(PAIRS, 1)

            def p2(r, q, w=2):
                sp.wait_ge(x1_made, r + 1)
                if w == 2:
                    sp.dma_start(xa[q], rows_of(xa_d, 2 * r, 2)).then_inc(xa_in[q], 16)
                else:
                    sp.dma_start(xa[q][:, 0, :], xa_d[(NT - 1) * P:NP, :]).then_inc(xa_in[q], 16)

            with sp.Fori(0, PAIRS // 2) as u:
                for q in range(2):
                    p2(2 * u + q, q)
            p2(PAIRS, 0, 1)

            with sp.Fori(0, PAIRS) as u:
                for q in range(2):
                    sp.wait_ge(out_made, 2 * u + q + 1 + 2)
                    sp.dma_start(out[bass.ds((2 * u + q) * P, P), :], ot[q]).then_inc(out_stored[q], 16)
            sp.wait_ge(out_made, NT + 2)
            sp.dma_start(out[(NT - 1) * P:N, :], ot[0][0:LAST, :]).then_inc(out_stored[0], 16)
            sp.wait_ge(out_stored[0], 16 * (PAIRS + 2))
            sp.wait_ge(out_stored[1], 16 * (PAIRS + 1))

        @block.gpsimd
        def _(pool):
            n = [0]

            def link(ins):
                n[0] += 1
                ins.then_inc(const, 1)
                pool.wait_ge(const, n[0])

            pool.memset(pad_i[:, 0, :], 0).then_inc(pads, 1)
            pool.memset(pad_i[:, 1, :], PAD_DST).then_inc(pads, 1)
            link(pool.memset(ones[:], 1.0))
            pool.memset(half[:], -0.5)
            link(pool.memset(zeros[:], 0.0))
            link(pool.memset(ident[:], 0.0))
            link(pool.affine_select(out=ident[:], in_=ident[:], compare_op=ALU.not_equal, fill=1.0, base=0,
                                    pattern=[[-1, P]], channel_multiplier=1))
            link(pool.iota(bnum, [[0, 1]], base=1, channel_multiplier=1, allow_small_or_imprecise_dtypes=True))
            link(pool.iota(bthr, [[0, 1]], base=P, channel_multiplier=P, allow_small_or_imprecise_dtypes=True))
            link(pool.iota(stepk, [[1, SW]], base=0, channel_multiplier=0, allow_small_or_imprecise_dtypes=True))
            link(pool.iota(kcol, [[P, SC]], base=0, channel_multiplier=1, allow_small_or_imprecise_dtypes=True))
            link(pool.iota(iota_f[:], [[1, P]], base=0, channel_multiplier=0, allow_small_or_imprecise_dtypes=True))
            link(pool.memset(headmask[:], 0.0))
            for k in range(P // FH):
                last = pool.memset(headmask[FH * k:FH * k + FH, FH * k:FH * k + FH], 1.0)
            link(last)
            link(pool.memset(kbmask[:], 0.0))
            for c in range(C):
                for k in range(P // FH):
                    last = pool.memset(kbmask[FH * k:FH * k + FH, c, 4 * c + k:4 * c + k + 1], 1.0)
            link(last)
            for k, rows in enumerate((D, D, HIDDEN, HIDDEN, HIDDEN, HIDDEN, 1)):
                off = (0, P, 0, P, 2 * P, 3 * P, 0)[k]
                last = pool.memset(mult7[:, k:k + 1], float(rows))
                pool.iota(pidx7[:, k:k + 1], [[0, 1]], base=off, channel_multiplier=1 if k < 6 else 0, allow_small_or_imprecise_dtypes=True)
            link(last)
            link(pool.memset(accx[:, NT - 1, :], 0.0))
            assert n[0] == CONSTS, n[0]
            pool.wait_ge(setup_dve, 8)
            pool.wait_ge(padded, 64)
            for k, t in enumerate((src_pad, dst_pad)):
                for c in range(SC):
                    pool.indirect_dma_start(out=rows_i[:, k, c, :], out_offset=None, in_=t[:, :],
                                            in_offset=bass.IndirectOffsetOnAxis(ap=tcol_i[:, c:c + 1], axis=0)).then_inc(rows_got, 16)
            pool.wait_ge(wts, 16 * WEIGHTS)
            pool.tensor_add(bsum[:], bos[:], gbs[:]).then_inc(const, 1)

            def keep(i, j, q):
                pool.wait_ge(xts_out, i + 1 + 2)
                pool.tensor_copy(xTv[:, :, bass.ds(i * P, P)], xts[q]).then_inc(xts_kept, 1)
                pool.wait_ge(ht_out, i + 1 + 2)
                pool.tensor_copy(aav[:, bass.ds(i, 1), 0:16], ht[:, j:j + 1, D:HW]).then_inc(aa_kept, 1)

            pool.sem_inc(xts_kept, 2)
            pool.sem_inc(aa_kept, 16)
            def deviation(g, h, width=8):
                pool.wait_ge(stat, 3 * g + 3)
                pool.tensor_tensor(rstd[h][:, 0:width], mv[h][:, 0:width, 1], half[:, 0:width], ALU.pow).then_inc(rstd_made, 1)

            def round_(u, last=False):
                for h in range(2):
                    deviation(2 * u + h + 1, 1 - h, 1 if last and h else 8)
                    for j in range(8):
                        keep(16 * u + 8 * h + j, 8 * h + j, j % 2)

            deviation(0, 0)
            with pool.Fori(0, 2) as u:
                round_(u)
            round_(2, last=True)
            keep(NT - 1, 0, 0)

            pool.wait_ge(shift_dve, 8)
            general = pool.value_load(flag[0:1, 0:1], min_val=0, max_val=1)
            with pool.If(general):
                exact_maxima_pool(pool)
            pool.sem_inc(sm_ready, 1)

            pool.wait_ge(stored[0], 16 * 5)
            pool.wait_ge(stored[1], 16 * 4)

            def gathers(i):
                for j in range(BODY):
                    if j % QUAD == 0:
                        pool.wait_ge(idx_staged, 4 * i + j // QUAD + 1)
                        pool.wait_ge(summed, BODY * i + j + QUAD)
                        settle(pool)                  
                    pool.indirect_dma_start(out=gath[:, j, :], out_offset=None, in_=table[:, :],
                                            in_offset=bass.IndirectOffsetOnAxis(ap=idx[:, j:j + 1], axis=0)).then_inc(got[j], 16)

            with pool.Fori(0, BODIES) as i:
                gathers(i)

            def deviation2(r, q, w=2):
                pool.wait_ge(x1_dve, 4 * r + 4)
                pool.tensor_tensor(mv2[q][:, 0:w, 1], mv2[q][:, 0:w, 1], half[:, 0:w], ALU.pow).then_inc(rstd2_made, 1)

            with pool.Fori(0, PAIRS // 2) as u:
                for q in range(2):
                    deviation2(2 * u + q, q)
            deviation2(PAIRS, 0, 1)

            pool.wait_ge(route_dve, ROUTE)
            for e in range(TOPK):
                def pick(out_, tab, k):
                    pool.indirect_dma_start(out=out_, out_offset=None, in_=tab,
                                            in_offset=bass.IndirectOffsetOnAxis(ap=eidx[:, e, k:k + 1], axis=0)).then_inc(w_picked, 16)
                for c in range(C):
                    pick(w1s[:, e, c, :], W1.rearrange("e d f -> (e d) f"), c)
                for j in range(FJ):
                    pick(w2s[:, e * FJ + j, :], W2.rearrange("e f d -> (e f) d"), 2 + j)
                    pick(b1s[:, e * FJ + j:e * FJ + j + 1], b1.rearrange("e (f a) -> (e f) a", a=1), 2 + j)
                pick(b2s[:, e, :], b2[:, :], 6)

            pool.wait_ge(out_stored[0], 16)
            pool.wait_ge(out_stored[1], 16)

            def tail(i, q, u):
                pool.wait_ge(yb_made, i + 1)
                pool.tensor_add(yb[q], yb[q], b2w).then_inc(yb_full, 1)
                pool.wait_ge(z_dve, 3 * i + 3)
                pool.tensor_tensor(mv3[:, 1:2], mv3[:, 1:2], half[:, 0:1], ALU.pow).then_inc(rstd3_made, 1)
                pool.wait_ge(zn_made, i + 1)
                pool.tensor_mul(zt[q], zt[q], gam[:]).then_inc(zg_made, 1)
                pool.wait_ge(zg_made, 2 * i + 1)
                pool.tensor_add(zt[q], zt[q], bet[:]).then_inc(zg_made, 1)
                pool.wait_ge(zg_made, 2 * i + 2)
                pool.wait_ge(out_stored[q], 16 * u + 16)
                pool.tensor_add(ot[q], zt[q], accv[:, bass.ds(i, 1), 0:D].rearrange("p a f -> p (a f)")).then_inc(out_made, 1)

            pool.wait_ge(w2_scaled, 1)
            pool.sem_inc(out_made, 2)
            with pool.Fori(0, PAIRS) as u:
                for q in range(2):
                    tail(2 * u + q, q, u)
            tail(NT - 1, 0, PAIRS)

        @block.scalar
        def _(act):
            act.sem_inc(xts_out, 2)
            act.sem_inc(ht_out, 2)

            def turn_out(i, q):
                act.wait_ge(xs_turned, i + 1 + 2)
                act.wait_ge(h_made, i + 1)
                act.wait_ge(xts_kept, i + 1)
                act.copy(xts[q], bank[q][:, 0:D].rearrange("p (c n) -> p c n", c=C)).then_inc(xts_out, 1)

            def h_out(i, j, q, u, first):
                act.wait_ge(h_made, i + 1 + 2)
                if first:
                    act.wait_ge(stored[j // 8], 16 * u + 16)
                act.wait_ge(aa_kept, i + 1)
                act.copy(ht[:, j, :], bank[2 + q][:, 0:HW]).then_inc(ht_out, 1)

            with act.Fori(0, 3) as u:
                for j in range(0, 16, 2):
                    for q in range(2):
                        turn_out(16 * u + j + q, q)
                    for q in range(2):
                        h_out(16 * u + j + q, j + q, q, u, (j + q) % 8 == 0)
            turn_out(NT - 1, 0)
            h_out(NT - 1, 0, 0, 3, True)

            act.wait_ge(srci_made, 1)
            act.copy(idx[:], srci[:, 0:BODY]).then_inc(idx_staged, 4)
            act.wait_ge(shift_ready, 1)

            def oht_evac(q):
                act.wait_ge(oh_turned, q + 1)
                act.wait_ge(ad_made, q + 1)
                act.copy(oht, bank[2][:].rearrange("p (t d) -> p t d", t=QUAD)).then_inc(oht_out, 1)

            def stage(q, j):
                o = QUAD * (j % 4)
                act.copy(idx[:, o:o + QUAD], srci[:, bass.ds(QUAD * q + BODY, QUAD)]).then_inc(idx_staged, 1)

            def p_of(q, j):
                act.wait_ge(eu_made, q + 1)
                act.activation(ev, eu[j % 2], ACT.Relu).then_inc(eu_pos, 1)
                act.wait_ge(eu_pos, q + 1)
                act.activation(gath[:, 4 * (j % 4):4 * (j % 4) + 4, D:ROW], ev, ACT.Exp, scale=-1.0).then_inc(p_made, 1)

            def kv_h0(r, w=2):
                n = w * P
                act.wait_ge(k_made, r + 1)
                act.copy(kxs[:, :, 0:n], xTv[:, :, bass.ds(2 * P * r, n)]).then_inc(kx_out, 1)
                act.wait_ge(k_made, r + 2)
                act.wait_ge(phi_made, r + 1)
                act.activation(ea[:, 0:w * D], bank[5][:, 0:w * D], ACT.Exp)
                act.activation(eb[:, 0:w * D], bank[5][:, 0:w * D], ACT.Relu).then_inc(k_out, 1)

            def att_h0(r, w=2):
                n = w * P
                act.wait_ge(q_made, r + 1)
                act.wait_ge(phiq_made, r + 1)
                for m in range(C):
                    sl = slice(m * 2 * P, m * 2 * P + n)
                    act.activation(ea[:, sl], bank[5][:, sl], ACT.Exp, bias=bqs[:, m:m + 1])
                    last = act.activation(eb[:, sl], bank[5][:, sl], ACT.Relu, bias=bqs[:, m:m + 1])
                last.then_inc(q_out, 1)

            def att_h1(r, w=2):
                act.wait_ge(rq_made, r + 1)
                act.wait_ge(rq_spread, r + 1)
                act.copy(rqx[:, 0:w * D].rearrange("p (k f) -> p k f", f=FH),
                         rq[:, 0:w * HEADS].unsqueeze(2).broadcast_to([P, w * HEADS, FH])).then_inc(rqx_made, 1)

            def body(i, hooks, last=False):
                for j in range(4):
                    q = 4 * i + j
                    if not (last and j == 3):
                        p_of(q + 1, j + 1)
                    if not last:
                        stage(q + 1, j + 1)
                    if not (last and j >= 2):
                        oht_evac(q + 2)
                    if j in hooks:
                        hooks[j]()

            act.sem_inc(k_out, 1)
            act.sem_inc(q_out, 1)
            oht_evac(0)
            p_of(0, 0)
            stage(0, 0)
            oht_evac(1)
            with act.Fori(0, PAIRS) as i:
                body(i, {0: lambda: kv_h0(i)})
            body(PAIRS, {0: lambda: kv_h0(PAIRS, 1)})
            body(PAIRS + 1, {})
            A = PAIRS + 2
            with act.Fori(0, PAIRS) as r:
                body(A + r, {0: lambda: att_h0(r), 1: lambda: att_h1(r)})
            body(A + PAIRS, {0: lambda: att_h0(PAIRS, 1), 1: lambda: att_h1(PAIRS, 1)})
            body(BODIES - 1, {}, last=True)

            def y_evac(r, q, w=2):
                act.wait_ge(y_turned, r + 1)
                act.copy(xTv[:, :, bass.ds(2 * P * r, w * P)],
                         bank[q][:].rearrange("p (c n) -> p c n", c=C)[:, :, 0:w * P]).then_inc(y_out, 1)

            act.sem_inc(y_out, 2)
            with act.Fori(0, PAIRS // 2) as u:
                for q in range(2):
                    y_evac(2 * u + q, q)
            y_evac(PAIRS, 0, 1)

            for k, sl in enumerate((slice(16, 24), slice(40, 48), slice(90, 91))):
                act.wait_ge(route_dve, EXPS[k])
                act.activation(rt[:, sl], rt[:, sl], ACT.Exp).then_inc(route_act, 1)

            act.wait_ge(w_picked, 16 * TOPK * (C + 2 * FJ + 1))

            def hidden(g, w=4):
                for k in range(EJ):
                    act.wait_ge(hid_made, EJ * g + k + 1)
                    act.activation(hT[:, k, 0:w * P], bank[k % 4][:, 0:w * P], ACT.Gelu, bias=b1s[:, k:k + 1]).then_inc(hid_out, 1)

            act.sem_inc(hid_out, 4)
            with act.Fori(0, NT // 4) as g:
                hidden(g)
            hidden(NT // 4, 1)

        @block.tensor
        def _(pe):
            pe.wait_ge(const, CONSTS)
            pe.wait_ge(setup_dve, 1)
            cut = (0, 400, WHOLE)
            for k in range(2):
                last = pe.matmul(bank[k][0:NB, 0:cut[k + 1] - cut[k]], ones[0:1, 0:NB], ld_f[0:1, cut[k]:cut[k + 1]], start=True, stop=True)
            last.then_inc(setup_pe, 1)
            pe.wait_ge(setup_dve, 5)
            for k in range(2):
                pe.matmul(bank[2 + k][0:1, 0:SW // 2], ones[0:NB, 0:1], moved[:, k * SW // 2:(k + 1) * SW // 2], start=True, stop=True)
            for c in range(SC):
                last = pe.matmul(bank[4][:, c:c + 1], moved[:, c * P:c * P + P], ones[0:NB, 0:1], start=True, stop=True)
            last.then_inc(setup_pe, 1)

            pe.sem_inc(xs_turned, 2)
            pe.sem_inc(h_made, 2)
            pe.wait_ge(setup_dve, 8)
            pe.wait_ge(watt, 2)

            def turn(i, q):
                pe.wait_ge(xs_made, i + 1)
                pe.wait_ge(xts_out, i + 1)
                for c in range(C):
                    last = pe.transpose(bank[q][:, c * P:c * P + P], xs[q][:, c * P:c * P + P], ident[:])
                last.then_inc(xs_turned, 1)

            def project(i, q):
                pe.wait_ge(xts_out, i + 1 + 2)
                pe.wait_ge(ht_out, i + 1)
                for c in range(C):
                    last = pe.matmul(bank[2 + q][:, 0:HW], xts[q][:, c, :], wg[:, c, :], start=(c == 0), stop=(c == C - 1))
                last.then_inc(h_made, 1)

            with pe.Fori(0, 3) as u:
                for j in range(0, 16, 2):
                    for q in range(2):
                        turn(16 * u + j + q, q)
                    for q in range(2):
                        project(16 * u + j + q, q)
            turn(NT - 1, 0)
            project(NT - 1, 0)

            pe.wait_ge(setup_dve, 9)
            pe.wait_ge(ht_out, NT + 2)
            for k in (1, 0):
                for c in range(SC):
                    b = 2 * k + c // 4
                    last = pe.transpose(bank[b][:, c % 4 * P:c % 4 * P + P], rows_f[:, k, c, :], ident[:])
                last.then_inc(rows_turned, 1)
            pe.wait_ge(shift_dve, 2)
            pe.transpose(bank[4][0:16, 0:P], ext, ident[:]).then_inc(shift_pe, 1)
            pe.wait_ge(shift_dve, 4)
            pe.matmul(bank[4][:, 128:144], ones[0:16, :], exd, start=True, stop=True).then_inc(shift_pe, 1)
            pe.wait_ge(shift_dve, 8)
            general = pe.value_load(flag[0:1, 0:1], min_val=0, max_val=1)
            with pe.If(general):
                exact_maxima_pe(pe)

            pe.wait_ge(shift_ready, 1)
            pe.sem_inc(summed, BODY)
            pe.sem_inc(ad_made, 1)
            for m in range(C):
                pe.matmul(bank[6 + m][:, 0:XW], zeros[:, 0:P], zeros[:, :], start=True, stop=False)
            for t in (k_made, g_made, rq_spread, att_made):
                pe.sem_inc(t, 1)

            def turn_oh(q, j):
                pe.wait_ge(oh_made, q + 1)
                for t in range(QUAD):
                    last = pe.transpose(bank[2][:, t * P:t * P + P], oh[j % 4][:, t, :], ident[:])
                last.then_inc(oh_turned, 1)

            def spread_ad(q, b):
                pe.wait_ge(oht_out, q + 1)
                for t in range(QUAD):
                    last = pe.matmul(bank[2][:, 16 * t:16 * t + 16], oht[:, t, :], aa[:, 8:][:, bass.ds(b[t], 16)], start=True, stop=True)
                last.then_inc(ad_made, 1)

            def sum_up(q, j):
                pe.wait_ge(weighed, q + 1)
                for t in range(QUAD):
                    pe.wait_ge(added, QUAD * q + t + 1)
                    pe.matmul(bank[SUMS[t]][:, 0:ROW], oh[j % 4][:, t, :], gath[:, 4 * (j % 4) + t, :], start=True, stop=True).then_inc(summed, 1)

            def kv_h0(r, w=2):
                pe.wait_ge(kx_out, r + 1)
                pe.wait_ge(k_out, r + 1)
                for t in range(w):
                    o = bank[5][:, t * D:t * D + D]
                    pe.matmul(o, ones[0:1, :], bks[0:1, :], start=True, stop=False)
                    for c in range(C):
                        last = pe.matmul(o, kxs[:, c, t * P:t * P + P], wks[:, c, :], start=False, stop=(c == C - 1))
                last.then_inc(k_made, 1)

            def kv_h2(r, w=2):
                k = P if w == 2 else LAST
                pe.wait_ge(phi_made, r + 2)
                pe.wait_ge(xg_in, 16 * r + 16)
                for t in range(w):
                    for m in range(C):
                        last = pe.matmul(bank[6 + m][:, 0:XW], ph[0:k, t * D + m * P:t * D + m * P + P], xg[0:k, t, :],
                                         start=False, stop=(w == 1))
                last.then_inc(g_made, 1)

            def m_stage():
                pe.wait_ge(m_dve, 1)
                for c in range(C):
                    for m in range(C):
                        pe.transpose(bank[5][:, c * D + m * P:c * D + m * P + P], kvg[:, m, c * P:c * P + P], ident[:])
                for m in range(C):
                    last = pe.matmul(bank[6][0:1, m * P:m * P + P], kvg[:, m, D:XW], ident[:], start=True, stop=True)
                last.then_inc(m_pe, 1)
                pe.wait_ge(m_dve, 2)
                for m in range(C):
                    o = bank[7][:, m * P:m * P + P]
                    pe.matmul(o, bvs[0:1, m * P:m * P + P], ksr[0:1, m * P:m * P + P], start=True, stop=False)
                    for c in range(C):
                        last = pe.matmul(o, wvs[:, c, m * P:m * P + P], gT[:, c * D + m * P:c * D + m * P + P], start=False, stop=(c == C - 1))
                last.then_inc(m_pe, 1)
                pe.wait_ge(m_dve, 3)
                for m in range(C):
                    last = pe.matmul(bank[6][:, m * D:m * D + D], kvm[:, m, :], wos[:, m, :], start=True, stop=True)
                last.then_inc(m_pe, 1)
                pe.wait_ge(m_dve, 4)

            def att_h0(r, w=2):
                n = w * P
                pe.wait_ge(q_out, r + 1)
                for m in range(C):
                    for c in range(C):
                        last = pe.matmul(bank[5][:, m * 2 * P:m * 2 * P + n], wqs[:, c, m * P:m * P + P], xTv[:, c, bass.ds(2 * P * r, n)],
                                         start=(c == 0), stop=(c == C - 1))
                last.then_inc(q_made, 1)

            def att_h1(r, w=2):
                pe.wait_ge(phiq_made, r + 2)
                for t in range(w):
                    for m in range(C):
                        last = pe.matmul(bank[5][:, 8 * t:8 * t + 8], ph[:, m * 2 * P + t * P:m * 2 * P + t * P + P], kb[:, m, :],
                                         start=(m == 0), stop=(m == C - 1))
                last.then_inc(norm_made, 1)

            def att_h2(r, w=2):
                pe.wait_ge(rqx_made, r + 1)
                pe.wait_ge(qn_made, r + 1)
                for m in range(C):
                    for t in range(w):
                        last = pe.transpose(bank[6][:, m * 2 * P + t * P:m * 2 * P + t * P + P], rqx[:, t * D + m * P:t * D + m * P + P], ident[:])
                last.then_inc(rq_spread, 1)
                pe.wait_ge(qn_made, r + 2)
                pe.wait_ge(xo_made, r + 1)
                for t in range(w):
                    o = bank[7][:, t * D:t * D + D]
                    pe.matmul(o, ones[0:1, :], bsum[0:1, :], start=True, stop=False)
                    for m in range(C):
                        last = pe.matmul(o, qn[:, m * 2 * P + t * P:m * 2 * P + t * P + P], m_sb[:, m, :], start=False, stop=(m == C - 1))
                last.then_inc(att_made, 1)

            def body(i, hooks, last=False):
                b = blocks_of(mybir.EngineType.PE, brow_aa, 24, BODY * i + 2 * QUAD, 2 * QUAD if last else BODY)
                for j in range(4):
                    q = 4 * i + j
                    sum_up(q, j)
                    if not (last and j >= 2):
                        turn_oh(q + 2, j + 2)
                    if j in hooks:
                        hooks[j]()
                    if not (last and j >= 2):
                        spread_ad(q + 2, b[QUAD * j:QUAD * j + QUAD])

            b = blocks_of(mybir.EngineType.PE, brow_aa, 24, 0, 2 * QUAD)
            for q in range(2):
                turn_oh(q, q)
                spread_ad(q, b[QUAD * q:QUAD * q + QUAD])
            with pe.Fori(0, PAIRS) as i:
                body(i, {0: lambda: kv_h0(i), 2: lambda: kv_h2(i)})
            body(PAIRS, {0: lambda: kv_h0(PAIRS, 1), 2: lambda: kv_h2(PAIRS, 1)})
            body(PAIRS + 1, {0: m_stage})
            A = PAIRS + 2
            with pe.Fori(0, PAIRS) as r:
                body(A + r, {0: lambda: att_h0(r), 1: lambda: att_h1(r), 2: lambda: att_h2(r)})
            body(A + PAIRS, {0: lambda: att_h0(PAIRS, 1), 1: lambda: att_h1(PAIRS, 1), 2: lambda: att_h2(PAIRS, 1)})
            body(BODIES - 1, {}, last=True)

            pe.wait_ge(added, STEPS + 4)
            pe.matmul(bank[2][0:1, 0:D], zeros[:, 0:1], zeros[:, 0:D], start=True, stop=False)
            pe.sem_inc(y_used, 2)

            def turn_y(r, q, w=2):
                pe.wait_ge(y_made, r + 1)
                pe.wait_ge(y_out, r + 1)
                for c in range(C):
                    for t in range(w):
                        last = pe.transpose(bank[q][:, c * D + t * P:c * D + t * P + P], ys[q][:, t, c * P:c * P + P], ident[:])
                last.then_inc(y_turned, 1)
                k = P if w == 2 else LAST
                for t in range(w):
                    last = pe.matmul(bank[2][0:1, 0:D], ones[0:k, 0:1], ys[q][0:k, t, :], start=False, stop=(w == 1))
                last.then_inc(y_used, 1)

            with pe.Fori(0, PAIRS // 2) as u:
                for q in range(2):
                    turn_y(2 * u + q, q)
            turn_y(PAIRS, 0, 1)

            pe.wait_ge(route_dve, 1)
            for c in range(C):
                last = pe.matmul(bank[3][:, c:c + 1], mrow[0:1, c * P:c * P + P], ones[0:1, 0:1], start=True, stop=True)
            last.then_inc(route_pe, 1)
            pe.wait_ge(route_dve, 2)
            for c in range(C):
                last = pe.matmul(bank[3][0:1, 16:16 + EXPERTS], mcol[:, c:c + 1], wrs[:, c, :], start=(c == 0), stop=(c == C - 1))
            last.then_inc(route_pe, 1)
            pe.wait_ge(route_dve, ROUTE - 2)
            pe.matmul(bank[3][:, 32:36], ones[0:1, :], sel, start=True, stop=True).then_inc(route_pe, 1)

            pe.wait_ge(w_picked, 16 * TOPK * (C + 2 * FJ + 1))
            pe.wait_ge(w2_scaled, 1)
            pe.wait_ge(y_out, PAIRS + 3)

            def experts(g, w=4):
                n = w * P
                for k in range(EJ):
                    e, j = k // FJ, k % FJ
                    pe.wait_ge(hid_out, EJ * g + k + 1)
                    for c in range(C):
                        last = pe.matmul(bank[k % 4][:, 0:n], w1s[:, e, c, j * P:j * P + P], xTv[:, c, bass.ds(4 * P * g, n)],
                                         start=(c == 0), stop=(c == C - 1))
                    last.then_inc(hid_made, 1)
                for t in range(w):
                    pe.wait_ge(z_made, 4 * g + t + 1)
                    for k in range(EJ):
                        if t == 0:
                            pe.wait_ge(hid_out, EJ * g + k + 5)
                        last = pe.matmul(bank[4 + t % 2][:, 0:D], hT[:, k, t * P:t * P + P], w2s[:, k, :], start=(k == 0), stop=(k == EJ - 1))
                    last.then_inc(moe_made, 1)

            with pe.Fori(0, NT // 4) as g:
                experts(g)
            experts(NT // 4, 1)

        @block.vector
        def _(dve):
            def linker(s, n=0):
                count = [n]

                def then(ins):
                    count[0] = count[0] + 1
                    ins.then_inc(s, 1)
                    dve.wait_ge(s, count[0])
                return then

            then = linker(setup_dve)
            dve.wait_ge(ld, 16)
            then(dve.tensor_copy(ld_f, ld_i))
            dve.wait_ge(const, CONSTS)
            dve.wait_ge(setup_pe, 1)
            cut = (0, 400, WHOLE)
            for k in range(2):
                last = dve.tensor_scalar(before[:, cut[k]:cut[k + 1]], bank[k][0:NB, 0:cut[k + 1] - cut[k]], bthr, None, ALU.is_lt)
            then(last)
            then(dve.tensor_reduce(cnt, before, AX_X, ALU.add))
            then(dve.tensor_add(key, cnt, bnum))
            then(dve.tensor_scalar(moved, stepk, key, None, ALU.is_ge))
            dve.wait_ge(setup_pe, 2)
            for k in range(2):
                for t, width in ((brow_aa, 24), (brow_acc, ROW)):
                    dve.tensor_scalar(t[0:1, k * SW // 2:(k + 1) * SW // 2], bank[2 + k][0:1, 0:SW // 2], float(width), None, ALU.mult)
            then(dve.tensor_copy(bcol, bank[4][:, 0:SC]))
            dve.tensor_scalar(b128, bcol, float(P), None, ALU.mult)
            then(dve.scalar_tensor_tensor(out=tcol, in0=bcol, scalar=-1.0, in1=kcol, op0=ALU.mult, op1=ALU.add))
            then(dve.tensor_scalar(tcol_i, tcol, float(ET - 1), None, ALU.min))

            dve.wait_ge(wts, 16 * WEIGHTS)
            for k in range(2):
                dve.wait_ge(stored[k], 16)
                last = dve.tensor_mul(prod[:, k, :, :], wg[:, :, 0:D], attb[:, k:k + 1, :].broadcast_to([P, C, D]))
            last.then_inc(watt, 1)
            dve.wait_ge(watt, 1)
            for k in range(2):
                for c in range(C):
                    last = dve.tensor_reduce(wg[:, c, D + HEADS * k:D + HEADS * k + HEADS], prod[:, k, c, :].rearrange("p (h f) -> p h f", f=FH), AX_X, ALU.add)
            last.then_inc(watt, 1)

            def tile_of(i):
                return accx[:, bass.ds(i, 1), :].rearrange("p a f -> p (a f)")

            def statistics(g, h, u, width=8):
                dve.wait_ge(x_in[h], 16 * u + 16)
                then = linker(stat, 3 * g)
                settle(dve)                           
                for j in range(width):
                    last = dve.bn_stats(stats[:, j, :], tile_of(8 * g + j))
                then(last)
                settle(dve)
                for j in range(width):
                    last = dve.bn_aggr(mv[h][:, j, :], stats[:, j, :])
                then(last)
                dve.tensor_scalar(mv[h][:, 0:width, 1], mv[h][:, 0:width, 1], LN_EPS, None, ALU.add).then_inc(stat, 1)

            def normalize(g, h, width=8):
                dve.wait_ge(rstd_made, g + 1)
                for j in range(width):
                    xj = tile_of(8 * g + j)
                    mean, rs = mv[h][:, j, 0:1], rstd[h][:, j:j + 1]
                    dve.wait_ge(xs_turned, 8 * g + j + 1)
                    dve.tensor_scalar(xs[j % 2], xj, mean, rs, ALU.subtract, ALU.mult).then_inc(xs_made, 1)
                    dve.tensor_scalar(xj, xj, mean, rs, ALU.subtract, ALU.mult).then_inc(xn_made, 1)

            def round_(u, last=False):
                statistics(2 * u + 1, 1, u)
                normalize(2 * u, 0)
                statistics(2 * u + 2, 0, u + 1, 1 if last else 8)
                normalize(2 * u + 1, 1)

            statistics(0, 0, 0)
            with dve.Fori(0, 2) as u:
                round_(u)
            round_(2, last=True)
            normalize(6, 0, 1)

            dve.wait_ge(rows_got, 16 * 2 * SC)
            dve.tensor_copy(rows_f[:, 0, :, :], rows_i[:, 0, :, :])
            for c in range(SC):
                last = dve.tensor_scalar(rows_f[:, 1, c, :], rows_i[:, 1, c, :], b128[:, c:c + 1], None, ALU.subtract)
            last.then_inc(setup_dve, 1)
            for k, t in ((1, dl), (0, srci)):
                dve.wait_ge(rows_turned, 2 - k)
                dve.tensor_copy(t[:, 0:512], bank[2 * k][:])
                last = dve.tensor_copy(t[:, 512:SW], bank[2 * k + 1][:, 0:SW - 512])
            last.then_inc(srci_made, 1)

            then = linker(shift_dve)
            dve.wait_ge(aa_kept, NT + 16)
            by_head = aav[:, :, 0:HEADS].rearrange("p n k -> p k n")
            dve.tensor_reduce(ext[:, 0:8], by_head, AX_X, ALU.max)
            then(dve.tensor_reduce(ext[:, 8:16], by_head, AX_X, ALU.min))
            then(dve.tensor_scalar(ext[:, 8:16], ext[:, 8:16], -1.0, None, ALU.mult))
            dve.wait_ge(shift_pe, 1)
            then(dve.tensor_reduce(exr, bank[4][0:16, 0:P], AX_X, ALU.max))
            then(dve.tensor_scalar(exd, ident[0:16, 0:16], exr, None, ALU.mult))
            dve.wait_ge(shift_pe, 2)
            then(dve.tensor_copy(exb, bank[4][:, 128:144]))
            dve.tensor_copy(sm, exb[:, 0:8].unsqueeze(1).broadcast_to([P, NT, HEADS]))
            then(dve.tensor_add(exm, exb[:, 0:8], exb[:, 8:16]))
            then(dve.tensor_reduce(ext[:, 0:1], exm, AX_X, ALU.max))
            then(dve.tensor_scalar(flag[0:1, 0:1], ext[0:1, 0:1], spread, None, ALU.is_gt))
            dve.wait_ge(xn_stored, 16 * 7)
            general = dve.value_load(flag[0:1, 0:1], min_val=0, max_val=1)
            with dve.If(general):
                exact_maxima_dve(dve, linker)
            dve.wait_ge(sm_ready, 1)
            then(dve.tensor_add(sm, sm, aav[:, :, 8:16]))
            dve.scalar_tensor_tensor(out=aav[:, :, 16:24], in0=sm, scalar=SLOPE, in1=sm, op0=ALU.mult, op1=ALU.max).then_inc(shift_ready, 1)

            dve.memset(acc[:], 0.0).then_inc(acc_zero, 1)
            dve.memset(xg[:, :, D:XW], 1.0).then_inc(acc_zero, 1)
            dve.wait_ge(acc_zero, 2)
            dve.sem_inc(added, 4)
            for t in (phi_made, phiq_made, qn_made, xo_made, xo_free):
                dve.sem_inc(t, 1)

            def one_hot(q, j):
                dve.tensor_tensor(oh[j % 4], iota_f[:].unsqueeze(1).broadcast_to([P, QUAD, P]),
                                  dl[:, bass.ds(QUAD * q, QUAD)].unsqueeze(2).broadcast_to([P, QUAD, P]), ALU.is_equal).then_inc(oh_made, 1)

            def scores(q, j, i):
                for t in range(QUAD):
                    dve.wait_ge(got[4 * (j % 4) + t], 16 * i + 16)
                dve.wait_ge(ad_made, q + 1 + 1)
                ad = bank[2][:, 0:16 * QUAD].rearrange("p (t k) -> p t k", t=QUAD)
                then = linker(e_dve, 2 * q)
                then(dve.tensor_add(et, gath[:, 4 * (j % 4):4 * (j % 4) + 4, D:ROW], ad[:, :, 0:8]))
                then(dve.scalar_tensor_tensor(out=el, in0=et, scalar=SLOPE, in1=et, op0=ALU.mult, op1=ALU.max))
                dve.tensor_sub(eu[j % 2], ad[:, :, 8:16], el).then_inc(eu_made, 1)

            def weigh(q, j):
                dve.wait_ge(p_made, q + 1)
                g = gath[:, 4 * (j % 4):4 * (j % 4) + 4, :]
                h = g[:, :, 0:D].rearrange("p t (k f) -> p t k f", f=FH)
                dve.tensor_mul(h, h, g[:, :, D:ROW].unsqueeze(3).broadcast_to([P, QUAD, HEADS, FH])).then_inc(weighed, 1)

            def add(q, b):
                for t in range(QUAD):
                    k = QUAD * q + t
                    sums = acc[:, bass.ds(b[t], ROW)]
                    dve.wait_ge(summed, k + 1 + BODY)
                    dve.wait_ge(added, k + 4)
                    dve.tensor_add(sums, sums, bank[SUMS[t]][:, 0:ROW]).then_inc(added, 1)

            def halves(t, n):
                return t[:, 0:2 * D].rearrange("p (m n) -> p m n", m=2)[:, :, 0:n]

            def kv_h1(r, w=2):
                dve.wait_ge(k_out, r + 2)
                dve.wait_ge(g_made, r + 1)
                dve.scalar_tensor_tensor(out=ph[:, 0:w * D], in0=ea[:, 0:w * D], scalar=1.0, in1=eb[:, 0:w * D],
                                         op0=ALU.min, op1=ALU.add).then_inc(phi_made, 1)

            def m_stage():
                then = linker(m_dve)
                dve.wait_ge(g_made, PAIRS + 2)
                for m in range(C):
                    last = dve.tensor_copy(kvg[:, m, :], bank[6 + m][:, 0:XW])
                then(last)
                for m in range(C):
                    dve.tensor_scalar(kb[:, m, :], kbmask[:, m, :], kvg[:, m, D:XW], None, ALU.mult)
                dve.wait_ge(m_pe, 1)
                dve.tensor_copy(gT, bank[5][:])
                then(dve.tensor_copy(ksr, bank[6][0:1, 0:D]))
                dve.wait_ge(m_pe, 2)
                then(dve.tensor_mul(kvm, bank[7][:, 0:D].rearrange("p (m f) -> p m f", m=C), headmask[:].unsqueeze(1).broadcast_to([P, C, P])))
                dve.wait_ge(m_pe, 3)
                then(dve.tensor_copy(m_sb[:], bank[6][:].rearrange("p (m f) -> p m f", m=C)))

            def att_h1(r, w=2):
                n = w * P
                dve.wait_ge(q_out, r + 2)
                dve.scalar_tensor_tensor(out=halves(ph, n), in0=halves(ea, n), scalar=1.0, in1=halves(eb, n),
                                         op0=ALU.min, op1=ALU.add).then_inc(phiq_made, 1)
                dve.wait_ge(norm_made, r + 1)
                then = linker(norm_dve, r)
                then(dve.tensor_scalar(rq2[:, 0:8 * w], bank[5][:, 0:8 * w], NORM_EPS, None, ALU.add))
                dve.reciprocal(rq[:, 0:8 * w], rq2[:, 0:8 * w]).then_inc(rq_made, 1)

            def att_h2(r, w=2):
                n = w * P
                dve.wait_ge(rq_spread, r + 2)
                dve.wait_ge(att_made, r + 1)
                dve.tensor_mul(halves(qn, n), halves(ph, n), halves(bank[6], n)).then_inc(qn_made, 1)

            def att_h3(r, w=2):
                dve.wait_ge(att_made, r + 2)
                dve.wait_ge(xr_in, 16 * r + 16)
                dve.wait_ge(xo_free, r + 1)
                dve.tensor_add(xo[:, 0:w, :], bank[7][:, 0:w * D].rearrange("p (t f) -> p t f", f=D), xr[:, 0:w, :]).then_inc(xo_made, 1)

            def body(i, hooks, last=False):
                b = blocks_of(mybir.EngineType.DVE, brow_acc, ROW, BODY * i, BODY)
                for j in range(4):
                    q = 4 * i + j
                    if not (last and j == 3):
                        scores(q + 1, j + 1, i + (j + 1) // 4)
                    if not (last and j >= 2):
                        one_hot(q + 2, j + 2)
                    if not (last and j == 3):
                        weigh(q + 1, j + 1)
                    add(q, b[QUAD * j:QUAD * j + QUAD])
                    if j in hooks:
                        hooks[j]()

            one_hot(0, 0)
            scores(0, 0, 0)
            one_hot(1, 1)
            weigh(0, 0)
            with dve.Fori(0, PAIRS) as i:
                body(i, {1: lambda: kv_h1(i)})
            body(PAIRS, {1: lambda: kv_h1(PAIRS, 1)})
            body(PAIRS + 1, {0: m_stage})
            A = PAIRS + 2
            with dve.Fori(0, PAIRS) as r:
                body(A + r, {1: lambda: att_h1(r), 2: lambda: att_h2(r), 3: lambda: att_h3(r)})
            body(A + PAIRS, {1: lambda: att_h1(PAIRS, 1), 2: lambda: att_h2(PAIRS, 1), 3: lambda: att_h3(PAIRS, 1)})
            body(BODIES - 1, {}, last=True)

            dve.wait_ge(added, STEPS + 4)
            then = linker(den_done)
            den = accv[:, :, D:ROW]
            then(dve.tensor_scalar(den, den, 1e-30, None, ALU.max))
            then(dve.reciprocal(den, den))
            dve.sem_inc(x1_made, 2)

            def x1_of(r, q, u, w=2):
                then = linker(x1_dve, 4 * r)
                t1 = accv[:, bass.ds(2 * r, w), :]
                h = t1[:, :, 0:D].rearrange("p t (k f) -> p t k f", f=FH)
                then(dve.tensor_mul(h, h, t1[:, :, D:ROW].unsqueeze(3).broadcast_to([P, w, HEADS, FH])))
                dve.wait_ge(xa_in[q], 16 * u + 16)
                dve.tensor_add(t1[:, :, 0:D], t1[:, :, 0:D], xa[q][:, 0:w, :]).then_inc(x1_made, 1)
                dve.wait_ge(x1_made, r + 1 + 2)
                settle(dve)
                for t in range(w):
                    last = dve.bn_stats(st2[:, t, :], t1[:, t, 0:D])
                then(last)
                settle(dve)
                for t in range(w):
                    last = dve.bn_aggr(mv2[q][:, t, :], st2[:, t, :])
                then(last)
                dve.tensor_scalar(mv2[q][:, 0:w, 1], mv2[q][:, 0:w, 1], LN_EPS, None, ALU.add).then_inc(x1_dve, 1)

            def y_of(r, q, w=2):
                t1 = accv[:, bass.ds(2 * r, w), :]
                dve.wait_ge(rstd2_made, r + 1)
                dve.tensor_copy(mrv[:, bass.ds(2 * r, w), :], mv2[q][:, 0:w, :])
                dve.wait_ge(y_used, r + 1)
                for t in range(w):
                    last = dve.tensor_scalar(ys[q][:, t, :], t1[:, t, 0:D], mv2[q][:, t, 0:1], mv2[q][:, t, 1:2], ALU.subtract, ALU.mult)
                last.then_inc(y_made, 1)

            def round_(u, w=2):
                x1_of(2 * u + 1, 1, u)
                y_of(2 * u, 0)
                x1_of(2 * u + 2, 0, u + 1, w)
                y_of(2 * u + 1, 1)

            x1_of(0, 0, 0)
            with dve.Fori(0, PAIRS // 2 - 1) as u:
                round_(u)
            round_(PAIRS // 2 - 1, 1)
            y_of(PAIRS, 0, 1)

            def softmax(src_, ex, k, out_, a, then):
                then(dve.tensor_reduce(rt[:, a:a + 1], src_, AX_X, ALU.max))
                then(dve.tensor_scalar(ex, src_, rt[:, a:a + 1], None, ALU.subtract))
                dve.wait_ge(route_act, k)
                then(dve.tensor_reduce(rt[:, a:a + 1], ex, AX_X, ALU.add))
                then(dve.reciprocal(rt[:, a + 1:a + 2], rt[:, a:a + 1]))
                then(dve.tensor_scalar(out_, ex, rt[:, a + 1:a + 2], None, ALU.mult))

            def first_greatest(v, top, where, then):
                then(dve.tensor_reduce(top, v, AX_X, ALU.max))
                then(dve.tensor_scalar(rt[:, 72:80], v, top, 100.0, ALU.is_lt, ALU.mult))
                then(dve.tensor_add(rt[:, 80:88], rt[:, 72:80], iota_f[0:1, 0:8]))
                then(dve.tensor_reduce(where, rt[:, 80:88], AX_X, ALU.min))

            then = linker(route_dve)
            dve.wait_ge(y_used, PAIRS + 1 + 2)
            then(dve.tensor_scalar(mrow, bank[2][0:1, 0:D], 1.0 / N, None, ALU.mult))
            dve.wait_ge(route_pe, 1)
            then(dve.tensor_copy(mcol, bank[3][:, 0:C]))
            dve.wait_ge(route_pe, 2)
            then(dve.tensor_add(rt[:, 0:8], bank[3][0:1, 16:24], brs[:]))
            softmax(rt[:, 0:8], rt[:, 16:24], 1, rt[:, 26:34], 24, then)
            then(dve.tensor_scalar(rt[:, 64:72], rt[:, 26:34], float(N), 1e-30, ALU.mult, ALU.max))
            then(dve.reciprocal(rt[:, 72:80], rt[:, 64:72]))
            then(dve.tensor_scalar(rt[:, 80:88], rt[:, 72:80], CAPACITY, 1.0, ALU.mult, ALU.min))
            then(dve.tensor_mul(rt[:, 96:104], rt[:, 26:34], rt[:, 80:88]))
            softmax(rt[:, 96:104], rt[:, 40:48], 2, rt[:, 56:64], 48, then)
            first_greatest(rt[:, 56:64], rt[:, 88:89], sel[:, 2:3], then)
            then(dve.tensor_scalar(rt[:, 104:112], iota_f[0:1, 0:8], sel[:, 2:3], -4.0, ALU.is_equal, ALU.mult))
            then(dve.tensor_add(rt[:, 112:120], rt[:, 56:64], rt[:, 104:112]))
            first_greatest(rt[:, 112:120], rt[:, 89:90], sel[:, 3:4], then)
            then(dve.tensor_sub(rt[:, 90:91], rt[:, 89:90], rt[:, 88:89]))
            dve.wait_ge(route_act, 3)
            then(dve.tensor_scalar(rt[:, 91:92], rt[:, 90:91], 1.0, None, ALU.add))
            then(dve.reciprocal(sel[:, 0:1], rt[:, 91:92]))
            then(dve.tensor_mul(sel[:, 1:2], rt[:, 90:91], sel[:, 0:1]))
            dve.wait_ge(route_pe, 3)
            then(dve.tensor_copy(selb, bank[3][:, 32:36]))
            for e in range(TOPK):
                last = dve.scalar_tensor_tensor(out=eidx[:, e, :], in0=mult7[:], scalar=selb[:, 2 + e:3 + e], in1=pidx7[:], op0=ALU.mult, op1=ALU.add)
            then(last)
            dve.wait_ge(route_dve, ROUTE)
            dve.wait_ge(w_picked, 16 * TOPK * (C + 2 * FJ + 1))
            for e in range(TOPK):
                w2e = w2s[:, e * FJ:(e + 1) * FJ, :]
                dve.tensor_scalar(w2e, w2e, selb[:, e:e + 1], None, ALU.mult)
            then(dve.tensor_scalar(b2w, b2s[:, 0, :], selb[:, 0:1], None, ALU.mult))
            dve.scalar_tensor_tensor(out=b2w, in0=b2s[:, 1, :], scalar=selb[:, 1:2], in1=b2w, op0=ALU.mult, op1=ALU.add).then_inc(w2_scaled, 1)

            dve.sem_inc(z_made, 2)

            def finish(i, q):
                x1 = accv[:, bass.ds(i, 1), 0:D].rearrange("p a f -> p (a f)")
                dve.tensor_scalar(yb[q], x1, mr[:, bass.ds(2 * i, 1)], mr[:, bass.ds(2 * i + 1, 1)], ALU.subtract, ALU.mult).then_inc(yb_made, 1)
                dve.wait_ge(moe_made, i + 1)
                dve.wait_ge(yb_full, i + 1)
                dve.wait_ge(out_made, i + 1)
                dve.tensor_add(zt[q], bank[4 + q][:, 0:D], yb[q]).then_inc(z_made, 1)
                dve.wait_ge(z_made, i + 1 + 2)
                then = linker(z_dve, 3 * i)
                settle(dve)                           
                then(dve.bn_stats(st3, zt[q]))
                settle(dve)
                then(dve.bn_aggr(mv3, st3))
                dve.tensor_scalar(mv3[:, 1:2], mv3[:, 1:2], LN_EPS, None, ALU.add).then_inc(z_dve, 1)
                dve.wait_ge(rstd3_made, i + 1)
                dve.tensor_scalar(zt[q], zt[q], mv3[:, 0:1], mv3[:, 1:2], ALU.subtract, ALU.mult).then_inc(zn_made, 1)

            with dve.Fori(0, PAIRS) as u:
                for q in range(2):
                    finish(2 * u + q, q)
            finish(NT - 1, 0)


_INS = ["x", "src", "dst", "L0_gnn_W", "L0_gnn_att_src", "L0_gnn_att_dst", "L0_gnn_bias", "L0_mix_wq", "L0_mix_bq",
        "L0_mix_wk", "L0_mix_bk", "L0_mix_wv", "L0_mix_bv", "L0_mix_wo", "L0_mix_bo", "L0_ffn_Wr", "L0_ffn_br",
        "L0_ffn_W1", "L0_ffn_b1", "L0_ffn_W2", "L0_ffn_b2", "L0_ffn_gamma", "L0_ffn_beta"]
_SCRATCH = [("table", (NP, ROW), F32), ("src_pad", (ET, P), I32), ("dst_pad", (ET, P), I32), ("asrc_tab", (NP, HEADS), F32),
            ("smax_tab", (NP, HEADS), F32), ("xn_d", (NP, D), F32), ("xa_d", (NP, D), F32)]


def kernel(**inputs):
    import numpy as _np
    import concourse.bacc as _bacc
    from concourse import mybir as _mybir
    from concourse.bass_utils import run_bass_kernel_spmd as _run

    nc = _bacc.Bacc("TRN2", target_bir_lowering=False, num_devices=1)
    arrays, args = {}, []
    for name in _INS:
        a = _np.ascontiguousarray(inputs[name])
        arrays[f"in_{name}_dram"] = a
        args.append(nc.dram_tensor(f"in_{name}_dram", a.shape, _mybir.dt.from_np(a.dtype), kind="ExternalInput").ap())
    args.append(nc.dram_tensor("out_0_dram", (N, D), F32, kind="ExternalOutput").ap())
    for name, shape, dt in _SCRATCH:
        args.append(nc.dram_tensor(name, shape, dt, kind="Internal").ap())
    gps_layer(nc, *args, SPREAD)
    r = _run(nc, [arrays], core_ids=[0])
    return r.results[0]["out_0_dram"]
```

```python
from contextlib import ExitStack

import concourse.bass as bass
from concourse import mybir

F32 = mybir.dt.float32
I32 = mybir.dt.int32
BF16 = mybir.dt.bfloat16
ALU = mybir.AluOpType
ACT = mybir.ActivationFunctionType
AX_X = mybir.AxisListType.X

P = 128
N, D = 6250, 256
HEADS, FH = 8, 32
EDGES = 100000
EXPERTS, HIDDEN, TOPK = 8, 512, 2
LN_EPS = 1e-5
NORM_EPS = 1e-6
SLOPE = 0.2
CAPACITY = float(-(-N * 5 // (4 * EXPERTS)))
SPREAD = 60.0
LOW = -1.0e38
CONSTS, WEIGHTS, ROUTE = 16, 12, 33
EXPS = (5, 14, 28)

NT = -(-N // P)
NP = NT * P
LAST = N - (NT - 1) * P
ROW = D + HEADS
C = D // P
HW = D + 2 * HEADS
QUAD = 4
BODY = 4 * QUAD
ET = 784
EP = ET * P
STEPS = ET + NT - 1
BODIES = STEPS // BODY
SC = -(-STEPS // P)
SW = SC * P
WHOLE = EDGES // P
NB = NT - 1
CH = 112
CL = EP // CH
SUMS = (0, 1, 3, 4)
AD_AT = 448
PAIRS = NT // 2
FJ = HIDDEN // P
EJ = TOPK * FJ
PAD_DST = NP - 1
assert STEPS == BODIES * BODY and NT % 16 == 1 and BODIES >= 2 * PAIRS + 4 and CL % 16 == 0


def gps_layer(nc, x, src, dst, gW, g_as, g_ad, g_bias, wq, bq, wk, bk, wv, bv, wo, bo, Wr, br, W1, b1, W2, b2,
              gamma, beta, out, table, src_pad, dst_pad, asrc_tab, smax_tab, xn_d, xa_d, dst_rows, spread):
    with ExitStack() as ctx:
        def sb(name, shape, dt=F32):
            return ctx.enter_context(nc.sbuf_tensor(name, shape, dt))

        def sem(name):
            return ctx.enter_context(nc.semaphore(name))

        bank = [ctx.enter_context(nc.psum_tensor(f"bank{i}", [P, 512], F32)) for i in range(8)]

        xT = sb("xT", [P, C * NP])
        xTv = xT[:].rearrange("p (c n) -> p c n", c=C)
        acc = sb("acc", [P, NT * ROW])
        accx = acc[:, 0:NT * D].rearrange("p (n f) -> p n f", f=D)
        accv = acc[:].rearrange("p (n f) -> p n f", f=ROW)
        aa = sb("aa", [P, NT * 24])
        aav = aa[:].rearrange("p (n k) -> p n k", k=24)
        mr = sb("mr", [P, NT * 2])
        mrv = mr[:].rearrange("p (n k) -> p n k", k=2)
        ident = sb("ident", [P, P])
        iota_f = sb("iota_f", [P, P])
        ones = sb("ones", [P, P])
        zeros = sb("zeros", [P, D])
        headmask = sb("headmask", [P, P])
        kbmask = sb("kbmask", [P, C, HEADS])
        wg = sb("wg", [P, C, HW])
        wqs, wks, wvs, wos = (sb(n, [P, C, D]) for n in ("wqs", "wks", "wvs", "wos"))
        bks, bvs, bos, gbs, bsum = (sb(n, [1, D]) for n in ("bks", "bvs", "bos", "gbs", "bsum"))
        brs = sb("brs", [1, EXPERTS])
        bqs = sb("bqs", [P, C])
        gam = sb("gam", [P, D])
        bet = sb("bet", [P, D])
        wrs = sb("wrs", [P, C, EXPERTS])
        brow_aa = sb("brow_aa", [1, SW], I32)
        brow_acc = sb("brow_acc", [1, SW], I32)
        dl = sb("dl", [P, SW])
        srci = sb("srci", [P, SW], I32)
        idx = sb("idx", [P, BODY], I32)
        kb = sb("kb", [P, C, HEADS])
        m_sb = sb("m_sb", [P, C, D])
        half = sb("half", [P, 8])
        place = sb("place", [P, 1])
        flag = sb("flag", [1, 1], I32)
        mult7 = sb("mult7", [P, 7])
        pidx7 = sb("pidx7", [P, 7])

        WORK = 17072
        work = sb("work", [P, WORK])
        worki = work[:].bitcast(I32)
        at = [0]

        def area(size, parts=P, ints=False):
            a = at[0]
            at[0] += size
            assert at[0] <= WORK, at[0]
            return (worki if ints else work)[0:parts, a:a + size]

        ld_i, ld_f = area(WHOLE, 1, True), area(WHOLE, 1)
        before, stepk, moved = area(WHOLE, NB), area(SW, NB), area(SW, NB)
        kcol, bcol, tcol, tcol_i = area(SC), area(SC), area(SC), area(SC, ints=True)
        b128 = area(SC)
        bthr, bnum, cnt, key = area(1, NB), area(1, NB), area(1, NB), area(1, NB)
        pad_i = area(2 * (EP - EDGES), 1, True).rearrange("p (k e) -> p k e", k=2)
        rows_i = area(2 * SW, ints=True).rearrange("p (k c e) -> p k c e", k=2, c=SC)
        rows_f = area(2 * SW).rearrange("p (k c e) -> p k c e", k=2, c=SC)
        dlb = area(SW // 2).bitcast(BF16).rearrange("p (c e) -> p c e", c=SC)
        stats = area(48).rearrange("p (t k) -> p t k", k=6)
        mv = [area(16).rearrange("p (t k) -> p t k", k=2) for _ in range(2)]
        rstd = [area(8) for _ in range(2)]
        attb = area(2 * D).rearrange("p (k f) -> p k f", k=2)
        xs = [area(D) for _ in range(2)]
        xts = [area(D).rearrange("p (c n) -> p c n", c=C) for _ in range(2)]
        prod = area(2 * C * D).rearrange("p (k c f) -> p k c f", k=2, c=C)
        ext, exb, exm, exr, exd = area(16), area(16), area(8), area(1, 16), area(16, 16)
        ht = area(16 * HW).rearrange("p (t f) -> p t f", f=HW)
        sm = area(NT * HEADS).rearrange("p (n k) -> p n k", k=HEADS)

        at[0] = 0
        gath = area(BODY * ROW).rearrange("p (t f) -> p t f", f=ROW)
        oh = [area(QUAD * P).rearrange("p (t d) -> p t d", t=QUAD) for _ in range(4)]
        oht = [area(QUAD * P).rearrange("p (t e) -> p t e", t=QUAD) for _ in range(2)]
        away = [area(QUAD * P).rearrange("p (t d) -> p t d", t=QUAD) for _ in range(2)]
        dlr = area(BODY * P // 2).bitcast(BF16).rearrange("p (t e) -> p t e", t=BODY)
        et, el = area(QUAD * HEADS).rearrange("p (t k) -> p t k", t=QUAD), area(QUAD * HEADS).rearrange("p (t k) -> p t k", t=QUAD)
        eu = [area(QUAD * HEADS).rearrange("p (t k) -> p t k", t=QUAD) for _ in range(2)]
        ev = area(QUAD * HEADS).rearrange("p (t k) -> p t k", t=QUAD)
        kxs = area(2 * D).rearrange("p (c n) -> p c n", c=C)
        ea, eb, ph, qn = area(2 * D), area(2 * D), area(2 * D), area(2 * D)
        xg = area(2 * D).rearrange("p (t f) -> p t f", f=D)
        xr, xo = area(2 * D).rearrange("p (t f) -> p t f", f=D), area(2 * D).rearrange("p (t f) -> p t f", f=D)
        rq, rq2, rqx = area(16), area(16), area(2 * D)
        kvg, ksum = area(C * D).rearrange("p (m f) -> p m f", m=C), area(C)
        gT, kvm, ksr = area(C * D), area(C * P).rearrange("p (m f) -> p m f", m=C), area(D, 1)

        at[0] = 0
        ys = [area(2 * D).rearrange("p (t f) -> p t f", f=D) for _ in range(2)]
        xa = [area(2 * D).rearrange("p (t f) -> p t f", f=D) for _ in range(2)]
        st2 = area(12).rearrange("p (t k) -> p t k", k=6)
        mv2 = [area(4).rearrange("p (t k) -> p t k", k=2) for _ in range(2)]
        mrow, mcol, rt, sel, selb = area(D, 1), area(C), area(128, 1), area(4, 1), area(4)
        eidx = area(7 * TOPK, ints=True).rearrange("p (e k) -> p e k", k=7)
        w1s = area(TOPK * C * HIDDEN).rearrange("p (e c f) -> p e c f", e=TOPK, c=C)
        w2s = area(EJ * D).rearrange("p (k f) -> p k f", f=D)
        b1s = area(EJ)
        b2s = area(TOPK * D).rearrange("p (e f) -> p e f", e=TOPK)
        b2w = dl[:, 2 * D:3 * D]
        hT = area(EJ * 4 * P).rearrange("p (k n) -> p k n", k=EJ)
        zt, ot = ([area(D) for _ in range(2)] for _ in range(2))
        yb = [dl[:, D * k:D * k + D] for k in range(2)]
        st3, mv3 = area(6), area(2)

        const, ld, pads, padded, wts, w_att = (sem(n) for n in ("const", "ld", "pads", "padded", "weights", "w_att"))
        setup_dve, setup_pe, rows_got, watt = (sem(n) for n in ("setup_dve", "setup_pe", "rows_got", "watt"))
        x_in, x_rest = [sem(f"x_in{i}") for i in range(2)], sem("x_rest")
        rstd_made, rstd2_made, rstd3_made = (sem(n) for n in ("rstd_made", "rstd2_made", "rstd3_made"))
        stat, xs_made, xn_made, xs_turned, xts_out, xts_kept = (sem(n) for n in ("stat", "xs_made", "xn_made", "xs_turned", "xts_out", "xts_kept"))
        h_made, ht_out, aa_kept, xn_stored = (sem(n) for n in ("h_made", "ht_out", "aa_kept", "xn_stored"))
        stored = [sem(f"table_stored{i}") for i in range(2)]
        rows_turned, srci_made, shift_dve, shift_pe, sm_ready, shift_ready = (sem(n) for n in ("rows_turned", "srci_made", "shift_dve", "shift_pe", "sm_ready", "shift_ready"))
        gen_dve, gen_pe, gen_pool, gen_dma, gen_copy, gen_copy2, gen_got, gen_put, gen_scan, gen_done = (
            sem(n) for n in ("gen_dve", "gen_pe", "gen_pool", "gen_dma", "gen_copy", "gen_copy2", "gen_got", "gen_put",
                             "gen_scan", "gen_done"))
        acc_zero, seeded = sem("acc_zero"), sem("seeded")
        idx_staged, oh_made, oht_made, ad_made, eu_made, eu_pos, p_made, weighed, summed, added = (
            sem(n) for n in ("idx_staged", "oh_made", "oht_made", "ad_made", "eu_made", "eu_pos", "p_made",
                             "weighed", "summed", "added"))
        e_dve, away_made, dlr_used, ksum_added, dlb_made, dst_rows_out = (sem(n) for n in ("e_dve", "away_made", "dlr_used", "ksum_added", "dlb_made", "dst_rows_out"))
        dlr_in = [sem(f"dlr_in{j}") for j in range(4)]
        got = [sem(f"gathered{i}") for i in range(BODY)]
        xg_in, kx_out, k_made, k_out, phi_made, g_made = (sem(n) for n in ("xg_in", "kx_out", "k_made", "k_out", "phi_made", "g_made"))
        m_dve, m_pe = sem("m_dve"), sem("m_pe")
        xr_in, q_made, q_out, phiq_made, norm_made, norm_dve, rq_made, rqx_made, rq_spread, qn_made, att_made, xo_made, xo_stored, xo_free = (
            sem(n) for n in ("xr_in", "q_made", "q_out", "phiq_made", "norm_made", "norm_dve", "rq_made", "rqx_made",
                             "rq_spread", "qn_made", "att_made", "xo_made", "xo_stored", "xo_free"))
        den_done, x1_dve, x1_made, y_made, y_turned, y_out, y_used = (sem(n) for n in ("den_done", "x1_dve", "x1_made", "y_made", "y_turned", "y_out", "y_used"))
        xa_in = [sem(f"xa_in{i}") for i in range(2)]
        route_dve, route_pe, route_act, w_picked, w2_scaled = (sem(n) for n in ("route_dve", "route_pe", "route_act", "w_picked", "w2_scaled"))
        hid_made, hid_out, moe_made, yb_made, yb_full, z_made, z_dve, zn_made, zg_made, out_made = (
            sem(n) for n in ("hid_made", "hid_out", "moe_made", "yb_made", "yb_full", "z_made", "z_dve", "zn_made", "zg_made", "out_made"))
        out_stored = [sem(f"out_stored{i}") for i in range(2)]

        def field(a, ints=False):
            return (acc[:].bitcast(I32) if ints else acc[:])[0:CH, CL * a:CL * a + CL]

        score = acc[0:CH, 0:CL * HEADS].rearrange("p (j k) -> p j k", k=HEADS)
        f_step, f_dst, i_src, i_dst, i_to = field(8), field(9), field(10, True), field(11, True), field(12, True)
        gx = acc[0:CH, CL * 13:CL * 13 + 16 * HEADS].rearrange("p (j k) -> p j k", k=HEADS)
        gi = acc[:].bitcast(I32)[0:CH, CL * 13 + 128:CL * 13 + 144]
        ends = acc[0:CH, CL * 13 + 144:CL * 13 + 168].rearrange("p (a k) -> p a k", k=HEADS)
        f_next = acc[0:CH, CL * 13 + 168:CL * 13 + 169]
        i_next = acc[:].bitcast(I32)[0:CH, CL * 13 + 169:CL * 13 + 170]
        carry = acc[0:CH, CL * 13 + 176:CL * 13 + 184]
        erow = acc[0:HEADS, CL * 13 + 184:CL * 13 + 184 + 3 * CH].rearrange("p (a c) -> p a c", a=3)
        crow = acc[0:HEADS, CL * 13 + 520:CL * 13 + 520 + 3 * CH].rearrange("p (a c) -> p a c", a=3)
        FAR = 65536.0

        def exact_maxima_pool(pool):
            dst_flat, src_flat = dst_pad.rearrange("t e -> (t e)"), src_pad.rearrange("t e -> (t e)")
            pool.wait_ge(xn_stored, 16 * 7)
            pool.memset(i_next, PAD_DST + 1).then_inc(gen_pool, 1)
            pool.wait_ge(gen_pool, 1)
            pool.dma_start(i_src, src_flat.rearrange("(p j) -> p j", j=CL)).then_inc(gen_dma, 16)
            pool.dma_start(i_dst, dst_flat.rearrange("(p j) -> p j", j=CL)).then_inc(gen_dma, 16)
            with nc.allow_non_contiguous_dma(reason="one number for each chunk"):
                pool.dma_start(i_next[0:CH - 1, :], dst_flat.rearrange("(p j) -> p j", j=CL)[1:CH, 0:1]).then_inc(gen_dma, 16)
            for t in (asrc_tab, smax_tab):
                pool.dma_start(t.rearrange("(n p) f -> p n f", p=P), aav[:, :, 0:HEADS]).then_inc(gen_dma, 16)
            pool.wait_ge(gen_dma, 80)
            pool.sem_inc(gen_pool, 1)
            with pool.Fori(0, CL // 16) as i:
                pool.tensor_copy(gi, i_src[:, bass.ds(16 * i, 16)]).then_inc(gen_copy, 1)
                pool.wait_ge(gen_copy, 2 * i + 1)
                settle(pool)                   
                for j in range(16):
                    pool.indirect_dma_start(out=gx[:, j, :], out_offset=None, in_=asrc_tab[:, :],
                                            in_offset=bass.IndirectOffsetOnAxis(ap=gi[:, j:j + 1], axis=0)).then_inc(gen_got, 16)
                pool.wait_ge(gen_got, 256 * i + 256)
                pool.tensor_copy(score[:, bass.ds(16 * i, 16), :], gx).then_inc(gen_copy, 1)
                pool.wait_ge(gen_copy, 2 * i + 2)
                settle(pool)
            pool.sem_inc(gen_pool, 1)
            pool.wait_ge(gen_done, 1)
            with pool.Fori(0, CL // 16) as i:
                pool.tensor_copy(gi, i_to[:, bass.ds(16 * i, 16)]).then_inc(gen_copy2, 1)
                pool.tensor_copy(gx, score[:, bass.ds(16 * i, 16), :]).then_inc(gen_copy2, 1)
                pool.wait_ge(gen_copy2, 2 * i + 2)
                settle(pool)
                for j in range(16):
                    pool.indirect_dma_start(out=smax_tab[:, :], out_offset=bass.IndirectOffsetOnAxis(ap=gi[:, j:j + 1], axis=0),
                                            in_=gx[:, j, :], in_offset=None, bounds_check=NP - 1, oob_is_err=False).then_inc(gen_put, 16)
                pool.wait_ge(gen_put, 256 * i + 256)
                settle(pool)
            pool.dma_start(sm, smax_tab.rearrange("(n p) f -> p n f", p=P)).then_inc(gen_dma, 16)
            pool.wait_ge(gen_dma, 96)

        def exact_maxima_pe(pe):
            pe.wait_ge(gen_dve, 6)
            for a in range(3):
                last = pe.matmul(bank[0][0:HEADS, a * CH:a * CH + CH], ends[:, a, :], ident[0:CH, 0:CH], start=True, stop=True)
            last.then_inc(gen_pe, 1)
            pe.wait_ge(gen_dve, 12)
            pe.matmul(bank[1][0:CH, 0:HEADS], crow[:, 2, :], ident[0:HEADS, 0:HEADS], start=True, stop=True).then_inc(gen_pe, 1)

        def exact_maxima_dve(dve, linker):
            then = linker(gen_dve)
            dve.wait_ge(gen_pool, 2)
            dve.tensor_copy(f_next, i_next)
            then(dve.tensor_copy(f_dst, i_dst))
            dve.tensor_tensor(f_step[:, 0:CL - 1], f_dst[:, 0:CL - 1], f_dst[:, 1:CL], ALU.is_equal)
            then(dve.tensor_tensor(f_step[:, CL - 1:CL], f_dst[:, CL - 1:CL], f_next, ALU.is_equal))
            then(dve.scalar_tensor_tensor(out=i_to, in0=f_step, scalar=FAR, in1=f_dst, op0=ALU.mult, op1=ALU.add))
            dve.tensor_tensor(f_step[:, 1:CL], f_dst[:, 1:CL], f_dst[:, 0:CL - 1], ALU.not_equal)
            dve.memset(f_step[:, 0:1], 1.0)
            dve.wait_ge(gen_pool, 3)
            then(dve.tensor_copy(ends[:, 1, :], f_dst[:, CL - 1:CL].broadcast_to([CH, HEADS])))
            dve.tensor_copy(ends[:, 2, :], f_dst[:, 0:1].broadcast_to([CH, HEADS]))
            then(dve.tensor_scalar(f_step, f_step, LOW, None, ALU.mult))
            for k in range(HEADS):
                last = dve.tensor_tensor_scan(score[:, :, k], f_step, score[:, :, k], LOW, ALU.add, ALU.max)
            last.then_inc(gen_scan, 1)
            dve.wait_ge(gen_scan, 1)
            then(dve.tensor_copy(ends[:, 0, :], score[:, CL - 1, :]))
            dve.wait_ge(gen_pe, 1)
            then(dve.tensor_copy(erow, bank[0][0:HEADS, 0:3 * CH].rearrange("p (a c) -> p a c", a=3)))
            dve.memset(crow[:, 0, 0:1], LOW)
            dve.memset(crow[:, 2, 0:1], LOW)
            then(dve.tensor_tensor(crow[:, 0, 1:CH], erow[:, 1, 1:CH], erow[:, 1, 0:CH - 1], ALU.not_equal))
            then(dve.tensor_scalar(crow[:, 0, 1:CH], crow[:, 0, 1:CH], LOW, None, ALU.mult))
            dve.tensor_tensor(crow[:, 2, 1:CH], erow[:, 2, 1:CH], erow[:, 1, 0:CH - 1], ALU.not_equal)
            then(dve.tensor_tensor_scan(crow[:, 1, :], crow[:, 0, :], erow[:, 0, :], LOW, ALU.add, ALU.max))
            then(dve.tensor_scalar(crow[:, 2, 1:CH], crow[:, 2, 1:CH], LOW, None, ALU.mult))
            then(dve.tensor_add(crow[:, 2, 1:CH], crow[:, 2, 1:CH], crow[:, 1, 0:CH - 1]))
            dve.wait_ge(gen_pe, 2)
            dve.tensor_copy(carry, bank[1][0:CH, 0:HEADS])
            then(dve.tensor_scalar(f_step, f_dst, f_dst[:, 0:1], None, ALU.not_equal))
            then(dve.tensor_scalar(f_step, f_step, LOW, None, ALU.mult))
            for k in range(HEADS):
                last = dve.scalar_tensor_tensor(out=score[:, :, k], in0=f_step, scalar=carry[:, k:k + 1], in1=score[:, :, k], op0=ALU.add, op1=ALU.max)
            last.then_inc(gen_done, 1)

        block = ctx.enter_context(nc.Block())
        settled = sem("settled")

        def settle(eng):
            eng.sem_inc(settled, 1)

        def blocks_of(engine, starts, width, k, n):
            return nc.values_load_multi_w_load_instructions(
                starts[0:1, bass.ds(k, n)], engines=[engine], min_val=0, max_val=NB * width,
                skip_runtime_bounds_check_because="a block is the sum of NB comparisons, times width")[1]

        def rows_of(t, i, n=1):
            return t[bass.ds(i * P, n * P), :].rearrange("(n p) f -> p n f", p=P)

        @block.sync
        def _(sp):
            with nc.allow_non_contiguous_dma(reason="the last destination of each edge tile"):
                sp.dma_start(ld_i, dst[0:WHOLE * P].rearrange("(t e) -> e t", e=P)[P - 1:P, :]).then_inc(ld, 16)
            for k in range(2):
                sp.dma_start(accx[:, 8 * k:8 * k + 8, :], rows_of(x, 8 * k, 8)).then_inc(x_in[k], 16)
            for k, (a, b) in enumerate(((src, src_pad), (dst, dst_pad))):
                flat = b.rearrange("t e -> (t e)")
                sp.dma_start(flat[0:EDGES].rearrange("(a b) -> a b", a=32), a.rearrange("(a b) -> a b", a=32)).then_inc(padded, 16)
                if k == 0:
                    sp.wait_ge(pads, 2)
                sp.dma_start(flat[EDGES:EP].rearrange("(a b) -> a b", a=1), pad_i[:, k, :]).then_inc(padded, 16)
            for t, w in ((wg[:, :, 0:D], gW), (wks[:], wk), (wqs[:], wq), (wvs[:], wv), (wos[:], wo), (wrs[:], Wr)):
                sp.dma_start(t, w.rearrange("(c p) f -> p c f", p=P)).then_inc(wts, 16)
            for t, w in ((bks, bk), (bvs, bv), (bos, bo), (gbs, g_bias), (brs, br)):
                sp.dma_start(t[:], w.rearrange("(a f) -> a f", a=1)).then_inc(wts, 16)
            with nc.allow_non_contiguous_dma(reason="256 numbers"):
                sp.dma_start(bqs[:], bq.rearrange("(c p) -> p c", p=P)).then_inc(wts, 16)
            for k, (t, w) in enumerate(((gam, gamma), (bet, beta))):
                sp.dma_start(t[:], w.rearrange("(a f) -> a f", a=1).broadcast_to([P, D])).then_inc(out_stored[k], 16)
            for k, w in enumerate((g_as, g_ad)):
                sp.dma_start(attb[:, k, :], w.rearrange("(a h) f -> a (h f)", a=1).broadcast_to([P, D])).then_inc(stored[k], 16)

            sp.dma_start(accx[:, 16:NT - 1, :], rows_of(x, 16, NT - 17)).then_inc(x_rest, 16)
            sp.wait_ge(const, CONSTS)
            sp.dma_start(accx[0:LAST, NT - 1, :], x[(NT - 1) * P:N, :]).then_inc(x_rest, 16)

            def store(u, h):
                g = 2 * u + h
                sp.wait_ge(ht_out, 8 * (g + 1) + 2)
                sp.dma_start(rows_of(table, 8 * g, 8), ht[:, 8 * h:8 * h + 8, 0:ROW]).then_inc(stored[h], 16)
                sp.wait_ge(xn_made, 8 * (g + 1))
                sp.dma_start(rows_of(xn_d, 8 * g, 8), accx[:, bass.ds(8 * g, 8), :]).then_inc(xn_stored, 16)

            with sp.Fori(0, 3) as u:
                for h in range(2):
                    store(u, h)
            sp.wait_ge(ht_out, NT + 2)
            sp.dma_start(table[(NT - 1) * P:NP, :], ht[:, 0, 0:ROW]).then_inc(stored[0], 16)
            sp.wait_ge(xn_made, NT)
            sp.dma_start(xn_d[(NT - 1) * P:NP, :], accx[:, NT - 1, :]).then_inc(xn_stored, 16)
            sp.wait_ge(xn_stored, 16 * 7)

            sp.wait_ge(dlb_made, 1)
            sp.dma_start(dst_rows.rearrange("(c p) e -> p c e", p=P), dlb).then_inc(dst_rows_out, 16)

            def kv(r, w=2):
                sp.wait_ge(g_made, r + 1)
                if w == 2:
                    sp.dma_start(xg[:, :, 0:D], rows_of(xn_d, 2 * r, 2)).then_inc(xg_in, 16)
                else:
                    sp.dma_start(xg[:, 0, 0:D], xn_d[(NT - 1) * P:NP, :]).then_inc(xg_in, 16)

            def att(r, w=2):
                sp.wait_ge(xo_made, r + 1)
                if w == 2:
                    sp.dma_start(xr, rows_of(x, 2 * r, 2)).then_inc(xr_in, 16)
                else:
                    sp.dma_start(xr[0:LAST, 0, :], x[(NT - 1) * P:N, :]).then_inc(xr_in, 16)
                sp.wait_ge(xo_made, r + 2)
                if w == 2:
                    sp.dma_start(rows_of(xa_d, 2 * r, 2), xo).then_inc(xo_stored, 16)
                else:
                    sp.dma_start(xa_d[(NT - 1) * P:NP, :], xo[:, 0, :]).then_inc(xo_stored, 16)
                sp.wait_ge(xo_stored, 16 * (r + 1))
                sp.sem_inc(xo_free, 1)

            with sp.Fori(0, PAIRS) as r:
                kv(r)
            kv(PAIRS, 1)
            with sp.Fori(0, PAIRS) as r:
                att(r)
            att(PAIRS, 1)

            def p2(r, q, w=2):
                sp.wait_ge(x1_made, r + 1)
                if w == 2:
                    sp.dma_start(xa[q], rows_of(xa_d, 2 * r, 2)).then_inc(xa_in[q], 16)
                else:
                    sp.dma_start(xa[q][:, 0, :], xa_d[(NT - 1) * P:NP, :]).then_inc(xa_in[q], 16)

            with sp.Fori(0, PAIRS // 2) as u:
                for q in range(2):
                    p2(2 * u + q, q)
            p2(PAIRS, 0, 1)

            with sp.Fori(0, PAIRS) as u:
                for q in range(2):
                    sp.wait_ge(out_made, 2 * u + q + 1 + 2)
                    sp.dma_start(out[bass.ds((2 * u + q) * P, P), :], ot[q]).then_inc(out_stored[q], 16)
            sp.wait_ge(out_made, NT + 2)
            sp.dma_start(out[(NT - 1) * P:N, :], ot[0][0:LAST, :]).then_inc(out_stored[0], 16)
            sp.wait_ge(out_stored[0], 16 * (PAIRS + 2))
            sp.wait_ge(out_stored[1], 16 * (PAIRS + 1))

        @block.gpsimd
        def _(pool):
            n = [0]

            def link(ins):
                n[0] += 1
                ins.then_inc(const, 1)
                pool.wait_ge(const, n[0])

            pool.memset(pad_i[:, 0, :], 0).then_inc(pads, 1)
            pool.memset(pad_i[:, 1, :], PAD_DST).then_inc(pads, 1)
            link(pool.memset(ones[:], 1.0))
            pool.memset(half[:], -0.5)
            link(pool.memset(zeros[:], 0.0))
            link(pool.memset(ident[:], 0.0))
            link(pool.affine_select(out=ident[:], in_=ident[:], compare_op=ALU.not_equal, fill=1.0, base=0,
                                    pattern=[[-1, P]], channel_multiplier=1))
            link(pool.iota(place[:], [[0, 1]], base=0, channel_multiplier=1, allow_small_or_imprecise_dtypes=True))
            link(pool.iota(bnum, [[0, 1]], base=1, channel_multiplier=1, allow_small_or_imprecise_dtypes=True))
            link(pool.iota(bthr, [[0, 1]], base=P, channel_multiplier=P, allow_small_or_imprecise_dtypes=True))
            link(pool.iota(stepk, [[1, SW]], base=0, channel_multiplier=0, allow_small_or_imprecise_dtypes=True))
            link(pool.iota(kcol, [[P, SC]], base=0, channel_multiplier=1, allow_small_or_imprecise_dtypes=True))
            link(pool.iota(iota_f[:], [[1, P]], base=0, channel_multiplier=0, allow_small_or_imprecise_dtypes=True))
            link(pool.memset(headmask[:], 0.0))
            for k in range(P // FH):
                last = pool.memset(headmask[FH * k:FH * k + FH, FH * k:FH * k + FH], 1.0)
            link(last)
            link(pool.memset(kbmask[:], 0.0))
            for c in range(C):
                for k in range(P // FH):
                    last = pool.memset(kbmask[FH * k:FH * k + FH, c, 4 * c + k:4 * c + k + 1], 1.0)
            link(last)
            for k, rows in enumerate((D, D, HIDDEN, HIDDEN, HIDDEN, HIDDEN, 1)):
                off = (0, P, 0, P, 2 * P, 3 * P, 0)[k]
                last = pool.memset(mult7[:, k:k + 1], float(rows))
                pool.iota(pidx7[:, k:k + 1], [[0, 1]], base=off, channel_multiplier=1 if k < 6 else 0, allow_small_or_imprecise_dtypes=True)
            link(last)
            link(pool.memset(accx[:, NT - 1, :], 0.0))
            assert n[0] == CONSTS, n[0]
            def deviation(g, h, width=8):
                pool.wait_ge(stat, 3 * g + 3)
                pool.tensor_tensor(rstd[h][:, 0:width], mv[h][:, 0:width, 1], half[:, 0:width], ALU.pow).then_inc(rstd_made, 1)

            for k, t in enumerate((dst_pad, src_pad)):
                deviation(k, k)
                if k == 0:
                    pool.wait_ge(setup_dve, 8)
                    pool.wait_ge(padded, 64)
                for c in range(SC):
                    pool.indirect_dma_start(out=rows_i[:, 1 - k, c, :], out_offset=None, in_=t[:, :],
                                            in_offset=bass.IndirectOffsetOnAxis(ap=tcol_i[:, c:c + 1], axis=0)).then_inc(rows_got, 16)
            pool.wait_ge(wts, 16 * WEIGHTS)
            pool.tensor_add(bsum[:], bos[:], gbs[:]).then_inc(const, 1)

            def keep(i, j):
                pool.wait_ge(ht_out, i + 1 + 2)
                pool.tensor_copy(aav[:, bass.ds(i, 1), 0:16], ht[:, j:j + 1, D:HW]).then_inc(aa_kept, 1)

            pool.sem_inc(aa_kept, 16)
            with pool.Fori(0, 2) as u:
                for h in range(2):
                    for j in range(8):
                        keep(16 * u + 8 * h + j, 8 * h + j)
                    deviation(2 * u + 2 + h, h)
            for j in range(8):
                keep(32 + j, j)
            deviation(6, 0, 1)
            for j in range(8):
                keep(40 + j, 8 + j)
            keep(NT - 1, 0)

            pool.wait_ge(shift_dve, 8)
            general = pool.value_load(flag[0:1, 0:1], min_val=0, max_val=1)
            with pool.If(general):
                exact_maxima_pool(pool)
            pool.sem_inc(sm_ready, 1)

            pool.wait_ge(stored[0], 16 * 5)
            pool.wait_ge(stored[1], 16 * 4)

            def gathers(i):
                for j in range(BODY):
                    if j % QUAD == 0:
                        pool.wait_ge(idx_staged, 4 * i + j // QUAD + 1)
                        pool.wait_ge(summed, BODY * i + j + QUAD)
                        settle(pool)                  
                    pool.indirect_dma_start(out=gath[:, j, :], out_offset=None, in_=table[:, :],
                                            in_offset=bass.IndirectOffsetOnAxis(ap=idx[:, j:j + 1], axis=0)).then_inc(got[j], 16)

            with pool.Fori(0, BODIES) as i:
                gathers(i)

            def deviation2(r, q, w=2):
                pool.wait_ge(x1_dve, 4 * r + 4)
                pool.tensor_tensor(mv2[q][:, 0:w, 1], mv2[q][:, 0:w, 1], half[:, 0:w], ALU.pow).then_inc(rstd2_made, 1)

            with pool.Fori(0, PAIRS // 2) as u:
                for q in range(2):
                    deviation2(2 * u + q, q)
            deviation2(PAIRS, 0, 1)

            pool.wait_ge(route_dve, ROUTE)
            for e in range(TOPK):
                def pick(out_, tab, k):
                    pool.indirect_dma_start(out=out_, out_offset=None, in_=tab,
                                            in_offset=bass.IndirectOffsetOnAxis(ap=eidx[:, e, k:k + 1], axis=0)).then_inc(w_picked, 16)
                for c in range(C):
                    pick(w1s[:, e, c, :], W1.rearrange("e d f -> (e d) f"), c)
                for j in range(FJ):
                    pick(w2s[:, e * FJ + j, :], W2.rearrange("e f d -> (e f) d"), 2 + j)
                    pick(b1s[:, e * FJ + j:e * FJ + j + 1], b1.rearrange("e (f a) -> (e f) a", a=1), 2 + j)
                pick(b2s[:, e, :], b2[:, :], 6)

            pool.wait_ge(out_stored[0], 16)
            pool.wait_ge(out_stored[1], 16)

            def tail(i, q, u):
                pool.wait_ge(yb_made, i + 1)
                pool.tensor_add(yb[q], yb[q], b2w).then_inc(yb_full, 1)
                pool.wait_ge(z_dve, 3 * i + 3)
                pool.tensor_tensor(mv3[:, 1:2], mv3[:, 1:2], half[:, 0:1], ALU.pow).then_inc(rstd3_made, 1)
                pool.wait_ge(zn_made, i + 1)
                pool.tensor_mul(zt[q], zt[q], gam[:]).then_inc(zg_made, 1)
                pool.wait_ge(zg_made, 2 * i + 1)
                pool.tensor_add(zt[q], zt[q], bet[:]).then_inc(zg_made, 1)
                pool.wait_ge(zg_made, 2 * i + 2)
                pool.wait_ge(out_stored[q], 16 * u + 16)
                pool.tensor_add(ot[q], zt[q], accv[:, bass.ds(i, 1), 0:D].rearrange("p a f -> p (a f)")).then_inc(out_made, 1)

            pool.wait_ge(w2_scaled, 1)
            pool.sem_inc(out_made, 2)
            with pool.Fori(0, PAIRS) as u:
                for q in range(2):
                    tail(2 * u + q, q, u)
            tail(NT - 1, 0, PAIRS)

        @block.scalar
        def _(act):
            act.sem_inc(xts_out, 2)
            act.sem_inc(xts_kept, 2)
            act.sem_inc(ht_out, 2)

            def turn_out(i, q):
                act.wait_ge(xs_turned, i + 1 + 2)
                act.wait_ge(h_made, i + 1)
                act.copy(xts[q], bank[q][:, 0:D].rearrange("p (c n) -> p c n", c=C)).then_inc(xts_out, 1)

            def keep_turned(i, q):
                act.copy(xTv[:, :, bass.ds(i * P, P)], bank[q][:, 0:D].rearrange("p (c n) -> p c n", c=C)).then_inc(xts_kept, 1)

            def h_out(i, j, q, u, first):
                act.wait_ge(h_made, i + 1 + 2)
                if first:
                    act.wait_ge(stored[j // 8], 16 * u + 16)
                act.wait_ge(aa_kept, i + 1)
                act.copy(ht[:, j, :], bank[2 + q][:, 0:HW]).then_inc(ht_out, 1)

            with act.Fori(0, 3) as u:
                for j in range(0, 16, 2):
                    for q in range(2):
                        turn_out(16 * u + j + q, q)
                    for q in range(2):
                        keep_turned(16 * u + j + q, q)
                    for q in range(2):
                        h_out(16 * u + j + q, j + q, q, u, (j + q) % 8 == 0)
            turn_out(NT - 1, 0)
            keep_turned(NT - 1, 0)
            h_out(NT - 1, 0, 0, 3, True)

            act.wait_ge(srci_made, 1)
            act.copy(idx[:], srci[:, 0:BODY]).then_inc(idx_staged, 4)
            act.wait_ge(shift_ready, 1)

            def load_dlr(q, j):
                act.wait_ge(dlr_used, q + 1)
                act.dma_start(dlr[:, QUAD * (j % 4):QUAD * (j % 4) + QUAD, :],
                              dst_rows[bass.ds(QUAD * q, QUAD), :].rearrange("(a t) e -> a t e", a=1).broadcast_to([P, QUAD, P])).then_inc(dlr_in[j % 4], 16)

            def one_hot_far(q):
                act.wait_ge(oh_made, q + 1)
                for t in range(QUAD):
                    last = act.activation(away[1][:, t, :], iota_f[:], ACT.Abs, bias=dl[:, bass.ds(QUAD * q + t, 1)], scale=-1.0)
                last.then_inc(away_made, 1)

            def one_hots(q, j, u):
                act.wait_ge(dlr_in[j % 4], 16 * u + 16)
                act.wait_ge(oht_made, q + 1)
                act.activation(away[0], dlr[:, QUAD * (j % 4):QUAD * (j % 4) + QUAD, :], ACT.Abs, bias=place[:], scale=-1.0).then_inc(dlr_used, 1)
                act.wait_ge(away_made, q + 1)
                act.wait_ge(summed, QUAD * q + QUAD)
                act.activation(oh[j % 4], away[1], ACT.Relu, bias=ones[:, 0:1], scale=-1.0).then_inc(oh_made, 1)
                act.wait_ge(dlr_used, q + 1 + 4)
                act.wait_ge(ad_made, q + 1)
                act.activation(oht[j % 2], away[0], ACT.Relu, bias=ones[:, 0:1], scale=-1.0).then_inc(oht_made, 1)

            def p_of(q, j):
                act.wait_ge(eu_made, q + 1)
                act.activation(ev, eu[j % 2], ACT.Relu).then_inc(eu_pos, 1)
                act.wait_ge(eu_pos, q + 1)
                act.activation(gath[:, 4 * (j % 4):4 * (j % 4) + 4, D:ROW], ev, ACT.Exp, scale=-1.0).then_inc(p_made, 1)

            def stage(q, j):
                o = QUAD * (j % 4)
                act.copy(idx[:, o:o + QUAD], srci[:, bass.ds(QUAD * q + BODY, QUAD)]).then_inc(idx_staged, 1)

            def kv_h0(r, w=2):
                n = w * P
                act.wait_ge(k_made, r + 1)
                act.copy(kxs[:, :, 0:n], xTv[:, :, bass.ds(2 * P * r, n)]).then_inc(kx_out, 1)

            def kv_h1(r, w=2):
                act.wait_ge(k_made, r + 2)
                act.wait_ge(phi_made, r + 1)
                act.activation(ea[:, 0:w * D], bank[5][:, 0:w * D], ACT.Exp)
                act.activation(eb[:, 0:w * D], bank[5][:, 0:w * D], ACT.Relu).then_inc(k_out, 1)

            def att_h0(r, w=2):
                n = w * P
                act.wait_ge(q_made, r + 1)
                act.wait_ge(phiq_made, r + 1)
                for m in range(C):
                    sl = slice(m * 2 * P, m * 2 * P + n)
                    act.activation(ea[:, sl], bank[5][:, sl], ACT.Exp, bias=bqs[:, m:m + 1])
                    last = act.activation(eb[:, sl], bank[5][:, sl], ACT.Relu, bias=bqs[:, m:m + 1])
                last.then_inc(q_out, 1)

            def att_h1(r, w=2):
                act.wait_ge(rq_made, r + 1)
                act.wait_ge(rq_spread, r + 1)
                act.copy(rqx[:, 0:w * D].rearrange("p (k f) -> p k f", f=FH),
                         rq[:, 0:w * HEADS].unsqueeze(2).broadcast_to([P, w * HEADS, FH])).then_inc(rqx_made, 1)

            def body(i, early, late, left=2):
                for j in range(4):
                    q = 4 * i + j
                    if j in early:
                        early[j]()
                    if left:
                        one_hot_far(q + 4)
                    if left or j < 2:
                        p_of(q + 2, j + 2)
                    if left:
                        stage(q + 2, j + 2)
                        one_hots(q + 4, j, i + 1)
                        if left > 1:
                            load_dlr(q + 8, j)
                    if j in late:
                        late[j]()

            act.sem_inc(dlr_used, 4)
            act.sem_inc(oht_made, 1)
            act.sem_inc(oh_made, 1)
            act.sem_inc(k_out, 1)
            act.sem_inc(q_out, 1)
            act.wait_ge(dst_rows_out, 16)
            for q in range(4):
                load_dlr(q, q)
            for q in range(4):
                one_hot_far(q)
                one_hots(q, q, 0)
                load_dlr(q + 4, q)
                if q >= 2:
                    p_of(q - 2, q - 2)
                    stage(q - 2, q - 2)
            body(0, {2: lambda: kv_h0(0)}, {})
            with act.Fori(1, PAIRS) as i:
                body(i, {0: lambda: kv_h1(i - 1), 2: lambda: kv_h0(i)}, {})
            body(PAIRS, {0: lambda: kv_h1(PAIRS - 1), 2: lambda: kv_h0(PAIRS, 1)}, {})
            body(PAIRS + 1, {0: lambda: kv_h1(PAIRS, 1)}, {})
            A = PAIRS + 2
            with act.Fori(0, PAIRS) as r:
                body(A + r, {0: lambda: att_h0(r)}, {1: lambda: att_h1(r)})
            body(A + PAIRS, {0: lambda: att_h0(PAIRS, 1)}, {1: lambda: att_h1(PAIRS, 1)}, left=1)
            body(BODIES - 1, {}, {}, left=0)

            def y_evac(r, q, w=2):
                act.wait_ge(y_turned, r + 1)
                act.copy(xTv[:, :, bass.ds(2 * P * r, w * P)],
                         bank[q][:].rearrange("p (c n) -> p c n", c=C)[:, :, 0:w * P]).then_inc(y_out, 1)

            act.sem_inc(y_out, 2)
            with act.Fori(0, PAIRS // 2) as u:
                for q in range(2):
                    y_evac(2 * u + q, q)
            y_evac(PAIRS, 0, 1)

            for k, sl in enumerate((slice(16, 24), slice(40, 48), slice(90, 91))):
                act.wait_ge(route_dve, EXPS[k])
                act.activation(rt[:, sl], rt[:, sl], ACT.Exp).then_inc(route_act, 1)

            act.wait_ge(w_picked, 16 * TOPK * (C + 2 * FJ + 1))

            def hidden(g, w=4):
                for k in range(EJ):
                    act.wait_ge(hid_made, EJ * g + k + 1)
                    act.activation(hT[:, k, 0:w * P], bank[k % 4][:, 0:w * P], ACT.Gelu, bias=b1s[:, k:k + 1]).then_inc(hid_out, 1)

            act.sem_inc(hid_out, 4)
            with act.Fori(0, NT // 4) as g:
                hidden(g)
            hidden(NT // 4, 1)

        @block.tensor
        def _(pe):
            pe.wait_ge(const, CONSTS)
            pe.wait_ge(setup_dve, 1)
            cut = (0, 400, WHOLE)
            for k in range(2):
                last = pe.matmul(bank[k][0:NB, 0:cut[k + 1] - cut[k]], ones[0:1, 0:NB], ld_f[0:1, cut[k]:cut[k + 1]], start=True, stop=True)
            last.then_inc(setup_pe, 1)
            pe.wait_ge(setup_dve, 5)
            for k in range(2):
                pe.matmul(bank[2 + k][0:1, 0:SW // 2], ones[0:NB, 0:1], moved[:, k * SW // 2:(k + 1) * SW // 2], start=True, stop=True)
            for c in range(SC):
                last = pe.matmul(bank[4][:, c:c + 1], moved[:, c * P:c * P + P], ones[0:NB, 0:1], start=True, stop=True)
            last.then_inc(setup_pe, 1)

            pe.sem_inc(xs_turned, 2)
            pe.sem_inc(h_made, 2)
            pe.wait_ge(setup_dve, 8)
            pe.wait_ge(watt, 2)

            def turn(i, q):
                pe.wait_ge(xs_made, i + 1)
                pe.wait_ge(xts_kept, i + 1)
                for c in range(C):
                    last = pe.transpose(bank[q][:, c * P:c * P + P], xs[q][:, c * P:c * P + P], ident[:])
                last.then_inc(xs_turned, 1)

            def project(i, q):
                pe.wait_ge(xts_out, i + 1 + 2)
                pe.wait_ge(ht_out, i + 1)
                for c in range(C):
                    last = pe.matmul(bank[2 + q][:, 0:HW], xts[q][:, c, :], wg[:, c, :], start=(c == 0), stop=(c == C - 1))
                last.then_inc(h_made, 1)

            with pe.Fori(0, 3) as u:
                for j in range(0, 16, 2):
                    for q in range(2):
                        turn(16 * u + j + q, q)
                    for q in range(2):
                        project(16 * u + j + q, q)
            turn(NT - 1, 0)
            project(NT - 1, 0)

            pe.wait_ge(setup_dve, 9)
            pe.wait_ge(ht_out, NT + 2)
            for k in (1, 0):
                for c in range(SC):
                    b = 2 * k + c // 4
                    last = pe.transpose(bank[b][:, c % 4 * P:c % 4 * P + P], rows_f[:, k, c, :], ident[:])
                last.then_inc(rows_turned, 1)
            pe.wait_ge(shift_dve, 2)
            pe.transpose(bank[4][0:16, 0:P], ext, ident[:]).then_inc(shift_pe, 1)
            pe.wait_ge(shift_dve, 4)
            pe.matmul(bank[4][:, 128:144], ones[0:16, :], exd, start=True, stop=True).then_inc(shift_pe, 1)
            pe.wait_ge(shift_dve, 8)
            general = pe.value_load(flag[0:1, 0:1], min_val=0, max_val=1)
            with pe.If(general):
                exact_maxima_pe(pe)

            pe.wait_ge(shift_ready, 1)
            pe.sem_inc(summed, BODY)
            pe.sem_inc(ad_made, 2)
            pe.matmul(bank[6][:], zeros[:, 0:P], zeros[:].unsqueeze(1).broadcast_to([P, C, D]), start=True, stop=False)
            for t in (k_made, g_made, rq_spread, att_made):
                pe.sem_inc(t, 1)

            def spread_ad(q, j, b):
                pe.wait_ge(oht_made, q + 1 + 1)
                if not (isinstance(q, int) and q < 2):
                    pe.wait_ge(eu_made, q - 1)
                for t in range(QUAD):
                    o = AD_AT + 16 * t
                    last = pe.matmul(bank[2 if j % 2 == 0 else 7][:, o:o + 16], oht[j % 2][:, t, :], aa[:, 8:][:, bass.ds(b[t], 16)], start=True, stop=True)
                last.then_inc(ad_made, 1)

            def sum_up(q, j):
                pe.wait_ge(oh_made, q + 1 + 1)
                pe.wait_ge(weighed, q + 1)
                for t in range(QUAD):
                    pe.wait_ge(added, QUAD * q + t + 1)
                    pe.matmul(bank[SUMS[t]][:, 0:ROW], oh[j % 4][:, t, :], gath[:, 4 * (j % 4) + t, :], start=True, stop=True).then_inc(summed, 1)

            def kv_h0(r, ts, w=2):
                pe.wait_ge(kx_out, r + 1)
                pe.wait_ge(k_out, r + 1)
                pe.wait_ge(ksum_added, r + 2)
                for t in ts:
                    o = bank[5][:, t * D:t * D + D]
                    pe.matmul(o, ones[0:1, :], bks[0:1, :], start=True, stop=False)
                    for c in range(C):
                        last = pe.matmul(o, kxs[:, c, t * P:t * P + P], wks[:, c, :], start=False, stop=(c == C - 1))
                if ts[-1] == w - 1:
                    last.then_inc(k_made, 1)

            def kv_h2(r, w=2):
                k = P if w == 2 else LAST
                pe.wait_ge(phi_made, r + 2)
                pe.wait_ge(xg_in, 16 * r + 16)
                for m in range(C):
                    for t in range(w):
                        pe.matmul(bank[6][:, m * D:m * D + D], ph[0:k, t * D + m * P:t * D + m * P + P], xg[0:k, t, :],
                                  start=False, stop=(w == 1 and m == C - 1))
                for m in range(C):
                    for t in range(w):
                        last = pe.matmul(bank[5][:, m:m + 1], ph[0:k, t * D + m * P:t * D + m * P + P], ones[0:k, 0:1],
                                         start=(t == 0), stop=(t == w - 1))
                last.then_inc(g_made, 1)

            def m_stage():
                pe.wait_ge(m_dve, 1)
                for c in range(C):
                    for m in range(C):
                        pe.transpose(bank[5][:, c * D + m * P:c * D + m * P + P], kvg[:, m, c * P:c * P + P], ident[:])
                for m in range(C):
                    last = pe.matmul(bank[6][0:1, m * P:m * P + P], ksum[:, m:m + 1], ident[:], start=True, stop=True)
                last.then_inc(m_pe, 1)
                pe.wait_ge(m_dve, 2)
                for m in range(C):
                    o = bank[5][:, m * P:m * P + P]
                    pe.matmul(o, bvs[0:1, m * P:m * P + P], ksr[0:1, m * P:m * P + P], start=True, stop=False)
                    for c in range(C):
                        last = pe.matmul(o, wvs[:, c, m * P:m * P + P], gT[:, c * D + m * P:c * D + m * P + P], start=False, stop=(c == C - 1))
                last.then_inc(m_pe, 1)
                pe.wait_ge(m_dve, 3)
                for m in range(C):
                    last = pe.matmul(bank[6][:, m * D:m * D + D], kvm[:, m, :], wos[:, m, :], start=True, stop=True)
                last.then_inc(m_pe, 1)
                pe.wait_ge(m_dve, 4)

            def att_h0(r, w=2):
                n = w * P
                pe.wait_ge(q_out, r + 1)
                if not (isinstance(r, int) and r == 0):
                    pe.wait_ge(xo_made, r)
                for m in range(C):
                    for c in range(C):
                        last = pe.matmul(bank[5][:, m * 2 * P:m * 2 * P + n], wqs[:, c, m * P:m * P + P], xTv[:, c, bass.ds(2 * P * r, n)],
                                         start=(c == 0), stop=(c == C - 1))
                last.then_inc(q_made, 1)

            def att_h1(r, w=2):
                pe.wait_ge(phiq_made, r + 2)
                for t in range(w):
                    for m in range(C):
                        last = pe.matmul(bank[5][:, 8 * t:8 * t + 8], ph[:, m * 2 * P + t * P:m * 2 * P + t * P + P], kb[:, m, :],
                                         start=(m == 0), stop=(m == C - 1))
                last.then_inc(norm_made, 1)

            def att_h2(r, w=2):
                pe.wait_ge(rqx_made, r + 1)
                pe.wait_ge(qn_made, r + 1)
                for m in range(C):
                    for t in range(w):
                        last = pe.transpose(bank[6][:, m * 2 * P + t * P:m * 2 * P + t * P + P], rqx[:, t * D + m * P:t * D + m * P + P], ident[:])
                last.then_inc(rq_spread, 1)

            def att_h3(r, rqs, w=2):
                pe.wait_ge(qn_made, r + 2)
                pe.wait_ge(rq_made, rqs)
                pe.wait_ge(xo_made, r + 1)
                for t in range(w):
                    o = bank[5][:, t * D:t * D + D]
                    pe.matmul(o, ones[0:1, :], bsum[0:1, :], start=True, stop=False)
                    for m in range(C):
                        last = pe.matmul(o, qn[:, m * 2 * P + t * P:m * 2 * P + t * P + P], m_sb[:, m, :], start=False, stop=(m == C - 1))
                last.then_inc(att_made, 1)

            def body(i, hooks, last=False):
                b = blocks_of(mybir.EngineType.PE, brow_aa, 24, BODY * i + 3 * QUAD, QUAD if last else BODY)
                for j in range(4):
                    q = 4 * i + j
                    if not (last and j >= 1):
                        spread_ad(q + 3, j + 3, b[QUAD * j:QUAD * j + QUAD])
                    if not (last and j == 3):
                        sum_up(q + 1, j + 1)
                    if j in hooks:
                        hooks[j]()

            b = blocks_of(mybir.EngineType.PE, brow_aa, 24, 0, 3 * QUAD)
            for q in range(3):
                spread_ad(q, q, b[QUAD * q:QUAD * q + QUAD])
            sum_up(0, 0)
            def ks(r, w=2):
                return {2 + t: lambda t=t: kv_h0(r, (t,), w) for t in range(w)}

            body(0, ks(0))
            with pe.Fori(1, PAIRS) as i:
                body(i, {**ks(i), 1: lambda: kv_h2(i - 1)})
            body(PAIRS, {**ks(PAIRS, 1), 1: lambda: kv_h2(PAIRS - 1)})
            body(PAIRS + 1, {1: lambda: kv_h2(PAIRS, 1), 2: m_stage, 3: lambda: att_h0(0)})
            A = PAIRS + 2

            def att(r, w=2, w_next=2):
                return {0: lambda: att_h1(r, w), 1: lambda: att_h3(r - 1, r + 1), 2: lambda: att_h2(r, w), 3: lambda: att_h0(r + 1, w_next)}

            body(A, {**att(0), 1: lambda: None})
            with pe.Fori(1, PAIRS - 1) as r:
                body(A + r, att(r))
            body(A + PAIRS - 1, att(PAIRS - 1, 2, 1))
            body(A + PAIRS, {**att(PAIRS, 1), 3: lambda: None})
            body(BODIES - 1, {1: lambda: att_h3(PAIRS, PAIRS + 1, 1)}, last=True)

            pe.wait_ge(added, STEPS + 4)
            pe.matmul(bank[2][0:1, 0:D], zeros[:, 0:1], zeros[:, 0:D], start=True, stop=False)
            pe.sem_inc(y_used, 2)

            def turn_y(r, q, w=2):
                pe.wait_ge(y_made, r + 1)
                pe.wait_ge(y_out, r + 1)
                for c in range(C):
                    for t in range(w):
                        last = pe.transpose(bank[q][:, c * D + t * P:c * D + t * P + P], ys[q][:, t, c * P:c * P + P], ident[:])
                last.then_inc(y_turned, 1)
                k = P if w == 2 else LAST
                for t in range(w):
                    last = pe.matmul(bank[2][0:1, 0:D], ones[0:k, 0:1], ys[q][0:k, t, :], start=False, stop=(w == 1))
                last.then_inc(y_used, 1)

            with pe.Fori(0, PAIRS // 2) as u:
                for q in range(2):
                    turn_y(2 * u + q, q)
            turn_y(PAIRS, 0, 1)

            pe.wait_ge(route_dve, 1)
            for c in range(C):
                last = pe.matmul(bank[3][:, c:c + 1], mrow[0:1, c * P:c * P + P], ones[0:1, 0:1], start=True, stop=True)
            last.then_inc(route_pe, 1)
            pe.wait_ge(route_dve, 2)
            for c in range(C):
                last = pe.matmul(bank[3][0:1, 16:16 + EXPERTS], mcol[:, c:c + 1], wrs[:, c, :], start=(c == 0), stop=(c == C - 1))
            last.then_inc(route_pe, 1)
            pe.wait_ge(route_dve, ROUTE - 2)
            pe.matmul(bank[3][:, 32:36], ones[0:1, :], sel, start=True, stop=True).then_inc(route_pe, 1)

            pe.wait_ge(w_picked, 16 * TOPK * (C + 2 * FJ + 1))
            pe.wait_ge(w2_scaled, 1)
            pe.wait_ge(y_out, PAIRS + 3)

            def experts(g, w=4):
                n = w * P
                for k in range(EJ):
                    e, j = k // FJ, k % FJ
                    pe.wait_ge(hid_out, EJ * g + k + 1)
                    for c in range(C):
                        last = pe.matmul(bank[k % 4][:, 0:n], w1s[:, e, c, j * P:j * P + P], xTv[:, c, bass.ds(4 * P * g, n)],
                                         start=(c == 0), stop=(c == C - 1))
                    last.then_inc(hid_made, 1)
                for t in range(w):
                    pe.wait_ge(z_made, 4 * g + t + 1)
                    for k in range(EJ):
                        if t == 0:
                            pe.wait_ge(hid_out, EJ * g + k + 5)
                        last = pe.matmul(bank[4 + t % 2][:, 0:D], hT[:, k, t * P:t * P + P], w2s[:, k, :], start=(k == 0), stop=(k == EJ - 1))
                    last.then_inc(moe_made, 1)

            with pe.Fori(0, NT // 4) as g:
                experts(g)
            experts(NT // 4, 1)

        @block.vector
        def _(dve):
            def linker(s, n=0):
                count = [n]

                def then(ins):
                    count[0] = count[0] + 1
                    ins.then_inc(s, 1)
                    dve.wait_ge(s, count[0])
                return then

            def tile_of(i):
                return accx[:, bass.ds(i, 1), :].rearrange("p a f -> p (a f)")

            def statistics(g, h, width=8):
                then = linker(stat, 3 * g)
                settle(dve)
                for j in range(width):
                    last = dve.bn_stats(stats[:, j, :], tile_of(8 * g + j))
                then(last)
                settle(dve)
                for j in range(width):
                    last = dve.bn_aggr(mv[h][:, j, :], stats[:, j, :])
                then(last)
                dve.tensor_scalar(mv[h][:, 0:width, 1], mv[h][:, 0:width, 1], LN_EPS, None, ALU.add).then_inc(stat, 1)

            def normalize(g, h, width=8):
                dve.wait_ge(rstd_made, g + 1)
                for j in range(width):
                    xj = tile_of(8 * g + j)
                    mean, rs = mv[h][:, j, 0:1], rstd[h][:, j:j + 1]
                    dve.wait_ge(xs_turned, 8 * g + j + 1)
                    dve.tensor_scalar(xs[j % 2], xj, mean, rs, ALU.subtract, ALU.mult).then_inc(xs_made, 1)
                    dve.tensor_scalar(xj, xj, mean, rs, ALU.subtract, ALU.mult).then_inc(xn_made, 1)

            then = linker(setup_dve)
            dve.wait_ge(ld, 16)
            then(dve.tensor_copy(ld_f, ld_i))
            for g in range(2):
                dve.wait_ge(x_in[g], 16)
                statistics(g, g)
            dve.wait_ge(const, CONSTS)
            dve.wait_ge(setup_pe, 1)
            cut = (0, 400, WHOLE)
            for k in range(2):
                last = dve.tensor_scalar(before[:, cut[k]:cut[k + 1]], bank[k][0:NB, 0:cut[k + 1] - cut[k]], bthr, None, ALU.is_lt)
            then(last)
            then(dve.tensor_reduce(cnt, before, AX_X, ALU.add))
            then(dve.tensor_add(key, cnt, bnum))
            then(dve.tensor_scalar(moved, stepk, key, None, ALU.is_ge))
            dve.wait_ge(setup_pe, 2)
            for k in range(2):
                for t, width in ((brow_aa, 24), (brow_acc, ROW)):
                    dve.tensor_scalar(t[0:1, k * SW // 2:(k + 1) * SW // 2], bank[2 + k][0:1, 0:SW // 2], float(width), None, ALU.mult)
            then(dve.tensor_copy(bcol, bank[4][:, 0:SC]))
            dve.tensor_scalar(b128, bcol, float(P), None, ALU.mult)
            then(dve.scalar_tensor_tensor(out=tcol, in0=bcol, scalar=-1.0, in1=kcol, op0=ALU.mult, op1=ALU.add))
            then(dve.tensor_scalar(tcol_i, tcol, float(ET - 1), None, ALU.min))

            dve.wait_ge(wts, 16 * WEIGHTS)
            for k in range(2):
                dve.wait_ge(stored[k], 16)
                last = dve.tensor_mul(prod[:, k, :, :], wg[:, :, 0:D], attb[:, k:k + 1, :].broadcast_to([P, C, D]))
            last.then_inc(watt, 1)
            dve.wait_ge(watt, 1)
            for k in range(2):
                for c in range(C):
                    last = dve.tensor_reduce(wg[:, c, D + HEADS * k:D + HEADS * k + HEADS], prod[:, k, c, :].rearrange("p (h f) -> p h f", f=FH), AX_X, ALU.add)
            last.then_inc(watt, 1)

            dve.wait_ge(x_rest, 32)
            with dve.Fori(0, 2) as u:
                for h in range(2):
                    normalize(2 * u + h, h)
                    statistics(2 * u + 2 + h, h)
            normalize(4, 0)
            statistics(6, 0, 1)
            normalize(5, 1)
            normalize(6, 0, 1)

            dve.wait_ge(rows_got, 16 * 2 * SC)
            dve.tensor_copy(rows_f[:, 0, :, :], rows_i[:, 0, :, :])
            for c in range(SC):
                last = dve.tensor_scalar(rows_f[:, 1, c, :], rows_i[:, 1, c, :], b128[:, c:c + 1], None, ALU.subtract)
            last.then_inc(setup_dve, 1)
            dve.wait_ge(setup_dve, 9)
            dve.tensor_copy(dlb, rows_f[:, 1, :, :]).then_inc(dlb_made, 1)
            for k, t in ((1, dl), (0, srci)):
                dve.wait_ge(rows_turned, 2 - k)
                dve.tensor_copy(t[:, 0:512], bank[2 * k][:])
                last = dve.tensor_copy(t[:, 512:SW], bank[2 * k + 1][:, 0:SW - 512])
            last.then_inc(srci_made, 1)

            then = linker(shift_dve)
            dve.wait_ge(aa_kept, NT + 16)
            by_head = aav[:, :, 0:HEADS].rearrange("p n k -> p k n")
            dve.tensor_reduce(ext[:, 0:8], by_head, AX_X, ALU.max)
            then(dve.tensor_reduce(ext[:, 8:16], by_head, AX_X, ALU.min))
            then(dve.tensor_scalar(ext[:, 8:16], ext[:, 8:16], -1.0, None, ALU.mult))
            dve.wait_ge(shift_pe, 1)
            then(dve.tensor_reduce(exr, bank[4][0:16, 0:P], AX_X, ALU.max))
            then(dve.tensor_scalar(exd, ident[0:16, 0:16], exr, None, ALU.mult))
            dve.wait_ge(shift_pe, 2)
            then(dve.tensor_copy(exb, bank[4][:, 128:144]))
            dve.tensor_copy(sm, exb[:, 0:8].unsqueeze(1).broadcast_to([P, NT, HEADS]))
            then(dve.tensor_add(exm, exb[:, 0:8], exb[:, 8:16]))
            then(dve.tensor_reduce(ext[:, 0:1], exm, AX_X, ALU.max))
            then(dve.tensor_scalar(flag[0:1, 0:1], ext[0:1, 0:1], spread, None, ALU.is_gt))
            dve.wait_ge(xn_stored, 16 * 7)
            general = dve.value_load(flag[0:1, 0:1], min_val=0, max_val=1)
            with dve.If(general):
                exact_maxima_dve(dve, linker)
            dve.wait_ge(sm_ready, 1)
            then(dve.tensor_add(sm, sm, aav[:, :, 8:16]))
            dve.scalar_tensor_tensor(out=aav[:, :, 16:24], in0=sm, scalar=SLOPE, in1=sm, op0=ALU.mult, op1=ALU.max).then_inc(shift_ready, 1)

            dve.memset(acc[:], 0.0).then_inc(acc_zero, 1)
            dve.memset(ksum, 0.0).then_inc(acc_zero, 1)
            dve.wait_ge(acc_zero, 2)
            dve.sem_inc(added, 4)
            dve.sem_inc(ksum_added, 2)
            for t in (phi_made, phiq_made, qn_made, xo_made, xo_free):
                dve.sem_inc(t, 1)

            def weigh(q, j):
                dve.wait_ge(p_made, q + 1)
                g = gath[:, 4 * (j % 4):4 * (j % 4) + 4, :]
                h = g[:, :, 0:D].rearrange("p t (k f) -> p t k f", f=FH)
                dve.tensor_mul(h, h, g[:, :, D:ROW].unsqueeze(3).broadcast_to([P, QUAD, HEADS, FH])).then_inc(weighed, 1)

            def score_and_add(score_q, js, u, add_q, b):
                def add(t):
                    if add_q is not None:
                        k = QUAD * add_q + t
                        sums = acc[:, bass.ds(b[t], ROW)]
                        dve.wait_ge(summed, k + 1 + BODY)
                        dve.wait_ge(added, k + 4)
                        dve.tensor_add(sums, sums, bank[SUMS[t]][:, 0:ROW]).then_inc(added, 1)

                if score_q is None:
                    for t in range(QUAD):
                        add(t)
                    return
                for t in range(QUAD):
                    dve.wait_ge(got[4 * (js % 4) + t], 16 * u + 16)
                dve.wait_ge(ad_made, score_q + 1 + 2)
                ad = bank[2 if js % 2 == 0 else 7][:, AD_AT:AD_AT + 16 * QUAD].rearrange("p (t k) -> p t k", t=QUAD)
                dve.tensor_add(et, gath[:, 4 * (js % 4):4 * (js % 4) + 4, D:ROW], ad[:, :, 0:8]).then_inc(e_dve, 1)
                add(0)
                dve.wait_ge(e_dve, 2 * score_q + 1)
                dve.scalar_tensor_tensor(out=el, in0=et, scalar=SLOPE, in1=et, op0=ALU.mult, op1=ALU.max).then_inc(e_dve, 1)
                add(1)
                dve.wait_ge(e_dve, 2 * score_q + 2)
                dve.tensor_sub(eu[js % 2], ad[:, :, 8:16], el).then_inc(eu_made, 1)
                add(2)
                add(3)

            def halves(t, n):
                return t[:, 0:2 * D].rearrange("p (m n) -> p m n", m=2)[:, :, 0:n]

            def kv_h1(r, w=2):
                dve.wait_ge(k_out, r + 2)
                dve.wait_ge(g_made, r + 1)
                dve.scalar_tensor_tensor(out=ph[:, 0:w * D], in0=ea[:, 0:w * D], scalar=1.0, in1=eb[:, 0:w * D],
                                         op0=ALU.min, op1=ALU.add).then_inc(phi_made, 1)

            def kv_h2(r):
                dve.wait_ge(g_made, r + 2)
                dve.wait_ge(ksum_added, r + 2)
                dve.tensor_add(ksum, ksum, bank[5][:, 0:C]).then_inc(ksum_added, 1)

            def m_stage():
                then = linker(m_dve)
                dve.wait_ge(g_made, PAIRS + 2)
                dve.wait_ge(ksum_added, PAIRS + 1 + 2)
                then(dve.tensor_copy(kvg, bank[6][:].rearrange("p (m f) -> p m f", m=C)))
                for m in range(C):
                    dve.tensor_scalar(kb[:, m, :], kbmask[:, m, :], ksum[:, m:m + 1], None, ALU.mult)
                dve.wait_ge(m_pe, 1)
                dve.tensor_copy(gT, bank[5][:])
                then(dve.tensor_copy(ksr, bank[6][0:1, 0:D]))
                dve.wait_ge(m_pe, 2)
                then(dve.tensor_mul(kvm, bank[5][:, 0:D].rearrange("p (m f) -> p m f", m=C), headmask[:].unsqueeze(1).broadcast_to([P, C, P])))
                dve.wait_ge(m_pe, 3)
                then(dve.tensor_copy(m_sb[:], bank[6][:].rearrange("p (m f) -> p m f", m=C)))

            def att_h1(r, w=2):
                n = w * P
                dve.wait_ge(q_out, r + 2)
                dve.wait_ge(qn_made, r + 1)
                dve.scalar_tensor_tensor(out=halves(ph, n), in0=halves(ea, n), scalar=1.0, in1=halves(eb, n),
                                         op0=ALU.min, op1=ALU.add).then_inc(phiq_made, 1)

            def att_h2(r, w=2):
                dve.wait_ge(norm_made, r + 1)
                then = linker(norm_dve, r)
                then(dve.tensor_scalar(rq2[:, 0:8 * w], bank[5][:, 0:8 * w], NORM_EPS, None, ALU.add))
                dve.reciprocal(rq[:, 0:8 * w], rq2[:, 0:8 * w]).then_inc(rq_made, 1)

            def att_h3(r, w=2):
                n = w * P
                dve.wait_ge(rq_spread, r + 2)
                dve.wait_ge(att_made, r + 1)
                dve.tensor_mul(halves(qn, n), halves(ph, n), halves(bank[6], n)).then_inc(qn_made, 1)

            def att_h4(r, w=2):
                dve.wait_ge(att_made, r + 2)
                dve.wait_ge(xr_in, 16 * r + 16)
                dve.wait_ge(xo_free, r + 1)
                dve.tensor_add(xo[:, 0:w, :], bank[5][:, 0:w * D].rearrange("p (t f) -> p t f", f=D), xr[:, 0:w, :]).then_inc(xo_made, 1)

            def body(i, hooks, last=False):
                b = blocks_of(mybir.EngineType.DVE, brow_acc, ROW, BODY * i, BODY)
                for j in range(4):
                    q = 4 * i + j
                    more = not (last and j >= 2)
                    score_and_add(q + 2 if more else None, j + 2, i + (j + 2) // 4, q, b[QUAD * j:QUAD * j + QUAD])
                    if j in hooks:
                        hooks[j]()
                    if more:
                        weigh(q + 2, j + 2)

            for q in range(2):
                score_and_add(q, q, 0, None, None)
                weigh(q, q)
            body(0, {})
            with dve.Fori(1, PAIRS) as i:
                body(i, {0: lambda: kv_h1(i - 1), 2: lambda: kv_h2(i - 1)})
            body(PAIRS, {0: lambda: kv_h1(PAIRS - 1), 2: lambda: kv_h2(PAIRS - 1)})

            def end_of_kv():
                kv_h2(PAIRS)
                m_stage()

            body(PAIRS + 1, {0: lambda: kv_h1(PAIRS, 1), 2: end_of_kv})
            A = PAIRS + 2

            def att(r, w=2):
                return {0: lambda: att_h1(r, w), 1: lambda: att_h2(r, w), 2: lambda: att_h4(r - 1), 3: lambda: att_h3(r, w)}

            body(A, {**att(0), 2: lambda: None})
            with dve.Fori(1, PAIRS) as r:
                body(A + r, att(r))
            body(A + PAIRS, att(PAIRS, 1))
            body(BODIES - 1, {2: lambda: att_h4(PAIRS, 1)}, last=True)

            dve.wait_ge(added, STEPS + 4)
            then = linker(den_done)
            den = accv[:, :, D:ROW]
            then(dve.tensor_scalar(den, den, 1e-30, None, ALU.max))
            then(dve.reciprocal(den, den))
            dve.sem_inc(x1_made, 2)

            def x1_of(r, q, u, w=2):
                then = linker(x1_dve, 4 * r)
                t1 = accv[:, bass.ds(2 * r, w), :]
                h = t1[:, :, 0:D].rearrange("p t (k f) -> p t k f", f=FH)
                then(dve.tensor_mul(h, h, t1[:, :, D:ROW].unsqueeze(3).broadcast_to([P, w, HEADS, FH])))
                dve.wait_ge(xa_in[q], 16 * u + 16)
                dve.tensor_add(t1[:, :, 0:D], t1[:, :, 0:D], xa[q][:, 0:w, :]).then_inc(x1_made, 1)
                dve.wait_ge(x1_made, r + 1 + 2)
                settle(dve)
                for t in range(w):
                    last = dve.bn_stats(st2[:, t, :], t1[:, t, 0:D])
                then(last)
                settle(dve)
                for t in range(w):
                    last = dve.bn_aggr(mv2[q][:, t, :], st2[:, t, :])
                then(last)
                dve.tensor_scalar(mv2[q][:, 0:w, 1], mv2[q][:, 0:w, 1], LN_EPS, None, ALU.add).then_inc(x1_dve, 1)

            def y_of(r, q, w=2):
                t1 = accv[:, bass.ds(2 * r, w), :]
                dve.wait_ge(rstd2_made, r + 1)
                dve.tensor_copy(mrv[:, bass.ds(2 * r, w), :], mv2[q][:, 0:w, :])
                dve.wait_ge(y_used, r + 1)
                for t in range(w):
                    last = dve.tensor_scalar(ys[q][:, t, :], t1[:, t, 0:D], mv2[q][:, t, 0:1], mv2[q][:, t, 1:2], ALU.subtract, ALU.mult)
                last.then_inc(y_made, 1)

            def round_(u, w=2):
                x1_of(2 * u + 1, 1, u)
                y_of(2 * u, 0)
                x1_of(2 * u + 2, 0, u + 1, w)
                y_of(2 * u + 1, 1)

            x1_of(0, 0, 0)
            with dve.Fori(0, PAIRS // 2 - 1) as u:
                round_(u)
            round_(PAIRS // 2 - 1, 1)
            y_of(PAIRS, 0, 1)

            def softmax(src_, ex, k, out_, a, then):
                then(dve.tensor_reduce(rt[:, a:a + 1], src_, AX_X, ALU.max))
                then(dve.tensor_scalar(ex, src_, rt[:, a:a + 1], None, ALU.subtract))
                dve.wait_ge(route_act, k)
                then(dve.tensor_reduce(rt[:, a:a + 1], ex, AX_X, ALU.add))
                then(dve.reciprocal(rt[:, a + 1:a + 2], rt[:, a:a + 1]))
                then(dve.tensor_scalar(out_, ex, rt[:, a + 1:a + 2], None, ALU.mult))

            def first_greatest(v, top, where, then):
                then(dve.tensor_reduce(top, v, AX_X, ALU.max))
                then(dve.tensor_scalar(rt[:, 72:80], v, top, 100.0, ALU.is_lt, ALU.mult))
                then(dve.tensor_add(rt[:, 80:88], rt[:, 72:80], iota_f[0:1, 0:8]))
                then(dve.tensor_reduce(where, rt[:, 80:88], AX_X, ALU.min))

            then = linker(route_dve)
            dve.wait_ge(y_used, PAIRS + 1 + 2)
            then(dve.tensor_scalar(mrow, bank[2][0:1, 0:D], 1.0 / N, None, ALU.mult))
            dve.wait_ge(route_pe, 1)
            then(dve.tensor_copy(mcol, bank[3][:, 0:C]))
            dve.wait_ge(route_pe, 2)
            then(dve.tensor_add(rt[:, 0:8], bank[3][0:1, 16:24], brs[:]))
            softmax(rt[:, 0:8], rt[:, 16:24], 1, rt[:, 26:34], 24, then)
            then(dve.tensor_scalar(rt[:, 64:72], rt[:, 26:34], float(N), 1e-30, ALU.mult, ALU.max))
            then(dve.reciprocal(rt[:, 72:80], rt[:, 64:72]))
            then(dve.tensor_scalar(rt[:, 80:88], rt[:, 72:80], CAPACITY, 1.0, ALU.mult, ALU.min))
            then(dve.tensor_mul(rt[:, 96:104], rt[:, 26:34], rt[:, 80:88]))
            softmax(rt[:, 96:104], rt[:, 40:48], 2, rt[:, 56:64], 48, then)
            first_greatest(rt[:, 56:64], rt[:, 88:89], sel[:, 2:3], then)
            then(dve.tensor_scalar(rt[:, 104:112], iota_f[0:1, 0:8], sel[:, 2:3], -4.0, ALU.is_equal, ALU.mult))
            then(dve.tensor_add(rt[:, 112:120], rt[:, 56:64], rt[:, 104:112]))
            first_greatest(rt[:, 112:120], rt[:, 89:90], sel[:, 3:4], then)
            then(dve.tensor_sub(rt[:, 90:91], rt[:, 89:90], rt[:, 88:89]))
            dve.wait_ge(route_act, 3)
            then(dve.tensor_scalar(rt[:, 91:92], rt[:, 90:91], 1.0, None, ALU.add))
            then(dve.reciprocal(sel[:, 0:1], rt[:, 91:92]))
            then(dve.tensor_mul(sel[:, 1:2], rt[:, 90:91], sel[:, 0:1]))
            dve.wait_ge(route_pe, 3)
            then(dve.tensor_copy(selb, bank[3][:, 32:36]))
            for e in range(TOPK):
                last = dve.scalar_tensor_tensor(out=eidx[:, e, :], in0=mult7[:], scalar=selb[:, 2 + e:3 + e], in1=pidx7[:], op0=ALU.mult, op1=ALU.add)
            then(last)
            dve.wait_ge(route_dve, ROUTE)
            dve.wait_ge(w_picked, 16 * TOPK * (C + 2 * FJ + 1))
            for e in range(TOPK):
                w2e = w2s[:, e * FJ:(e + 1) * FJ, :]
                dve.tensor_scalar(w2e, w2e, selb[:, e:e + 1], None, ALU.mult)
            then(dve.tensor_scalar(b2w, b2s[:, 0, :], selb[:, 0:1], None, ALU.mult))
            dve.scalar_tensor_tensor(out=b2w, in0=b2s[:, 1, :], scalar=selb[:, 1:2], in1=b2w, op0=ALU.mult, op1=ALU.add).then_inc(w2_scaled, 1)

            dve.sem_inc(z_made, 2)

            def finish(i, q):
                x1 = accv[:, bass.ds(i, 1), 0:D].rearrange("p a f -> p (a f)")
                dve.tensor_scalar(yb[q], x1, mr[:, bass.ds(2 * i, 1)], mr[:, bass.ds(2 * i + 1, 1)], ALU.subtract, ALU.mult).then_inc(yb_made, 1)
                dve.wait_ge(moe_made, i + 1)
                dve.wait_ge(yb_full, i + 1)
                dve.wait_ge(out_made, i + 1)
                dve.tensor_add(zt[q], bank[4 + q][:, 0:D], yb[q]).then_inc(z_made, 1)
                dve.wait_ge(z_made, i + 1 + 2)
                then = linker(z_dve, 3 * i)
                settle(dve)                           
                then(dve.bn_stats(st3, zt[q]))
                settle(dve)
                then(dve.bn_aggr(mv3, st3))
                dve.tensor_scalar(mv3[:, 1:2], mv3[:, 1:2], LN_EPS, None, ALU.add).then_inc(z_dve, 1)
                dve.wait_ge(rstd3_made, i + 1)
                dve.tensor_scalar(zt[q], zt[q], mv3[:, 0:1], mv3[:, 1:2], ALU.subtract, ALU.mult).then_inc(zn_made, 1)

            with dve.Fori(0, PAIRS) as u:
                for q in range(2):
                    finish(2 * u + q, q)
            finish(NT - 1, 0)


_INS = ["x", "src", "dst", "L0_gnn_W", "L0_gnn_att_src", "L0_gnn_att_dst", "L0_gnn_bias", "L0_mix_wq", "L0_mix_bq",
        "L0_mix_wk", "L0_mix_bk", "L0_mix_wv", "L0_mix_bv", "L0_mix_wo", "L0_mix_bo", "L0_ffn_Wr", "L0_ffn_br",
        "L0_ffn_W1", "L0_ffn_b1", "L0_ffn_W2", "L0_ffn_b2", "L0_ffn_gamma", "L0_ffn_beta"]
_SCRATCH = [("table", (NP, ROW), F32), ("src_pad", (ET, P), I32), ("dst_pad", (ET, P), I32), ("asrc_tab", (NP, HEADS), F32),
            ("smax_tab", (NP, HEADS), F32), ("xn_d", (NP, D), F32), ("xa_d", (NP, D), F32), ("dst_rows", (SW, P), BF16)]


def kernel(**inputs):
    import numpy as _np
    import concourse.bacc as _bacc
    from concourse import mybir as _mybir
    from concourse.bass_utils import run_bass_kernel_spmd as _run

    nc = _bacc.Bacc("TRN2", target_bir_lowering=False, num_devices=1)
    arrays, args = {}, []
    for name in _INS:
        a = _np.ascontiguousarray(inputs[name])
        arrays[f"in_{name}_dram"] = a
        args.append(nc.dram_tensor(f"in_{name}_dram", a.shape, _mybir.dt.from_np(a.dtype), kind="ExternalInput").ap())
    args.append(nc.dram_tensor("out_0_dram", (N, D), F32, kind="ExternalOutput").ap())
    for name, shape, dt in _SCRATCH:
        args.append(nc.dram_tensor(name, shape, dt, kind="Internal").ap())
    gps_layer(nc, *args, SPREAD)
    r = _run(nc, [arrays], core_ids=[0])
    return r.results[0]["out_0_dram"]
```

```python
from contextlib import ExitStack

import concourse.bass as bass
from concourse import mybir

F32 = mybir.dt.float32
I32 = mybir.dt.int32
BF16 = mybir.dt.bfloat16
ALU = mybir.AluOpType
ACT = mybir.ActivationFunctionType
AX_X = mybir.AxisListType.X

P = 128
N, D = 6250, 256
HEADS, FH = 8, 32
EDGES = 100000
EXPERTS, HIDDEN, TOPK = 8, 512, 2
LN_EPS = 1e-5
NORM_EPS = 1e-6
SLOPE = 0.2
CAPACITY = float(-(-N * 5 // (4 * EXPERTS)))
SPREAD = 60.0
LOW = -1.0e38
CONSTS, WEIGHTS, ROUTE = 15, 12, 32
EXPS = (5, 14, 28)

NT = -(-N // P)
NP = NT * P
LAST = N - (NT - 1) * P
ROW = D + HEADS
C = D // P
HW = D + 2 * HEADS
QUAD = 4
BODY = 4 * QUAD
ET = 784
EP = ET * P
STEPS = ET + NT - 1
BODIES = STEPS // BODY
SC = -(-STEPS // P)
SW = SC * P
WHOLE = EDGES // P
NB = NT - 1
CH = 112
CL = EP // CH
SUMS = (0, 1, 3, 4)
AD_AT = 448
PAIRS = NT // 2
FJ = HIDDEN // P
EJ = TOPK * FJ
THIRD = 65
PAD_DST = NP - 1
assert STEPS == BODIES * BODY and NT % 16 == 1 and BODIES >= 2 * PAIRS + 4 and CL % 16 == 0


def gps_layer(nc, x, src, dst, gW, g_as, g_ad, g_bias, wq, bq, wk, bk, wv, bv, wo, bo, Wr, br, W1, b1, W2, b2,
              gamma, beta, out, table, src_pad, dst_pad, asrc_tab, smax_tab, xn_d, xa_d, dst_rows, spread):
    with ExitStack() as ctx:
        def sb(name, shape, dt=F32):
            return ctx.enter_context(nc.sbuf_tensor(name, shape, dt))

        def sem(name):
            return ctx.enter_context(nc.semaphore(name))

        bank = [ctx.enter_context(nc.psum_tensor(f"bank{i}", [P, 512], F32)) for i in range(8)]

        xT = sb("xT", [P, C * NP])
        xTv = xT[:].rearrange("p (c n) -> p c n", c=C)
        acc = sb("acc", [P, NT * ROW])
        accx = acc[:, 0:NT * D].rearrange("p (n f) -> p n f", f=D)
        accv = acc[:].rearrange("p (n f) -> p n f", f=ROW)
        aa = sb("aa", [P, NT * 24])
        aav = aa[:].rearrange("p (n k) -> p n k", k=24)
        mr = sb("mr", [P, NT * 2])
        mrv = mr[:].rearrange("p (n k) -> p n k", k=2)
        ident = sb("ident", [P, P])
        iota_f = sb("iota_f", [P, P])
        ones = sb("ones", [P, P])
        zeros = sb("zeros", [P, D])
        headmask = sb("headmask", [P, P])
        kbmask = sb("kbmask", [P, C, HEADS])
        wg = sb("wg", [P, C, HW])
        wqs, wks, wvs, wos = (sb(n, [P, C, D]) for n in ("wqs", "wks", "wvs", "wos"))
        bvs = sb("bvs", [1, D])
        bk_parts, bsum_parts = (sb(n, [THIRD, D], BF16) for n in ("bk_parts", "bsum_parts"))
        part_ones = sb("part_ones", [THIRD, P], BF16)
        brs = sb("brs", [1, EXPERTS])
        bqs = sb("bqs", [P, C])
        gam = sb("gam", [P, D])
        bet = sb("bet", [P, D])
        wrs = sb("wrs", [P, C, EXPERTS])
        brow_aa = sb("brow_aa", [1, SW], I32)
        brow_acc = sb("brow_acc", [1, SW], I32)
        dl = sb("dl", [P, SW])
        srci = sb("srci", [P, SW], I32)
        idx = sb("idx", [P, BODY], I32)
        kb = sb("kb", [P, C, HEADS])
        m_sb = sb("m_sb", [P, C, D])
        half = sb("half", [P, 8])
        place = sb("place", [P, 1])
        flag = sb("flag", [1, 1], I32)

        WORK = 16272
        work = sb("work", [P, WORK])
        worki = work[:].bitcast(I32)
        at = [0]

        def area(size, parts=P, ints=False):
            a = at[0]
            at[0] += size
            assert at[0] <= WORK, at[0]
            return (worki if ints else work)[0:parts, a:a + size]

        ld_i, ld_f = area(WHOLE, 1, True), area(WHOLE, 1)
        ht = area(16 * HW).rearrange("p (t f) -> p t f", f=HW)
        htf = ht.rearrange("p t f -> p (t f)")[0:NB, :]
        before, stepk, moved = htf[:, 0:WHOLE], htf[:, WHOLE:WHOLE + SW], htf[:, WHOLE + SW:WHOLE + 2 * SW]
        kcol, bcol, tcol, tcol_i = area(SC), area(SC), area(SC), area(SC, ints=True)
        b128 = area(SC)
        bthr, bnum, cnt, key = area(1, NB), area(1, NB), area(1, NB), area(1, NB)
        pad_i = area(2 * (EP - EDGES), 1, True).rearrange("p (k e) -> p k e", k=2)
        rows_i = area(2 * SW, ints=True).rearrange("p (k c e) -> p k c e", k=2, c=SC)
        rows_f = area(2 * SW).rearrange("p (k c e) -> p k c e", k=2, c=SC)
        dlb = area(SW // 2).bitcast(BF16).rearrange("p (c e) -> p c e", c=SC)
        stats = area(48).rearrange("p (t k) -> p t k", k=6)
        mv = [area(16).rearrange("p (t k) -> p t k", k=2) for _ in range(2)]
        rstd = [area(8) for _ in range(2)]
        attb = area(2 * D).rearrange("p (k f) -> p k f", k=2)
        xs = [area(D) for _ in range(4)]
        xts = [area(D).rearrange("p (c n) -> p c n", c=C) for _ in range(4)]
        prod = area(2 * C * D).rearrange("p (k c f) -> p k c f", k=2, c=C)
        ext, exb, exm, exr, exd = area(16), area(16), area(8), area(1, 16), area(16, 16)
        bks, bos, gbs, bsum, rest = (area(D, THIRD) for _ in range(5))
        part = area(D // 2, THIRD).bitcast(BF16)
        sm = area(NT * HEADS).rearrange("p (n k) -> p n k", k=HEADS)

        at[0] = 0
        gath = area(BODY * ROW).rearrange("p (t f) -> p t f", f=ROW)
        oh = [area(QUAD * P).rearrange("p (t d) -> p t d", t=QUAD) for _ in range(4)]
        oht = [area(QUAD * P).rearrange("p (t e) -> p t e", t=QUAD) for _ in range(2)]
        away = [area(QUAD * P).rearrange("p (t d) -> p t d", t=QUAD) for _ in range(2)]
        dlr = area(BODY * P // 2).bitcast(BF16).rearrange("p (t e) -> p t e", t=BODY)
        et, el = area(QUAD * HEADS).rearrange("p (t k) -> p t k", t=QUAD), area(QUAD * HEADS).rearrange("p (t k) -> p t k", t=QUAD)
        eu = [area(QUAD * HEADS).rearrange("p (t k) -> p t k", t=QUAD) for _ in range(2)]
        ev = area(QUAD * HEADS).rearrange("p (t k) -> p t k", t=QUAD)
        kxs = area(2 * D).rearrange("p (c n) -> p c n", c=C)
        ea, eb, ph, qn = area(2 * D), area(2 * D), area(2 * D), area(2 * D)
        xg = area(2 * D).rearrange("p (t f) -> p t f", f=D)
        xr, xo = area(2 * D).rearrange("p (t f) -> p t f", f=D), area(2 * D).rearrange("p (t f) -> p t f", f=D)
        rq, rq2, rqx = area(16), area(16), area(2 * D)
        kvg, ksum = area(C * D).rearrange("p (m f) -> p m f", m=C), area(C)
        gT, kvm, ksr = area(C * D), area(C * P).rearrange("p (m f) -> p m f", m=C), area(D, 1)

        at[0] = 0
        ys = [area(2 * D).rearrange("p (t f) -> p t f", f=D) for _ in range(2)]
        xa = [area(2 * D).rearrange("p (t f) -> p t f", f=D) for _ in range(2)]
        st2 = area(12).rearrange("p (t k) -> p t k", k=6)
        ab2 = [area(4).rearrange("p (t k) -> p t k", k=2) for _ in range(2)]
        mv2 = [area(4).rearrange("p (t k) -> p t k", k=2) for _ in range(2)]
        mrow, mcol, rt, sel, selb = area(D, 1), area(C), area(128, 1), area(4, 1), area(4)
        sel_i = area(TOPK, 1, ints=True)
        w1s = area(TOPK * C * HIDDEN).rearrange("p (e c f) -> p e c f", e=TOPK, c=C)
        w2s = area(EJ * D).rearrange("p (k f) -> p k f", f=D)
        b1s = area(EJ)
        b2s = area(TOPK * D).rearrange("p (e f) -> p e f", e=TOPK)
        b2w = dl[:, 2 * D:3 * D]
        hT = area(EJ * 4 * P).rearrange("p (k n) -> p k n", k=EJ)
        zt, ot = ([area(D) for _ in range(2)] for _ in range(2))
        yb = [dl[:, D * k:D * k + D] for k in range(2)]
        st3, mv3 = area(6), area(2)

        const, ld, pads, padded, wts = (sem(n) for n in ("const", "ld", "pads", "padded", "weights"))
        setup_dve, setup_pe, rows_got, watt = (sem(n) for n in ("setup_dve", "setup_pe", "rows_got", "watt"))
        x_in, x_rest = [sem(f"x_in{i}") for i in range(2)], sem("x_rest")
        rstd_made, rstd2_made, rstd3_made = (sem(n) for n in ("rstd_made", "rstd2_made", "rstd3_made"))
        stat, xs_made, xn_made, xs_turned, xts_out, xts_kept = (sem(n) for n in ("stat", "xs_made", "xn_made", "xs_turned", "xts_out", "xts_kept"))
        h_made, ht_out, aa_kept, gen_zero = (sem(n) for n in ("h_made", "ht_out", "aa_kept", "gen_zero"))
        xn_stored = [sem(f"xn_stored{i}") for i in range(2)]
        stored = [sem(f"table_stored{i}") for i in range(2)]
        rows_turned, srci_made, shift_dve, shift_pe, sm_ready, shift_ready = (sem(n) for n in ("rows_turned", "srci_made", "shift_dve", "shift_pe", "sm_ready", "shift_ready"))
        gen_dve, gen_pe, gen_pool, gen_dma, gen_copy, gen_copy2, gen_got, gen_put, gen_scan, gen_done = (
            sem(n) for n in ("gen_dve", "gen_pe", "gen_pool", "gen_dma", "gen_copy", "gen_copy2", "gen_got", "gen_put",
                             "gen_scan", "gen_done"))
        zeroed, ksum_zero, parts_made = sem("zeroed"), sem("ksum_zero"), sem("parts_made")
        idx_staged, oh_made, oht_made, ad_made, eu_made, eu_pos, p_made, weighed, summed = (
            sem(n) for n in ("idx_staged", "oh_made", "oht_made", "ad_made", "eu_made", "eu_pos", "p_made",
                             "weighed", "summed"))
        added = [sem(f"added{t}") for t in range(QUAD)]
        et_made, el_made, away_made, dlr_used, ksum_added, dlb_made, dst_rows_out = (
            sem(n) for n in ("et_made", "el_made", "away_made", "dlr_used", "ksum_added", "dlb_made", "dst_rows_out"))
        dlr_in = [sem(f"dlr_in{j}") for j in range(4)]
        got = [sem(f"gathered{i}") for i in range(BODY)]
        xg_in, kx_out, k_made, k_out, phi_made, g_made = (sem(n) for n in ("xg_in", "kx_out", "k_made", "k_out", "phi_made", "g_made"))
        m_dve, m_pe = sem("m_dve"), sem("m_pe")
        xr_in, q_made, q_out, phiq_made, norm_made, norm_dve, rq_made, rqx_made, rq_spread, qn_made, att_made, xo_made, xo_stored, xo_free = (
            sem(n) for n in ("xr_in", "q_made", "q_out", "phiq_made", "norm_made", "norm_dve", "rq_made", "rqx_made",
                             "rq_spread", "qn_made", "att_made", "xo_made", "xo_stored", "xo_free"))
        den_done, x1_dve, x1_scaled, ab_made, x1_made, y_made, y_turned, y_out, y_used = (sem(n) for n in ("den_done", "x1_dve", "x1_scaled", "ab_made", "x1_made", "y_made", "y_turned", "y_out", "y_used"))
        xa_in = [sem(f"xa_in{i}") for i in range(2)]
        route_dve, route_pe, route_act, picked, w1_in, w2_in, w2_scaled = (
            sem(n) for n in ("route_dve", "route_pe", "route_act", "picked", "w1_in", "w2_in", "w2_scaled"))
        hid_made, hid_out, moe_made, yb_made, yb_full, z_made, z_dve, zn_made, zg_made, out_made = (
            sem(n) for n in ("hid_made", "hid_out", "moe_made", "yb_made", "yb_full", "z_made", "z_dve", "zn_made", "zg_made", "out_made"))
        out_stored = [sem(f"out_stored{i}") for i in range(2)]

        def field(a, ints=False):
            return (acc[:].bitcast(I32) if ints else acc[:])[0:CH, CL * a:CL * a + CL]

        score = acc[0:CH, 0:CL * HEADS].rearrange("p (j k) -> p j k", k=HEADS)
        f_step, f_dst, i_src, i_dst, i_to = field(8), field(9), field(10, True), field(11, True), field(12, True)
        gx = acc[0:CH, CL * 13:CL * 13 + 16 * HEADS].rearrange("p (j k) -> p j k", k=HEADS)
        gi = acc[:].bitcast(I32)[0:CH, CL * 13 + 128:CL * 13 + 144]
        ends = acc[0:CH, CL * 13 + 144:CL * 13 + 168].rearrange("p (a k) -> p a k", k=HEADS)
        f_next = acc[0:CH, CL * 13 + 168:CL * 13 + 169]
        i_next = acc[:].bitcast(I32)[0:CH, CL * 13 + 169:CL * 13 + 170]
        carry = acc[0:CH, CL * 13 + 176:CL * 13 + 184]
        erow = acc[0:HEADS, CL * 13 + 184:CL * 13 + 184 + 3 * CH].rearrange("p (a c) -> p a c", a=3)
        crow = acc[0:HEADS, CL * 13 + 520:CL * 13 + 520 + 3 * CH].rearrange("p (a c) -> p a c", a=3)
        FAR = 65536.0

        def exact_maxima_pool(pool):
            dst_flat, src_flat = dst_pad.rearrange("t e -> (t e)"), src_pad.rearrange("t e -> (t e)")
            pool.wait_ge(zeroed, 7)
            pool.memset(i_next, PAD_DST + 1).then_inc(gen_pool, 1)
            pool.wait_ge(gen_pool, 1)
            pool.dma_start(i_src, src_flat.rearrange("(p j) -> p j", j=CL)).then_inc(gen_dma, 16)
            pool.dma_start(i_dst, dst_flat.rearrange("(p j) -> p j", j=CL)).then_inc(gen_dma, 16)
            with nc.allow_non_contiguous_dma(reason="one number for each chunk"):
                pool.dma_start(i_next[0:CH - 1, :], dst_flat.rearrange("(p j) -> p j", j=CL)[1:CH, 0:1]).then_inc(gen_dma, 16)
            for t in (asrc_tab, smax_tab):
                pool.dma_start(t.rearrange("(n p) f -> p n f", p=P), aav[:, :, 0:HEADS]).then_inc(gen_dma, 16)
            pool.wait_ge(gen_dma, 80)
            pool.sem_inc(gen_pool, 1)
            with pool.Fori(0, CL // 16) as i:
                pool.tensor_copy(gi, i_src[:, bass.ds(16 * i, 16)]).then_inc(gen_copy, 1)
                pool.wait_ge(gen_copy, 2 * i + 1)
                settle(pool)
                for j in range(16):
                    pool.indirect_dma_start(out=gx[:, j, :], out_offset=None, in_=asrc_tab[:, :],
                                            in_offset=bass.IndirectOffsetOnAxis(ap=gi[:, j:j + 1], axis=0)).then_inc(gen_got, 16)
                pool.wait_ge(gen_got, 256 * i + 256)
                pool.tensor_copy(score[:, bass.ds(16 * i, 16), :], gx).then_inc(gen_copy, 1)
                pool.wait_ge(gen_copy, 2 * i + 2)
                settle(pool)
            pool.sem_inc(gen_pool, 1)
            pool.wait_ge(gen_done, 1)
            with pool.Fori(0, CL // 16) as i:
                pool.tensor_copy(gi, i_to[:, bass.ds(16 * i, 16)]).then_inc(gen_copy2, 1)
                pool.tensor_copy(gx, score[:, bass.ds(16 * i, 16), :]).then_inc(gen_copy2, 1)
                pool.wait_ge(gen_copy2, 2 * i + 2)
                settle(pool)
                for j in range(16):
                    pool.indirect_dma_start(out=smax_tab[:, :], out_offset=bass.IndirectOffsetOnAxis(ap=gi[:, j:j + 1], axis=0),
                                            in_=gx[:, j, :], in_offset=None, bounds_check=NP - 1, oob_is_err=False).then_inc(gen_put, 16)
                pool.wait_ge(gen_put, 256 * i + 256)
                settle(pool)
            pool.dma_start(sm, smax_tab.rearrange("(n p) f -> p n f", p=P)).then_inc(gen_dma, 16)
            pool.wait_ge(gen_dma, 96)

        def exact_maxima_pe(pe):
            pe.wait_ge(gen_dve, 6)
            for a in range(3):
                last = pe.matmul(bank[0][0:HEADS, a * CH:a * CH + CH], ends[:, a, :], ident[0:CH, 0:CH], start=True, stop=True)
            last.then_inc(gen_pe, 1)
            pe.wait_ge(gen_dve, 12)
            pe.matmul(bank[1][0:CH, 0:HEADS], crow[:, 2, :], ident[0:HEADS, 0:HEADS], start=True, stop=True).then_inc(gen_pe, 1)

        def exact_maxima_dve(dve, linker):
            then = linker(gen_dve)
            dve.wait_ge(gen_pool, 2)
            dve.tensor_copy(f_next, i_next)
            then(dve.tensor_copy(f_dst, i_dst))
            dve.tensor_tensor(f_step[:, 0:CL - 1], f_dst[:, 0:CL - 1], f_dst[:, 1:CL], ALU.is_equal)
            then(dve.tensor_tensor(f_step[:, CL - 1:CL], f_dst[:, CL - 1:CL], f_next, ALU.is_equal))
            then(dve.scalar_tensor_tensor(out=i_to, in0=f_step, scalar=FAR, in1=f_dst, op0=ALU.mult, op1=ALU.add))
            dve.tensor_tensor(f_step[:, 1:CL], f_dst[:, 1:CL], f_dst[:, 0:CL - 1], ALU.not_equal)
            dve.memset(f_step[:, 0:1], 1.0)
            dve.wait_ge(gen_pool, 3)
            then(dve.tensor_copy(ends[:, 1, :], f_dst[:, CL - 1:CL].broadcast_to([CH, HEADS])))
            dve.tensor_copy(ends[:, 2, :], f_dst[:, 0:1].broadcast_to([CH, HEADS]))
            then(dve.tensor_scalar(f_step, f_step, LOW, None, ALU.mult))
            for k in range(HEADS):
                last = dve.tensor_tensor_scan(score[:, :, k], f_step, score[:, :, k], LOW, ALU.add, ALU.max)
            last.then_inc(gen_scan, 1)
            dve.wait_ge(gen_scan, 1)
            then(dve.tensor_copy(ends[:, 0, :], score[:, CL - 1, :]))
            dve.wait_ge(gen_pe, 1)
            then(dve.tensor_copy(erow, bank[0][0:HEADS, 0:3 * CH].rearrange("p (a c) -> p a c", a=3)))
            dve.memset(crow[:, 0, 0:1], LOW)
            dve.memset(crow[:, 2, 0:1], LOW)
            then(dve.tensor_tensor(crow[:, 0, 1:CH], erow[:, 1, 1:CH], erow[:, 1, 0:CH - 1], ALU.not_equal))
            then(dve.tensor_scalar(crow[:, 0, 1:CH], crow[:, 0, 1:CH], LOW, None, ALU.mult))
            dve.tensor_tensor(crow[:, 2, 1:CH], erow[:, 2, 1:CH], erow[:, 1, 0:CH - 1], ALU.not_equal)
            then(dve.tensor_tensor_scan(crow[:, 1, :], crow[:, 0, :], erow[:, 0, :], LOW, ALU.add, ALU.max))
            then(dve.tensor_scalar(crow[:, 2, 1:CH], crow[:, 2, 1:CH], LOW, None, ALU.mult))
            then(dve.tensor_add(crow[:, 2, 1:CH], crow[:, 2, 1:CH], crow[:, 1, 0:CH - 1]))
            dve.wait_ge(gen_pe, 2)
            dve.tensor_copy(carry, bank[1][0:CH, 0:HEADS])
            then(dve.tensor_scalar(f_step, f_dst, f_dst[:, 0:1], None, ALU.not_equal))
            then(dve.tensor_scalar(f_step, f_step, LOW, None, ALU.mult))
            for k in range(HEADS):
                last = dve.scalar_tensor_tensor(out=score[:, :, k], in0=f_step, scalar=carry[:, k:k + 1], in1=score[:, :, k], op0=ALU.add, op1=ALU.max)
            last.then_inc(gen_done, 1)

        block = ctx.enter_context(nc.Block())
        settled = sem("settled")

        def settle(eng):
            eng.sem_inc(settled, 1)

        def blocks_of(engine, starts, width, k, n):
            return nc.values_load_multi_w_load_instructions(
                starts[0:1, bass.ds(k, n)], engines=[engine], min_val=0, max_val=NB * width,
                skip_runtime_bounds_check_because="a block is the sum of NB comparisons, times width")[1]

        def rows_of(t, i, n=1):
            return t[bass.ds(i * P, n * P), :].rearrange("(n p) f -> p n f", p=P)

        @block.sync
        def _(sp):
            with nc.allow_non_contiguous_dma(reason="the last destination of each edge tile"):
                sp.dma_start(ld_i, dst[0:WHOLE * P].rearrange("(t e) -> e t", e=P)[P - 1:P, :]).then_inc(ld, 16)
            for k in range(2):
                sp.dma_start(accx[:, 8 * k:8 * k + 8, :], rows_of(x, 8 * k, 8)).then_inc(x_in[k], 16)
            for k, (a, b) in enumerate(((src, src_pad), (dst, dst_pad))):
                flat = b.rearrange("t e -> (t e)")
                sp.dma_start(flat[0:EDGES].rearrange("(a b) -> a b", a=32), a.rearrange("(a b) -> a b", a=32)).then_inc(padded, 16)
                if k == 0:
                    sp.wait_ge(pads, 2)
                sp.dma_start(flat[EDGES:EP].rearrange("(a b) -> a b", a=1), pad_i[:, k, :]).then_inc(padded, 16)
            for t, w in ((wg[:, :, 0:D], gW), (wks[:], wk), (wqs[:], wq), (wvs[:], wv), (wos[:], wo), (wrs[:], Wr)):
                sp.dma_start(t, w.rearrange("(c p) f -> p c f", p=P)).then_inc(wts, 16)
            for t, w in ((bvs, bv), (brs, br)):
                sp.dma_start(t[:], w.rearrange("(a f) -> a f", a=1)).then_inc(wts, 16)
            for t, w in ((bks, bk), (bos, bo), (gbs, g_bias)):
                sp.dma_start(t, w.rearrange("(a f) -> a f", a=1).broadcast_to([THIRD, D])).then_inc(wts, 16)
            with nc.allow_non_contiguous_dma(reason="256 numbers"):
                sp.dma_start(bqs[:], bq.rearrange("(c p) -> p c", p=P)).then_inc(wts, 16)
            for k, (t, w) in enumerate(((gam, gamma), (bet, beta))):
                sp.dma_start(t[:], w.rearrange("(a f) -> a f", a=1).broadcast_to([P, D])).then_inc(out_stored[k], 16)
            for k, w in enumerate((g_as, g_ad)):
                sp.dma_start(attb[:, k, :], w.rearrange("(a h) f -> a (h f)", a=1).broadcast_to([P, D])).then_inc(stored[k], 16)

            sp.dma_start(accx[:, 16:NT - 1, :], rows_of(x, 16, NT - 17)).then_inc(x_rest, 16)
            sp.wait_ge(const, CONSTS)
            sp.dma_start(accx[0:LAST, NT - 1, :], x[(NT - 1) * P:N, :]).then_inc(x_rest, 16)

            def store(u, h):
                g = 2 * u + h
                sp.wait_ge(ht_out, 8 * (g + 1) + 2)
                sp.dma_start(rows_of(table, 8 * g, 8), ht[:, 8 * h:8 * h + 8, 0:ROW]).then_inc(stored[h], 16)
                sp.wait_ge(xn_made, 8 * (g + 1))
                sp.wait_ge(xn_stored[h], 16 * u + 16)
                sp.dma_start(rows_of(xn_d, 8 * g, 8), accx[:, bass.ds(8 * g, 8), :]).then_inc(xn_stored[h], 16)

            for h in range(2):
                sp.sem_inc(xn_stored[h], 16)
            with sp.Fori(0, 3) as u:
                for h in range(2):
                    store(u, h)
            sp.wait_ge(ht_out, NT + 2)
            sp.dma_start(table[(NT - 1) * P:NP, :], ht[:, 0, 0:ROW]).then_inc(stored[0], 16)
            sp.wait_ge(xn_made, NT)
            sp.wait_ge(xn_stored[0], 16 * 4)
            sp.dma_start(xn_d[(NT - 1) * P:NP, :], accx[:, NT - 1, :]).then_inc(xn_stored[0], 16)
            sp.wait_ge(xn_stored[0], 16 * 5)
            sp.wait_ge(xn_stored[1], 16 * 4)

            sp.wait_ge(dlb_made, 1)
            sp.dma_start(dst_rows.rearrange("(c p) e -> p c e", p=P), dlb).then_inc(dst_rows_out, 16)

            def kv(r, w=2):
                sp.wait_ge(g_made, r + 1)
                if w == 2:
                    sp.dma_start(xg[:, :, 0:D], rows_of(xn_d, 2 * r, 2)).then_inc(xg_in, 16)
                else:
                    sp.dma_start(xg[:, 0, 0:D], xn_d[(NT - 1) * P:NP, :]).then_inc(xg_in, 16)

            def att(r, w=2):
                sp.wait_ge(xo_made, r + 1)
                if w == 2:
                    sp.dma_start(xr, rows_of(x, 2 * r, 2)).then_inc(xr_in, 16)
                else:
                    sp.dma_start(xr[0:LAST, 0, :], x[(NT - 1) * P:N, :]).then_inc(xr_in, 16)
                sp.wait_ge(xo_made, r + 2)
                if w == 2:
                    sp.dma_start(rows_of(xa_d, 2 * r, 2), xo).then_inc(xo_stored, 16)
                else:
                    sp.dma_start(xa_d[(NT - 1) * P:NP, :], xo[:, 0, :]).then_inc(xo_stored, 16)
                sp.wait_ge(xo_stored, 16 * (r + 1))
                sp.sem_inc(xo_free, 1)

            with sp.Fori(0, PAIRS) as r:
                kv(r)
            kv(PAIRS, 1)
            with sp.Fori(0, PAIRS) as r:
                att(r)
            att(PAIRS, 1)

            def p2(r, q, w=2):
                sp.wait_ge(x1_made, r + 1)
                if w == 2:
                    sp.dma_start(xa[q], rows_of(xa_d, 2 * r, 2)).then_inc(xa_in[q], 16)
                else:
                    sp.dma_start(xa[q][:, 0, :], xa_d[(NT - 1) * P:NP, :]).then_inc(xa_in[q], 16)

            with sp.Fori(0, PAIRS // 2) as u:
                for q in range(2):
                    p2(2 * u + q, q)
            p2(PAIRS, 0, 1)

            sp.wait_ge(picked, 1)
            sp.wait_ge(y_out, PAIRS + 3)
            for e in range(TOPK):
                pick = bass.ds(sp.value_load(sel_i[0:1, e:e + 1], min_val=0, max_val=EXPERTS - 1), 1)
                sp.dma_start(w1s[:, e, :, :], W1[pick, :, :].rearrange("a (c p) f -> p (a c) f", p=P)).then_inc(w1_in, 16)
                with nc.allow_non_contiguous_dma(reason="512 numbers"):
                    sp.dma_start(b1s[:, e * FJ:(e + 1) * FJ], b1[pick, :].rearrange("a (j p) -> p (a j)", p=P)).then_inc(w1_in, 16)
                sp.dma_start(w2s[:, e * FJ:(e + 1) * FJ, :], W2[pick, :, :].rearrange("a (j p) f -> p (a j) f", p=P)).then_inc(w2_in, 16)
                sp.dma_start(b2s[:, e, :], b2[pick, :].broadcast_to([P, D])).then_inc(w2_in, 16)

            with sp.Fori(0, PAIRS) as u:
                for q in range(2):
                    sp.wait_ge(out_made, 2 * u + q + 1 + 2)
                    sp.dma_start(out[bass.ds((2 * u + q) * P, P), :], ot[q]).then_inc(out_stored[q], 16)
            sp.wait_ge(out_made, NT + 2)
            sp.dma_start(out[(NT - 1) * P:N, :], ot[0][0:LAST, :]).then_inc(out_stored[0], 16)
            sp.wait_ge(out_stored[0], 16 * (PAIRS + 2))
            sp.wait_ge(out_stored[1], 16 * (PAIRS + 1))

        @block.gpsimd
        def _(pool):
            n = [0]

            def link(ins):
                n[0] += 1
                ins.then_inc(const, 1)
                pool.wait_ge(const, n[0])

            pool.memset(pad_i[:, 0, :], 0).then_inc(pads, 1)
            pool.memset(pad_i[:, 1, :], PAD_DST).then_inc(pads, 1)
            link(pool.memset(ones[:], 1.0))
            pool.memset(half[:], -0.5)
            link(pool.memset(zeros[:], 0.0))
            link(pool.memset(ident[:], 0.0))
            link(pool.affine_select(out=ident[:], in_=ident[:], compare_op=ALU.not_equal, fill=1.0, base=0,
                                    pattern=[[-1, P]], channel_multiplier=1))
            link(pool.iota(place[:], [[0, 1]], base=0, channel_multiplier=1, allow_small_or_imprecise_dtypes=True))
            link(pool.iota(bnum, [[0, 1]], base=1, channel_multiplier=1, allow_small_or_imprecise_dtypes=True))
            link(pool.iota(bthr, [[0, 1]], base=P, channel_multiplier=P, allow_small_or_imprecise_dtypes=True))
            link(pool.iota(stepk, [[1, SW]], base=0, channel_multiplier=0, allow_small_or_imprecise_dtypes=True))
            link(pool.iota(kcol, [[P, SC]], base=0, channel_multiplier=1, allow_small_or_imprecise_dtypes=True))
            link(pool.iota(iota_f[:], [[1, P]], base=0, channel_multiplier=0, allow_small_or_imprecise_dtypes=True))
            link(pool.memset(headmask[:], 0.0))
            for k in range(P // FH):
                last = pool.memset(headmask[FH * k:FH * k + FH, FH * k:FH * k + FH], 1.0)
            link(last)
            link(pool.memset(kbmask[:], 0.0))
            for c in range(C):
                for k in range(P // FH):
                    last = pool.memset(kbmask[FH * k:FH * k + FH, c, 4 * c + k:4 * c + k + 1], 1.0)
            link(last)
            link(pool.memset(accx[:, NT - 1, :], 0.0))
            assert n[0] == CONSTS, n[0]
            def deviation(g, h, width=8):
                pool.wait_ge(stat, 3 * g + 3)
                pool.tensor_tensor(rstd[h][:, 0:width], mv[h][:, 0:width, 1], half[:, 0:width], ALU.pow).then_inc(rstd_made, 1)

            def in_parts(b, parts):
                left = b
                for row in (0, 32, 64):
                    link(pool.tensor_copy(part, left))
                    link(pool.tensor_copy(parts[row:row + 1, :], part[row:row + 1, :]))
                    if row < 64:
                        link(pool.tensor_sub(rest, left, part))
                        left = rest

            deviation(0, 0)
            pool.memset(part_ones[:], 1.0)
            pool.memset(bk_parts[:], 0.0)
            link(pool.memset(bsum_parts[:], 0.0))
            pool.wait_ge(wts, 16 * WEIGHTS)
            in_parts(bks, bk_parts)

            for k, t in enumerate((dst_pad, src_pad)):
                if k == 1:
                    deviation(1, 1)
                else:
                    pool.wait_ge(setup_dve, 8)
                    pool.wait_ge(padded, 64)
                for c in range(SC):
                    pool.indirect_dma_start(out=rows_i[:, 1 - k, c, :], out_offset=None, in_=t[:, :],
                                            in_offset=bass.IndirectOffsetOnAxis(ap=tcol_i[:, c:c + 1], axis=0)).then_inc(rows_got, 16)
            pool.wait_ge(wts, 16 * WEIGHTS)
            def keep(i, j):
                pool.wait_ge(ht_out, i + 1 + 2)
                pool.tensor_copy(aav[:, bass.ds(i, 1), 0:16], ht[:, j:j + 1, D:HW]).then_inc(aa_kept, 1)

            def zero(u, h):
                pool.wait_ge(xn_stored[h], 16 * u + 32)
                g = 2 * u + h
                pool.memset(accx[:, 8 * g:8 * g + 8, :], 0.0).then_inc(zeroed, 1)

            pool.sem_inc(aa_kept, 16)
            with pool.Fori(0, 2) as u:
                for h in range(2):
                    for j in range(8):
                        keep(16 * u + 8 * h + j, 8 * h + j)
                    deviation(2 * u + 2 + h, h)
            pool.wait_ge(rows_got, 16 * 2 * SC)
            link(pool.tensor_add(bsum, bos, gbs))
            in_parts(bsum, bsum_parts)
            pool.sem_inc(parts_made, 1)
            for j in range(8):
                keep(32 + j, j)
            deviation(6, 0, 1)
            zero(0, 0)
            zero(0, 1)
            zero(1, 0)
            for j in range(8):
                keep(40 + j, 8 + j)
            keep(NT - 1, 0)

            pool.wait_ge(shift_dve, 8)
            general = pool.value_load(flag[0:1, 0:1], min_val=0, max_val=1)
            with pool.If(general):
                exact_maxima_pool(pool)
            pool.sem_inc(sm_ready, 1)

            pool.wait_ge(stored[0], 16 * 5)
            pool.wait_ge(stored[1], 16 * 4)

            def gathers(i):
                for j in range(BODY):
                    if j % QUAD == 0:
                        pool.wait_ge(idx_staged, 4 * i + j // QUAD + 1)
                        if not isinstance(i, int):
                            pool.wait_ge(summed, 4 * i + j // QUAD + 1)
                        settle(pool)
                    pool.indirect_dma_start(out=gath[:, j, :], out_offset=None, in_=table[:, :],
                                            in_offset=bass.IndirectOffsetOnAxis(ap=idx[:, j:j + 1], axis=0)).then_inc(got[j], 16)

            pool.wait_ge(aa_kept, NT + 16)
            gathers(0)

            with pool.Fori(1, BODIES) as i:
                gathers(i)

            pool.sem_inc(x1_made, 2)

            def add_xa(r, q, u, w=2):
                t1 = accv[:, bass.ds(2 * r, w), 0:D]
                pool.wait_ge(x1_scaled, r + 1)
                pool.wait_ge(xa_in[q], 16 * u + 16)
                pool.tensor_add(t1, t1, xa[q][:, 0:w, :]).then_inc(x1_made, 1)

            def deviation2(r, q, w=2):
                pool.wait_ge(x1_dve, 3 * r + 3)
                pool.tensor_tensor(mv2[q][:, 0:w, 1], mv2[q][:, 0:w, 1], half[:, 0:w], ALU.pow).then_inc(rstd2_made, 1)

            add_xa(0, 0, 0)
            add_xa(1, 1, 0)
            deviation2(0, 0)
            with pool.Fori(0, PAIRS // 2 - 1) as u:
                for q in range(2):
                    add_xa(2 * u + q + 2, q, u + 1)
                    deviation2(2 * u + q + 1, 1 - q)
            add_xa(PAIRS, 0, PAIRS // 2, 1)
            deviation2(PAIRS - 1, 1)
            deviation2(PAIRS, 0, 1)

            pool.wait_ge(out_stored[0], 16)
            pool.wait_ge(out_stored[1], 16)

            def tail(i, q, u):
                pool.wait_ge(yb_made, i + 1)
                pool.tensor_add(yb[q], yb[q], b2w).then_inc(yb_full, 1)
                pool.wait_ge(z_dve, 3 * i + 3)
                pool.tensor_tensor(mv3[:, 1:2], mv3[:, 1:2], half[:, 0:1], ALU.pow).then_inc(rstd3_made, 1)
                pool.wait_ge(zn_made, i + 1)
                pool.tensor_mul(zt[q], zt[q], gam[:]).then_inc(zg_made, 1)
                pool.wait_ge(zg_made, 2 * i + 1)
                pool.tensor_add(zt[q], zt[q], bet[:]).then_inc(zg_made, 1)
                pool.wait_ge(zg_made, 2 * i + 2)
                pool.wait_ge(out_stored[q], 16 * u + 16)
                pool.tensor_add(ot[q], zt[q], accv[:, bass.ds(i, 1), 0:D].rearrange("p a f -> p (a f)")).then_inc(out_made, 1)

            pool.wait_ge(w2_scaled, 1)
            pool.sem_inc(out_made, 2)
            with pool.Fori(0, PAIRS) as u:
                for q in range(2):
                    tail(2 * u + q, q, u)
            tail(NT - 1, 0, PAIRS)

        @block.scalar
        def _(act):
            act.sem_inc(xts_out, 2)
            act.sem_inc(xts_kept, 2)
            act.sem_inc(ht_out, 2)

            def turn_out(i, q, k):
                act.wait_ge(xs_turned, i + 1 + 4)
                act.wait_ge(h_made, i + 1)
                act.copy(xts[k], bank[q][:, 0:D].rearrange("p (c n) -> p c n", c=C)).then_inc(xts_out, 1)

            def keep_turned(i, q):
                act.copy(xTv[:, :, bass.ds(i * P, P)], bank[q][:, 0:D].rearrange("p (c n) -> p c n", c=C)).then_inc(xts_kept, 1)

            def h_out(i, j, q, u, first):
                act.wait_ge(h_made, i + 1 + 4)
                if first:
                    act.wait_ge(stored[j // 8], 16 * u + 16)
                act.wait_ge(aa_kept, i + 1)
                act.copy(ht[:, j, :], bank[2 + q][:, 0:HW]).then_inc(ht_out, 1)

            def out_of_psum(i, j, u, ahead=2):
                for q in range(ahead):
                    turn_out(i + 2 + q, q, (j + 2 + q) % 4)
                for q in range(ahead):
                    keep_turned(i + 2 + q, q)
                for q in range(2):
                    h_out(i + q, j + q, q, u, (j + q) % 8 == 0)

            for q in range(2):
                turn_out(q, q, q)
            for q in range(2):
                keep_turned(q, q)
            with act.Fori(0, 2) as u:
                for j in range(0, 16, 2):
                    out_of_psum(16 * u + j, j, u)
            for j in range(0, 16, 2):
                out_of_psum(32 + j, j, 2, min(2, NT - 34 - j))
            h_out(NT - 1, 0, 0, 3, True)

            for g in range(3, 6):
                act.wait_ge(xn_stored[g % 2], 16 * (g // 2) + 32)
                act.copy(accx[:, 8 * g:8 * g + 8, :], zeros[:].unsqueeze(1).broadcast_to([P, 8, D])).then_inc(zeroed, 1)
            act.wait_ge(srci_made, 1)
            act.copy(idx[:], srci[:, 0:BODY]).then_inc(idx_staged, 4)
            act.wait_ge(xn_stored[0], 16 * 5)
            act.copy(acc[:, (NT - 1) * D:].rearrange("p (a f) -> p a f", a=3),
                     zeros[:, 0:(NT * ROW - (NT - 1) * D) // 3].unsqueeze(1).broadcast_to([P, 3, (NT * ROW - (NT - 1) * D) // 3])).then_inc(zeroed, 1)
            act.wait_ge(shift_ready, 1)

            def load_dlr(q, j):
                act.wait_ge(dlr_used, q + 1)
                act.dma_start(dlr[:, QUAD * (j % 4):QUAD * (j % 4) + QUAD, :],
                              dst_rows[bass.ds(QUAD * q, QUAD), :].rearrange("(a t) e -> a t e", a=1).broadcast_to([P, QUAD, P])).then_inc(dlr_in[j % 4], 16)

            def one_hot_far(q):
                act.wait_ge(oh_made, q + 1)
                for t in range(QUAD):
                    last = act.activation(away[1][:, t, :], iota_f[:], ACT.Abs, bias=dl[:, bass.ds(QUAD * q + t, 1)], scale=-1.0)
                last.then_inc(away_made, 1)

            def one_hots(q, j, u):
                act.wait_ge(dlr_in[j % 4], 16 * u + 16)
                act.wait_ge(oht_made, q + 1)
                act.activation(away[0], dlr[:, QUAD * (j % 4):QUAD * (j % 4) + QUAD, :], ACT.Abs, bias=place[:], scale=-1.0).then_inc(dlr_used, 1)
                act.wait_ge(away_made, q + 1)
                act.wait_ge(summed, q + 1)
                act.activation(oh[j % 4], away[1], ACT.Relu, bias=ones[:, 0:1], scale=-1.0).then_inc(oh_made, 1)
                act.wait_ge(dlr_used, q + 1 + 4)
                act.wait_ge(ad_made, q + 1)
                act.activation(oht[j % 2], away[0], ACT.Relu, bias=ones[:, 0:1], scale=-1.0).then_inc(oht_made, 1)

            def p_of(q, j):
                act.wait_ge(eu_made, q + 1)
                act.activation(ev, eu[j % 2], ACT.Relu).then_inc(eu_pos, 1)
                act.wait_ge(eu_pos, q + 1)
                act.activation(gath[:, 4 * (j % 4):4 * (j % 4) + 4, D:ROW], ev, ACT.Exp, scale=-1.0).then_inc(p_made, 1)

            def stage(q, j):
                o = QUAD * (j % 4)
                act.copy(idx[:, o:o + QUAD], srci[:, bass.ds(QUAD * q + BODY, QUAD)]).then_inc(idx_staged, 1)

            def kv_h0(r, w=2):
                n = w * P
                act.wait_ge(k_made, r + 1)
                act.copy(kxs[:, :, 0:n], xTv[:, :, bass.ds(2 * P * r, n)]).then_inc(kx_out, 1)

            def kv_h1(r, w=2):
                act.wait_ge(k_made, r + 2)
                act.wait_ge(phi_made, r + 1)
                act.activation(ea[:, 0:w * D], bank[5][:, 0:w * D], ACT.Exp)
                act.activation(eb[:, 0:w * D], bank[5][:, 0:w * D], ACT.Relu).then_inc(k_out, 1)

            def att_h0(r, w=2):
                n = w * P
                act.wait_ge(q_made, r + 1)
                act.wait_ge(phiq_made, r + 1)
                for m in range(C):
                    sl = slice(m * 2 * P, m * 2 * P + n)
                    act.activation(ea[:, sl], bank[5][:, sl], ACT.Exp, bias=bqs[:, m:m + 1])
                    last = act.activation(eb[:, sl], bank[5][:, sl], ACT.Relu, bias=bqs[:, m:m + 1])
                last.then_inc(q_out, 1)

            def att_h1(r, w=2):
                act.wait_ge(rq_made, r + 1)
                act.wait_ge(rq_spread, r + 1)
                act.copy(rqx[:, 0:w * D].rearrange("p (k f) -> p k f", f=FH),
                         rq[:, 0:w * HEADS].unsqueeze(2).broadcast_to([P, w * HEADS, FH])).then_inc(rqx_made, 1)

            def body(i, early, late, left=2):
                for j in range(4):
                    q = 4 * i + j
                    if j in early:
                        early[j]()
                    if left:
                        one_hot_far(q + 4)
                    if left or j < 2:
                        p_of(q + 2, j + 2)
                    if left:
                        stage(q + 2, j + 2)
                        one_hots(q + 4, j, i + 1)
                        if left > 1:
                            load_dlr(q + 8, j)
                    if j in late:
                        late[j]()

            act.sem_inc(dlr_used, 4)
            act.sem_inc(p_made, 2)
            act.sem_inc(oht_made, 1)
            act.sem_inc(oh_made, 1)
            act.sem_inc(k_out, 1)
            act.sem_inc(q_out, 1)
            act.wait_ge(dst_rows_out, 16)
            for q in range(4):
                load_dlr(q, q)
            for q in range(4):
                one_hot_far(q)
                one_hots(q, q, 0)
                load_dlr(q + 4, q)
                if q >= 1 and q < 3:
                    p_of(q - 1, q - 1)
                    stage(q - 1, q - 1)
            body(0, {2: lambda: kv_h0(0)}, {})
            with act.Fori(1, PAIRS) as i:
                body(i, {2: lambda: kv_h0(i)}, {0: lambda: kv_h1(i - 1)})
            body(PAIRS, {2: lambda: kv_h0(PAIRS, 1)}, {0: lambda: kv_h1(PAIRS - 1)})
            body(PAIRS + 1, {}, {0: lambda: kv_h1(PAIRS, 1)})
            A = PAIRS + 2
            with act.Fori(0, PAIRS) as r:
                body(A + r, {}, {0: lambda: att_h0(r), 2: lambda: att_h1(r)})
            body(A + PAIRS, {}, {0: lambda: att_h0(PAIRS, 1), 2: lambda: att_h1(PAIRS, 1)}, left=1)
            body(BODIES - 1, {}, {}, left=0)

            def y_evac(r, q, w=2):
                act.wait_ge(y_turned, r + 1)
                act.copy(xTv[:, :, bass.ds(2 * P * r, w * P)],
                         bank[q][:].rearrange("p (c n) -> p c n", c=C)[:, :, 0:w * P]).then_inc(y_out, 1)

            def normalize(r, q, w=2):
                act.wait_ge(ab_made, 3 * r + 3 + 3)
                act.wait_ge(y_used, r + 1)
                for t in range(w):
                    x1 = accv[:, bass.ds(2 * r + t, 1), 0:D].rearrange("p a f -> p (a f)")
                    last = act.activation(ys[q][:, t, :], x1, ACT.Identity, bias=ab2[q][:, t, 1:2], scale=ab2[q][:, t, 0:1])
                last.then_inc(y_made, 1)

            act.sem_inc(y_out, 2)
            act.sem_inc(y_made, 2)
            normalize(0, 0)
            with act.Fori(0, PAIRS // 2 - 1) as u:
                for q in range(2):
                    normalize(2 * u + q + 1, 1 - q)
                    y_evac(2 * u + q, q)
            normalize(PAIRS - 1, 1)
            y_evac(PAIRS - 2, 0)
            normalize(PAIRS, 0, 1)
            y_evac(PAIRS - 1, 1)
            y_evac(PAIRS, 0, 1)

            for k, sl in enumerate((slice(16, 24), slice(40, 48), slice(90, 91))):
                act.wait_ge(route_dve, EXPS[k])
                act.activation(rt[:, sl], rt[:, sl], ACT.Exp).then_inc(route_act, 1)

            act.wait_ge(w1_in, 16 * 2 * TOPK)

            def hidden(g, w=4):
                for k in range(EJ):
                    act.wait_ge(hid_made, EJ * g + k + 1)
                    act.activation(hT[:, k, 0:w * P], bank[k % 4][:, 0:w * P], ACT.Gelu, bias=b1s[:, k:k + 1]).then_inc(hid_out, 1)

            act.sem_inc(hid_out, 4)
            with act.Fori(0, NT // 4) as g:
                hidden(g)
            hidden(NT // 4, 1)

        @block.tensor
        def _(pe):
            pe.wait_ge(const, CONSTS)
            pe.wait_ge(setup_dve, 1)
            cut = (0, 400, WHOLE)
            for k in range(2):
                last = pe.matmul(bank[k][0:NB, 0:cut[k + 1] - cut[k]], ones[0:1, 0:NB], ld_f[0:1, cut[k]:cut[k + 1]], start=True, stop=True)
            last.then_inc(setup_pe, 1)
            pe.wait_ge(setup_dve, 5)
            for k in range(2):
                pe.matmul(bank[2 + k][0:1, 0:SW // 2], ones[0:NB, 0:1], moved[:, k * SW // 2:(k + 1) * SW // 2], start=True, stop=True)
            for c in range(SC):
                last = pe.matmul(bank[4][:, c:c + 1], moved[:, c * P:c * P + P], ones[0:NB, 0:1], start=True, stop=True)
            last.then_inc(setup_pe, 1)

            pe.sem_inc(xs_turned, 4)
            pe.sem_inc(h_made, 4)
            pe.wait_ge(setup_dve, 8)
            pe.wait_ge(watt, 2)

            def turn(i, q, k):
                pe.wait_ge(xs_made, i + 1)
                pe.wait_ge(xts_kept, i + 1)
                for c in range(C):
                    last = pe.transpose(bank[q][:, c * P:c * P + P], xs[k][:, c * P:c * P + P], ident[:])
                last.then_inc(xs_turned, 1)

            def project(i, q, k):
                pe.wait_ge(xts_out, i + 1 + 2)
                pe.wait_ge(ht_out, i + 1)
                for c in range(C):
                    last = pe.matmul(bank[2 + q][:, 0:HW], xts[k][:, c, :], wg[:, c, :], start=(c == 0), stop=(c == C - 1))
                last.then_inc(h_made, 1)

            for q in range(2):
                turn(q, q, q)
            with pe.Fori(0, 2) as u:
                for j in range(0, 16, 2):
                    for q in range(2):
                        turn(16 * u + j + q + 2, q, (j + q + 2) % 4)
                    for q in range(2):
                        project(16 * u + j + q, q, (j + q) % 4)
            for j in range(0, 16, 2):
                for q in range(2):
                    if 32 + j + q + 2 < NT:
                        turn(32 + j + q + 2, q, (j + q + 2) % 4)
                for q in range(2):
                    project(32 + j + q, q, (j + q) % 4)
            project(NT - 1, 0, 0)

            pe.wait_ge(setup_dve, 9)
            pe.wait_ge(ht_out, NT + 2)
            for k in (1, 0):
                for c in range(SC):
                    b = 2 * k + c // 4
                    last = pe.transpose(bank[b][:, c % 4 * P:c % 4 * P + P], rows_f[:, k, c, :], ident[:])
                last.then_inc(rows_turned, 1)
            pe.wait_ge(shift_dve, 2)
            pe.transpose(bank[4][0:16, 0:P], ext, ident[:]).then_inc(shift_pe, 1)
            pe.wait_ge(shift_dve, 4)
            pe.matmul(bank[4][:, 128:144], ones[0:16, :], exd, start=True, stop=True).then_inc(shift_pe, 1)
            pe.wait_ge(shift_dve, 8)
            general = pe.value_load(flag[0:1, 0:1], min_val=0, max_val=1)
            with pe.If(general):
                exact_maxima_pe(pe)

            pe.wait_ge(shift_ready, 1)
            pe.sem_inc(summed, 4)
            pe.sem_inc(ad_made, 2)
            pe.wait_ge(parts_made, 1)
            pe.matmul(bank[6][:], zeros[:, 0:P], zeros[:].unsqueeze(1).broadcast_to([P, C, D]), start=True, stop=False)
            for t in (k_made, g_made, rq_spread, att_made):
                pe.sem_inc(t, 1)

            def spread_ad(q, j, b):
                pe.wait_ge(oht_made, q + 1 + 1)
                if not (isinstance(q, int) and q < 2):
                    pe.wait_ge(eu_made, q - 1)
                for t in range(QUAD):
                    o = AD_AT + 16 * t
                    last = pe.matmul(bank[2 if j % 2 == 0 else 7][:, o:o + 16], oht[j % 2][:, t, :], aa[:, 8:][:, bass.ds(b[t], 16)], start=True, stop=True)
                last.then_inc(ad_made, 1)

            def sum_up(q, j):
                pe.wait_ge(oh_made, q + 1 + 1)
                pe.wait_ge(weighed, q + 1)
                for t in range(QUAD):
                    pe.wait_ge(added[t], q + 4 if t < QUAD - 1 else q + 5)
                    last = pe.matmul(bank[SUMS[t]][:, 0:ROW], oh[j % 4][:, t, :], gath[:, 4 * (j % 4) + t, :], start=True, stop=True)
                last.then_inc(summed, 1)

            def kv_h0(r, ts, w=2):
                pe.wait_ge(kx_out, r + 1)
                pe.wait_ge(k_out, r + 1)
                pe.wait_ge(ksum_added, r + 2)
                for t in ts:
                    o = bank[5][:, t * D:t * D + D]
                    pe.matmul(o, part_ones[:], bk_parts[:], start=True, stop=False)
                    for c in range(C):
                        last = pe.matmul(o, kxs[:, c, t * P:t * P + P], wks[:, c, :], start=False, stop=(c == C - 1))
                if ts[-1] == w - 1:
                    last.then_inc(k_made, 1)

            def kv_h2(r, w=2):
                k = P if w == 2 else LAST
                pe.wait_ge(phi_made, r + 2)
                pe.wait_ge(xg_in, 16 * r + 16)
                for m in range(C):
                    for t in range(w):
                        pe.matmul(bank[6][:, m * D:m * D + D], ph[0:k, t * D + m * P:t * D + m * P + P], xg[0:k, t, :],
                                  start=False, stop=(w == 1 and m == C - 1))
                for m in range(C):
                    for t in range(w):
                        last = pe.matmul(bank[5][:, m:m + 1], ph[0:k, t * D + m * P:t * D + m * P + P], ones[0:k, 0:1],
                                         start=(t == 0), stop=(t == w - 1))
                last.then_inc(g_made, 1)

            def m_stage():
                pe.wait_ge(m_dve, 1)
                for c in range(C):
                    for m in range(C):
                        pe.transpose(bank[5][:, c * D + m * P:c * D + m * P + P], kvg[:, m, c * P:c * P + P], ident[:])
                for m in range(C):
                    last = pe.matmul(bank[6][0:1, m * P:m * P + P], ksum[:, m:m + 1], ident[:], start=True, stop=True)
                last.then_inc(m_pe, 1)
                pe.wait_ge(m_dve, 2)
                for m in range(C):
                    o = bank[5][:, m * P:m * P + P]
                    pe.matmul(o, bvs[0:1, m * P:m * P + P], ksr[0:1, m * P:m * P + P], start=True, stop=False)
                    for c in range(C):
                        last = pe.matmul(o, wvs[:, c, m * P:m * P + P], gT[:, c * D + m * P:c * D + m * P + P], start=False, stop=(c == C - 1))
                last.then_inc(m_pe, 1)
                pe.wait_ge(m_dve, 3)
                for m in range(C):
                    last = pe.matmul(bank[6][:, m * D:m * D + D], kvm[:, m, :], wos[:, m, :], start=True, stop=True)
                last.then_inc(m_pe, 1)
                pe.wait_ge(m_dve, 4)

            def att_h0(r, w=2):
                n = w * P
                pe.wait_ge(q_out, r + 1)
                if not (isinstance(r, int) and r == 0):
                    pe.wait_ge(xo_made, r)
                for m in range(C):
                    for c in range(C):
                        last = pe.matmul(bank[5][:, m * 2 * P:m * 2 * P + n], wqs[:, c, m * P:m * P + P], xTv[:, c, bass.ds(2 * P * r, n)],
                                         start=(c == 0), stop=(c == C - 1))
                last.then_inc(q_made, 1)

            def att_h1(r, w=2):
                pe.wait_ge(phiq_made, r + 2)
                for t in range(w):
                    for m in range(C):
                        last = pe.matmul(bank[5][:, 8 * t:8 * t + 8], ph[:, m * 2 * P + t * P:m * 2 * P + t * P + P], kb[:, m, :],
                                         start=(m == 0), stop=(m == C - 1))
                last.then_inc(norm_made, 1)

            def att_h2(r, w=2):
                pe.wait_ge(rqx_made, r + 1)
                pe.wait_ge(qn_made, r + 1)
                for m in range(C):
                    for t in range(w):
                        last = pe.transpose(bank[6][:, m * 2 * P + t * P:m * 2 * P + t * P + P], rqx[:, t * D + m * P:t * D + m * P + P], ident[:])
                last.then_inc(rq_spread, 1)

            def att_h3(r, rqs, w=2):
                pe.wait_ge(qn_made, r + 2)
                pe.wait_ge(rq_made, rqs)
                pe.wait_ge(xo_made, r + 1)
                for t in range(w):
                    o = bank[5][:, t * D:t * D + D]
                    pe.matmul(o, part_ones[:], bsum_parts[:], start=True, stop=False)
                    for m in range(C):
                        last = pe.matmul(o, qn[:, m * 2 * P + t * P:m * 2 * P + t * P + P], m_sb[:, m, :], start=False, stop=(m == C - 1))
                last.then_inc(att_made, 1)

            def body(i, hooks, last=False):
                b = blocks_of(mybir.EngineType.PE, brow_aa, 24, BODY * i + 3 * QUAD, QUAD if last else BODY)
                for j in range(4):
                    q = 4 * i + j
                    if not (last and j >= 1):
                        spread_ad(q + 3, j + 3, b[QUAD * j:QUAD * j + QUAD])
                    if not (last and j == 3):
                        sum_up(q + 1, j + 1)
                    if j in hooks:
                        hooks[j]()

            b = blocks_of(mybir.EngineType.PE, brow_aa, 24, 0, 3 * QUAD)
            for q in range(3):
                spread_ad(q, q, b[QUAD * q:QUAD * q + QUAD])
            sum_up(0, 0)
            def ks(r, w=2):
                return {2 + t: lambda t=t: kv_h0(r, (t,), w) for t in range(w)}

            body(0, ks(0))
            with pe.Fori(1, PAIRS) as i:
                body(i, {**ks(i), 1: lambda: kv_h2(i - 1)})
            body(PAIRS, {**ks(PAIRS, 1), 1: lambda: kv_h2(PAIRS - 1)})
            body(PAIRS + 1, {1: lambda: kv_h2(PAIRS, 1), 2: m_stage, 3: lambda: att_h0(0)})
            A = PAIRS + 2

            def att(r, w=2, w_next=2):
                return {0: lambda: att_h2(r - 1), 1: lambda: att_h1(r, w), 2: lambda: att_h3(r - 1, r + 1), 3: lambda: att_h0(r + 1, w_next)}

            body(A, {1: lambda: att_h1(0), 3: lambda: att_h0(1)})
            with pe.Fori(1, PAIRS - 1) as r:
                body(A + r, att(r))
            body(A + PAIRS - 1, att(PAIRS - 1, 2, 1))
            body(A + PAIRS, {**att(PAIRS, 1), 3: lambda: None})
            body(BODIES - 1, {0: lambda: att_h2(PAIRS, 1), 2: lambda: att_h3(PAIRS, PAIRS + 1, 1)}, last=True)

            pe.wait_ge(added[QUAD - 1], STEPS // QUAD + 5)
            pe.matmul(bank[2][0:1, 0:D], zeros[:, 0:1], zeros[:, 0:D], start=True, stop=False)
            pe.sem_inc(y_used, 2)

            def turn_y(r, q, w=2):
                pe.wait_ge(y_made, r + 1 + 2)
                pe.wait_ge(y_out, r + 1)
                for c in range(C):
                    for t in range(w):
                        last = pe.transpose(bank[q][:, c * D + t * P:c * D + t * P + P], ys[q][:, t, c * P:c * P + P], ident[:])
                last.then_inc(y_turned, 1)
                k = P if w == 2 else LAST
                for t in range(w):
                    last = pe.matmul(bank[2][0:1, 0:D], ones[0:k, 0:1], ys[q][0:k, t, :], start=False, stop=(w == 1))
                last.then_inc(y_used, 1)

            with pe.Fori(0, PAIRS // 2) as u:
                for q in range(2):
                    turn_y(2 * u + q, q)
            turn_y(PAIRS, 0, 1)

            pe.wait_ge(route_dve, 1)
            for c in range(C):
                last = pe.matmul(bank[3][:, c:c + 1], mrow[0:1, c * P:c * P + P], ones[0:1, 0:1], start=True, stop=True)
            last.then_inc(route_pe, 1)
            pe.wait_ge(route_dve, 2)
            for c in range(C):
                last = pe.matmul(bank[3][0:1, 16:16 + EXPERTS], mcol[:, c:c + 1], wrs[:, c, :], start=(c == 0), stop=(c == C - 1))
            last.then_inc(route_pe, 1)
            pe.wait_ge(route_dve, ROUTE - 1)
            pe.matmul(bank[3][:, 32:36], ones[0:1, :], sel, start=True, stop=True).then_inc(route_pe, 1)

            pe.wait_ge(route_dve, ROUTE)
            pe.wait_ge(w1_in, 16 * 2 * TOPK)
            pe.wait_ge(y_out, PAIRS + 3)

            def experts(g, w=4):
                n = w * P
                for k in range(EJ):
                    e, j = k // FJ, k % FJ
                    pe.wait_ge(hid_out, EJ * g + k + 1)
                    for c in range(C):
                        last = pe.matmul(bank[k % 4][:, 0:n], w1s[:, e, c, j * P:j * P + P], xTv[:, c, bass.ds(4 * P * g, n)],
                                         start=(c == 0), stop=(c == C - 1))
                    last.then_inc(hid_made, 1)
                pe.wait_ge(w2_scaled, 1)
                for t in range(w):
                    pe.wait_ge(z_made, 4 * g + t + 1)
                    for k in range(EJ):
                        if t == 0:
                            pe.wait_ge(hid_out, EJ * g + k + 5)
                        last = pe.matmul(bank[4 + t % 2][:, 0:D], hT[:, k, t * P:t * P + P], w2s[:, k, :], start=(k == 0), stop=(k == EJ - 1))
                    last.then_inc(moe_made, 1)

            with pe.Fori(0, NT // 4) as g:
                experts(g)
            experts(NT // 4, 1)

        @block.vector
        def _(dve):
            def linker(s, n=0):
                count = [n]

                def then(ins):
                    count[0] = count[0] + 1
                    ins.then_inc(s, 1)
                    dve.wait_ge(s, count[0])
                return then

            def tile_of(i):
                return accx[:, bass.ds(i, 1), :].rearrange("p a f -> p (a f)")

            def statistics(g, h, width=8):
                then = linker(stat, 3 * g)
                settle(dve)
                for j in range(width):
                    last = dve.bn_stats(stats[:, j, :], tile_of(8 * g + j))
                then(last)
                settle(dve)
                for j in range(width):
                    last = dve.bn_aggr(mv[h][:, j, :], stats[:, j, :])
                then(last)
                dve.tensor_scalar(mv[h][:, 0:width, 1], mv[h][:, 0:width, 1], LN_EPS, None, ALU.add).then_inc(stat, 1)

            def normalize(g, h, width=8):
                dve.wait_ge(rstd_made, g + 1)
                for j in range(width):
                    xj = tile_of(8 * g + j)
                    mean, rs = mv[h][:, j, 0:1], rstd[h][:, j:j + 1]
                    dve.wait_ge(xs_turned, 8 * g + j + 1)
                    dve.tensor_scalar(xs[j % 4], xj, mean, rs, ALU.subtract, ALU.mult).then_inc(xs_made, 1)
                    dve.tensor_scalar(xj, xj, mean, rs, ALU.subtract, ALU.mult).then_inc(xn_made, 1)

            then = linker(setup_dve)
            dve.wait_ge(ld, 16)
            then(dve.tensor_copy(ld_f, ld_i))
            for g in range(2):
                dve.wait_ge(x_in[g], 16)
                statistics(g, g)
            dve.wait_ge(const, CONSTS)
            dve.wait_ge(setup_pe, 1)
            cut = (0, 400, WHOLE)
            for k in range(2):
                last = dve.tensor_scalar(before[:, cut[k]:cut[k + 1]], bank[k][0:NB, 0:cut[k + 1] - cut[k]], bthr, None, ALU.is_lt)
            then(last)
            then(dve.tensor_reduce(cnt, before, AX_X, ALU.add))
            then(dve.tensor_add(key, cnt, bnum))
            then(dve.tensor_scalar(moved, stepk, key, None, ALU.is_ge))
            dve.wait_ge(setup_pe, 2)
            for k in range(2):
                for t, width in ((brow_aa, 24), (brow_acc, ROW)):
                    dve.tensor_scalar(t[0:1, k * SW // 2:(k + 1) * SW // 2], bank[2 + k][0:1, 0:SW // 2], float(width), None, ALU.mult)
            then(dve.tensor_copy(bcol, bank[4][:, 0:SC]))
            dve.tensor_scalar(b128, bcol, float(P), None, ALU.mult)
            then(dve.scalar_tensor_tensor(out=tcol, in0=bcol, scalar=-1.0, in1=kcol, op0=ALU.mult, op1=ALU.add))
            then(dve.tensor_scalar(tcol_i, tcol, float(ET - 1), None, ALU.min))

            dve.wait_ge(wts, 16 * WEIGHTS)
            for k in range(2):
                dve.wait_ge(stored[k], 16)
                last = dve.tensor_mul(prod[:, k, :, :], wg[:, :, 0:D], attb[:, k:k + 1, :].broadcast_to([P, C, D]))
            last.then_inc(watt, 1)
            dve.wait_ge(watt, 1)
            for k in range(2):
                for c in range(C):
                    last = dve.tensor_reduce(wg[:, c, D + HEADS * k:D + HEADS * k + HEADS], prod[:, k, c, :].rearrange("p (h f) -> p h f", f=FH), AX_X, ALU.add)
            last.then_inc(watt, 1)

            dve.wait_ge(x_rest, 32)
            with dve.Fori(0, 2) as u:
                for h in range(2):
                    normalize(2 * u + h, h)
                    statistics(2 * u + 2 + h, h)
            normalize(4, 0)
            statistics(6, 0, 1)
            normalize(5, 1)
            normalize(6, 0, 1)

            dve.wait_ge(rows_got, 16 * 2 * SC)
            dve.tensor_copy(rows_f[:, 0, :, :], rows_i[:, 0, :, :])
            for c in range(SC):
                last = dve.tensor_scalar(rows_f[:, 1, c, :], rows_i[:, 1, c, :], b128[:, c:c + 1], None, ALU.subtract)
            last.then_inc(setup_dve, 1)
            dve.wait_ge(setup_dve, 9)
            dve.tensor_copy(dlb, rows_f[:, 1, :, :]).then_inc(dlb_made, 1)
            for k, t in ((1, dl), (0, srci)):
                dve.wait_ge(rows_turned, 2 - k)
                dve.tensor_copy(t[:, 0:512], bank[2 * k][:])
                last = dve.tensor_copy(t[:, 512:SW], bank[2 * k + 1][:, 0:SW - 512])
            last.then_inc(srci_made, 1)

            then = linker(shift_dve)
            dve.wait_ge(aa_kept, NT + 16)
            by_head = aav[:, :, 0:HEADS].rearrange("p n k -> p k n")
            dve.tensor_reduce(ext[:, 0:8], by_head, AX_X, ALU.max)
            then(dve.tensor_reduce(ext[:, 8:16], by_head, AX_X, ALU.min))
            then(dve.tensor_scalar(ext[:, 8:16], ext[:, 8:16], -1.0, None, ALU.mult))
            dve.wait_ge(shift_pe, 1)
            then(dve.tensor_reduce(exr, bank[4][0:16, 0:P], AX_X, ALU.max))
            then(dve.tensor_scalar(exd, ident[0:16, 0:16], exr, None, ALU.mult))
            dve.wait_ge(shift_pe, 2)
            then(dve.tensor_copy(exb, bank[4][:, 128:144]))
            dve.tensor_copy(sm, exb[:, 0:8].unsqueeze(1).broadcast_to([P, NT, HEADS]))
            then(dve.tensor_add(exm, exb[:, 0:8], exb[:, 8:16]))
            then(dve.tensor_reduce(ext[:, 0:1], exm, AX_X, ALU.max))
            then(dve.tensor_scalar(flag[0:1, 0:1], ext[0:1, 0:1], spread, None, ALU.is_gt))
            general = dve.value_load(flag[0:1, 0:1], min_val=0, max_val=1)
            with dve.If(general):
                exact_maxima_dve(dve, linker)
            dve.wait_ge(sm_ready, 1)
            with dve.If(general):
                dve.memset(acc[:], 0.0).then_inc(gen_zero, 1)
                dve.wait_ge(gen_zero, 1)
            then(dve.tensor_add(sm, sm, aav[:, :, 8:16]))
            dve.scalar_tensor_tensor(out=aav[:, :, 16:24], in0=sm, scalar=SLOPE, in1=sm, op0=ALU.mult, op1=ALU.max).then_inc(shift_ready, 1)

            dve.wait_ge(zeroed, 7)
            dve.memset(ksum, 0.0).then_inc(ksum_zero, 1)
            dve.wait_ge(ksum_zero, 1)
            for t in range(QUAD):
                dve.sem_inc(added[t], 4 if t < QUAD - 1 else 5)
            dve.sem_inc(et_made, 2)
            dve.sem_inc(el_made, 2)
            dve.sem_inc(ksum_added, 2)
            for t in (phi_made, phiq_made, qn_made, xo_made, xo_free):
                dve.sem_inc(t, 1)

            def weigh(q, j):
                dve.wait_ge(p_made, q + 1 + 2)
                g = gath[:, 4 * (j % 4):4 * (j % 4) + 4, :]
                h = g[:, :, 0:D].rearrange("p t (k f) -> p t k f", f=FH)
                dve.tensor_mul(h, h, g[:, :, D:ROW].unsqueeze(3).broadcast_to([P, QUAD, HEADS, FH])).then_inc(weighed, 1)

            def score_and_add(score_q, js, u, add_q, b):
                def add(t):
                    if add_q is not None:
                        sums = acc[:, bass.ds(b[t], ROW)]
                        if t == 0:
                            dve.wait_ge(summed, add_q + 1 + 4)
                        dve.wait_ge(added[t - 1], add_q + 5)
                        dve.tensor_add(sums, sums, bank[SUMS[t]][:, 0:ROW]).then_inc(added[t], 1)

                if score_q is None:
                    for t in range(QUAD):
                        add(t)
                    return
                for t in range(QUAD):
                    dve.wait_ge(got[4 * (js % 4) + t], 16 * u + 16)
                dve.wait_ge(ad_made, score_q + 1 + 2)
                ad = bank[2 if js % 2 == 0 else 7][:, AD_AT:AD_AT + 16 * QUAD].rearrange("p (t k) -> p t k", t=QUAD)
                dve.tensor_add(et, gath[:, 4 * (js % 4):4 * (js % 4) + 4, D:ROW], ad[:, :, 0:8]).then_inc(et_made, 1)
                add(0)
                dve.wait_ge(et_made, score_q + 1 + 2)
                dve.scalar_tensor_tensor(out=el, in0=et, scalar=SLOPE, in1=et, op0=ALU.mult, op1=ALU.max).then_inc(el_made, 1)
                add(1)
                dve.wait_ge(el_made, score_q + 1 + 2)
                dve.tensor_sub(eu[js % 2], ad[:, :, 8:16], el).then_inc(eu_made, 1)
                add(2)
                add(3)

            def halves(t, n):
                return t[:, 0:2 * D].rearrange("p (m n) -> p m n", m=2)[:, :, 0:n]

            def kv_h1(r, w=2):
                dve.wait_ge(k_out, r + 2)
                dve.wait_ge(g_made, r + 1)
                dve.scalar_tensor_tensor(out=ph[:, 0:w * D], in0=ea[:, 0:w * D], scalar=1.0, in1=eb[:, 0:w * D],
                                         op0=ALU.min, op1=ALU.add).then_inc(phi_made, 1)

            def kv_h2(r):
                dve.wait_ge(g_made, r + 2)
                dve.wait_ge(ksum_added, r + 2)
                dve.tensor_add(ksum, ksum, bank[5][:, 0:C]).then_inc(ksum_added, 1)

            def m_stage():
                then = linker(m_dve)
                dve.wait_ge(g_made, PAIRS + 2)
                dve.wait_ge(ksum_added, PAIRS + 1 + 2)
                then(dve.tensor_copy(kvg, bank[6][:].rearrange("p (m f) -> p m f", m=C)))
                for m in range(C):
                    dve.tensor_scalar(kb[:, m, :], kbmask[:, m, :], ksum[:, m:m + 1], None, ALU.mult)
                dve.wait_ge(m_pe, 1)
                dve.tensor_copy(gT, bank[5][:])
                then(dve.tensor_copy(ksr, bank[6][0:1, 0:D]))
                dve.wait_ge(m_pe, 2)
                then(dve.tensor_mul(kvm, bank[5][:, 0:D].rearrange("p (m f) -> p m f", m=C), headmask[:].unsqueeze(1).broadcast_to([P, C, P])))
                dve.wait_ge(m_pe, 3)
                then(dve.tensor_copy(m_sb[:], bank[6][:].rearrange("p (m f) -> p m f", m=C)))

            def att_h1(r, w=2):
                n = w * P
                dve.wait_ge(q_out, r + 2)
                dve.wait_ge(qn_made, r + 1)
                dve.scalar_tensor_tensor(out=halves(ph, n), in0=halves(ea, n), scalar=1.0, in1=halves(eb, n),
                                         op0=ALU.min, op1=ALU.add).then_inc(phiq_made, 1)

            def att_h2(r, w=2):
                dve.wait_ge(norm_made, r + 1)
                then = linker(norm_dve, r)
                then(dve.tensor_scalar(rq2[:, 0:8 * w], bank[5][:, 0:8 * w], NORM_EPS, None, ALU.add))
                dve.reciprocal(rq[:, 0:8 * w], rq2[:, 0:8 * w]).then_inc(rq_made, 1)

            def att_h3(r, w=2):
                n = w * P
                dve.wait_ge(rq_spread, r + 2)
                dve.wait_ge(att_made, r + 1)
                dve.tensor_mul(halves(qn, n), halves(ph, n), halves(bank[6], n)).then_inc(qn_made, 1)

            def att_h4(r, w=2):
                dve.wait_ge(att_made, r + 2)
                dve.wait_ge(xr_in, 16 * r + 16)
                dve.wait_ge(xo_free, r + 1)
                dve.tensor_add(xo[:, 0:w, :], bank[5][:, 0:w * D].rearrange("p (t f) -> p t f", f=D), xr[:, 0:w, :]).then_inc(xo_made, 1)

            def body(i, hooks, last=False):
                b = blocks_of(mybir.EngineType.DVE, brow_acc, ROW, BODY * i, BODY)
                for j in range(4):
                    q = 4 * i + j
                    more = not (last and j >= 2)
                    score_and_add(q + 2 if more else None, j + 2, i + (j + 2) // 4, q, b[QUAD * j:QUAD * j + QUAD])
                    if j in hooks:
                        hooks[j]()
                    if more:
                        weigh(q + 2, j + 2)

            for q in range(2):
                score_and_add(q, q, 0, None, None)
                weigh(q, q)
            body(0, {})
            with dve.Fori(1, PAIRS) as i:
                body(i, {1: lambda: kv_h1(i - 1), 2: lambda: kv_h2(i - 1)})
            body(PAIRS, {1: lambda: kv_h1(PAIRS - 1), 2: lambda: kv_h2(PAIRS - 1)})

            def end_of_kv():
                kv_h2(PAIRS)
                m_stage()

            body(PAIRS + 1, {1: lambda: kv_h1(PAIRS, 1), 2: end_of_kv})
            A = PAIRS + 2

            def att(r, w=2):
                def phi():
                    att_h3(r - 1)
                    att_h1(r, w)
                return {1: phi, 2: lambda: att_h2(r, w), 3: lambda: att_h4(r - 1)}

            body(A, {1: lambda: att_h1(0), 2: lambda: att_h2(0)})
            with dve.Fori(1, PAIRS) as r:
                body(A + r, att(r))
            body(A + PAIRS, att(PAIRS, 1))
            body(BODIES - 1, {1: lambda: att_h3(PAIRS, 1), 3: lambda: att_h4(PAIRS, 1)}, last=True)

            dve.wait_ge(added[QUAD - 1], STEPS // QUAD + 5)
            then = linker(den_done)
            den = accv[:, :, D:ROW]
            then(dve.tensor_scalar(den, den, 1e-30, None, ALU.max))
            then(dve.reciprocal(den, den))

            def scale(r, w=2):
                t1 = accv[:, bass.ds(2 * r, w), :]
                h = t1[:, :, 0:D].rearrange("p t (k f) -> p t k f", f=FH)
                dve.tensor_mul(h, h, t1[:, :, D:ROW].unsqueeze(3).broadcast_to([P, w, HEADS, FH])).then_inc(x1_scaled, 1)

            def statistics2(r, q, w=2):
                then = linker(x1_dve, 3 * r)
                dve.wait_ge(x1_made, r + 1 + 2)
                settle(dve)
                for t in range(w):
                    last = dve.bn_stats(st2[:, t, :], accv[:, bass.ds(2 * r + t, 1), 0:D].rearrange("p a f -> p (a f)"))
                then(last)
                if not (isinstance(r, int) and r == 0):
                    dve.wait_ge(ab_made, 3 * r)
                settle(dve)
                for t in range(w):
                    last = dve.bn_aggr(mv2[q][:, t, :], st2[:, t, :])
                then(last)
                dve.tensor_scalar(mv2[q][:, 0:w, 1], mv2[q][:, 0:w, 1], LN_EPS, None, ALU.add).then_inc(x1_dve, 1)

            def factors(r, q, w=2):
                dve.wait_ge(rstd2_made, r + 1)
                dve.wait_ge(y_made, r + 1)
                dve.tensor_copy(mrv[:, bass.ds(2 * r, w), :], mv2[q][:, 0:w, :]).then_inc(ab_made, 1)
                dve.tensor_copy(ab2[q][:, 0:w, 0], mv2[q][:, 0:w, 1]).then_inc(ab_made, 1)
                dve.scalar_tensor_tensor(out=ab2[q][:, 0:w, 1], in0=mv2[q][:, 0:w, 0], scalar=-1.0, in1=mv2[q][:, 0:w, 1],
                                         op0=ALU.mult, op1=ALU.mult).then_inc(ab_made, 1)

            dve.sem_inc(ab_made, 3)
            scale(0)
            scale(1)
            statistics2(0, 0)
            with dve.Fori(0, PAIRS // 2 - 1) as u:
                for q in range(2):
                    scale(2 * u + q + 2)
                    statistics2(2 * u + q + 1, 1 - q)
                    factors(2 * u + q, q)
            scale(PAIRS, 1)
            statistics2(PAIRS - 1, 1)
            factors(PAIRS - 2, 0)
            statistics2(PAIRS, 0, 1)
            factors(PAIRS - 1, 1)
            factors(PAIRS, 0, 1)

            def softmax(src_, ex, k, out_, a, then):
                then(dve.tensor_reduce(rt[:, a:a + 1], src_, AX_X, ALU.max))
                then(dve.tensor_scalar(ex, src_, rt[:, a:a + 1], None, ALU.subtract))
                dve.wait_ge(route_act, k)
                then(dve.tensor_reduce(rt[:, a:a + 1], ex, AX_X, ALU.add))
                then(dve.reciprocal(rt[:, a + 1:a + 2], rt[:, a:a + 1]))
                then(dve.tensor_scalar(out_, ex, rt[:, a + 1:a + 2], None, ALU.mult))

            def first_greatest(v, top, where, then):
                then(dve.tensor_reduce(top, v, AX_X, ALU.max))
                then(dve.tensor_scalar(rt[:, 72:80], v, top, 100.0, ALU.is_lt, ALU.mult))
                then(dve.tensor_add(rt[:, 80:88], rt[:, 72:80], iota_f[0:1, 0:8]))
                then(dve.tensor_reduce(where, rt[:, 80:88], AX_X, ALU.min))

            then = linker(route_dve)
            dve.wait_ge(y_used, PAIRS + 1 + 2)
            then(dve.tensor_scalar(mrow, bank[2][0:1, 0:D], 1.0 / N, None, ALU.mult))
            dve.wait_ge(route_pe, 1)
            then(dve.tensor_copy(mcol, bank[3][:, 0:C]))
            dve.wait_ge(route_pe, 2)
            then(dve.tensor_add(rt[:, 0:8], bank[3][0:1, 16:24], brs[:]))
            softmax(rt[:, 0:8], rt[:, 16:24], 1, rt[:, 26:34], 24, then)
            then(dve.tensor_scalar(rt[:, 64:72], rt[:, 26:34], float(N), 1e-30, ALU.mult, ALU.max))
            then(dve.reciprocal(rt[:, 72:80], rt[:, 64:72]))
            then(dve.tensor_scalar(rt[:, 80:88], rt[:, 72:80], CAPACITY, 1.0, ALU.mult, ALU.min))
            then(dve.tensor_mul(rt[:, 96:104], rt[:, 26:34], rt[:, 80:88]))
            softmax(rt[:, 96:104], rt[:, 40:48], 2, rt[:, 56:64], 48, then)
            first_greatest(rt[:, 56:64], rt[:, 88:89], sel[:, 2:3], then)
            then(dve.tensor_scalar(rt[:, 104:112], iota_f[0:1, 0:8], sel[:, 2:3], -4.0, ALU.is_equal, ALU.mult))
            then(dve.tensor_add(rt[:, 112:120], rt[:, 56:64], rt[:, 104:112]))
            first_greatest(rt[:, 112:120], rt[:, 89:90], sel[:, 3:4], then)
            dve.tensor_copy(sel_i, sel[:, 2:4]).then_inc(picked, 1)
            then(dve.tensor_sub(rt[:, 90:91], rt[:, 89:90], rt[:, 88:89]))
            dve.wait_ge(route_act, 3)
            then(dve.tensor_scalar(rt[:, 91:92], rt[:, 90:91], 1.0, None, ALU.add))
            then(dve.reciprocal(sel[:, 0:1], rt[:, 91:92]))
            then(dve.tensor_mul(sel[:, 1:2], rt[:, 90:91], sel[:, 0:1]))
            dve.wait_ge(route_pe, 3)
            then(dve.tensor_copy(selb, bank[3][:, 32:36]))
            dve.wait_ge(w2_in, 16 * 2 * TOPK)
            for e in range(TOPK):
                w2e = w2s[:, e * FJ:(e + 1) * FJ, :]
                dve.tensor_scalar(w2e, w2e, selb[:, e:e + 1], None, ALU.mult)
            then(dve.tensor_scalar(b2w, b2s[:, 0, :], selb[:, 0:1], None, ALU.mult))
            dve.scalar_tensor_tensor(out=b2w, in0=b2s[:, 1, :], scalar=selb[:, 1:2], in1=b2w, op0=ALU.mult, op1=ALU.add).then_inc(w2_scaled, 1)

            dve.sem_inc(z_made, 2)

            def finish(i, q):
                x1 = accv[:, bass.ds(i, 1), 0:D].rearrange("p a f -> p (a f)")
                dve.tensor_scalar(yb[q], x1, mr[:, bass.ds(2 * i, 1)], mr[:, bass.ds(2 * i + 1, 1)], ALU.subtract, ALU.mult).then_inc(yb_made, 1)
                dve.wait_ge(moe_made, i + 1)
                dve.wait_ge(yb_full, i + 1)
                dve.wait_ge(out_made, i + 1)
                dve.tensor_add(zt[q], bank[4 + q][:, 0:D], yb[q]).then_inc(z_made, 1)
                dve.wait_ge(z_made, i + 1 + 2)
                then = linker(z_dve, 3 * i)
                settle(dve)
                then(dve.bn_stats(st3, zt[q]))
                settle(dve)
                then(dve.bn_aggr(mv3, st3))
                dve.tensor_scalar(mv3[:, 1:2], mv3[:, 1:2], LN_EPS, None, ALU.add).then_inc(z_dve, 1)
                dve.wait_ge(rstd3_made, i + 1)
                dve.tensor_scalar(zt[q], zt[q], mv3[:, 0:1], mv3[:, 1:2], ALU.subtract, ALU.mult).then_inc(zn_made, 1)

            with dve.Fori(0, PAIRS) as u:
                for q in range(2):
                    finish(2 * u + q, q)
            finish(NT - 1, 0)


_INS = ["x", "src", "dst", "L0_gnn_W", "L0_gnn_att_src", "L0_gnn_att_dst", "L0_gnn_bias", "L0_mix_wq", "L0_mix_bq",
        "L0_mix_wk", "L0_mix_bk", "L0_mix_wv", "L0_mix_bv", "L0_mix_wo", "L0_mix_bo", "L0_ffn_Wr", "L0_ffn_br",
        "L0_ffn_W1", "L0_ffn_b1", "L0_ffn_W2", "L0_ffn_b2", "L0_ffn_gamma", "L0_ffn_beta"]
_SCRATCH = [("table", (NP, ROW), F32), ("src_pad", (ET, P), I32), ("dst_pad", (ET, P), I32), ("asrc_tab", (NP, HEADS), F32),
            ("smax_tab", (NP, HEADS), F32), ("xn_d", (NP, D), F32), ("xa_d", (NP, D), F32), ("dst_rows", (SW, P), BF16)]


def kernel(**inputs):
    import numpy as _np
    import concourse.bacc as _bacc
    from concourse import mybir as _mybir
    from concourse.bass_utils import run_bass_kernel_spmd as _run

    nc = _bacc.Bacc("TRN2", target_bir_lowering=False, num_devices=1)
    arrays, args = {}, []
    for name in _INS:
        a = _np.ascontiguousarray(inputs[name])
        arrays[f"in_{name}_dram"] = a
        args.append(nc.dram_tensor(f"in_{name}_dram", a.shape, _mybir.dt.from_np(a.dtype), kind="ExternalInput").ap())
    args.append(nc.dram_tensor("out_0_dram", (N, D), F32, kind="ExternalOutput").ap())
    for name, shape, dt in _SCRATCH:
        args.append(nc.dram_tensor(name, shape, dt, kind="Internal").ap())
    gps_layer(nc, *args, SPREAD)
    r = _run(nc, [arrays], core_ids=[0])
    return r.results[0]["out_0_dram"]
```
